# Optimizing a Trainium2 kernel written in Bass

```python
import numpy as np
import jax
import jax.numpy as jnp

def _softmax(x, axis=-1):
    return jax.nn.softmax(x, axis=axis)

def _gelu(x):
    return jax.nn.gelu(x, approximate=True)

def _silu(x):
    return jax.nn.silu(x)

def _sigmoid(x):
    return jax.nn.sigmoid(x)

def _layernorm(x, axis=-1, eps=1e-05):
    m = jnp.mean(x, axis=axis, keepdims=True)
    v = jnp.var(x, axis=axis, keepdims=True)
    return (x - m) / jnp.sqrt(v + eps)

def _scatter_add(tgt, idx, src, axis=0):
    return tgt.at[idx].add(src)

def _segment_sum(src, seg, n):
    return jax.ops.segment_sum(src, seg, n)
kernel_name = 'mk_seq_postln_d1_jaxref_r8_a4a2a6'

def setup_inputs(seed: int=0):
    np.random.seed(seed)
    _w = jnp.asarray

    def _L0_attn_setup():
        import jax, jax.numpy as jnp
        import numpy as np
        B, S, D = (2, 256, 128)
        H, P = (16, 64)
        NUM_OUT = 128
        key = jax.random.key(seed)
        ks = jax.random.split(key, 9)
        sc = 0.05
        return {'x': jax.random.normal(ks[0], (B, S, D), jnp.float32), 'q_w': jax.random.normal(ks[1], (H, P, D), jnp.float32) * sc, 'q_b': jax.random.normal(ks[2], (H, 1, P), jnp.float32) * sc, 'k_w': jax.random.normal(ks[3], (H, P, D), jnp.float32) * sc, 'k_b': jax.random.normal(ks[4], (H, 1, P), jnp.float32) * sc, 'v_w': jax.random.normal(ks[5], (H, P, D), jnp.float32) * sc, 'v_b': jax.random.normal(ks[6], (H, 1, P), jnp.float32) * sc, 'l_w': jax.random.normal(ks[7], (NUM_OUT, P * H), jnp.float32) * sc, 'l_b': jax.random.normal(ks[8], (1, NUM_OUT), jnp.float32) * sc}
    _L0_attn_in = _L0_attn_setup()

    def _L0_ffn_setup():
        import jax, jax.numpy as jnp
        import numpy as np
        DIM = 128
        DEPTH = 6
        HEADS = 16
        DIM_HEAD = 64
        WINDOW = 32
        INNER = HEADS * DIM_HEAD
        DIM_INNER = int(DIM * 4 * 2 / 3)
        QK_SCALE = 8.0

        def shift_tokens(t):
            a, s = jnp.split(t, 2, -1)
            s = jnp.pad(s, ((0, 0), (1, 0), (0, 0)))[:, :-1]
            return jnp.concatenate([a, s], -1)

        def l2norm(t):
            return t / jnp.maximum(jnp.linalg.norm(t, axis=-1, keepdims=True), 1e-12)

        def rotate_half(x):
            x1, x2 = jnp.split(x, 2, -1)
            return jnp.concatenate([-x2, x1], -1)

        def rotary_tables(n):
            half = jnp.arange(0, DIM_HEAD, 2, dtype=jnp.float32)
            inv_freq = 1.0 / 10000.0 ** (half / DIM_HEAD)
            t = jnp.arange(n, dtype=jnp.float32)
            freqs = t[:, None] * inv_freq[None, :]
            freqs = jnp.concatenate([freqs, freqs], -1)
            base_scale = (half + 0.4 * DIM_HEAD) / (1.4 * DIM_HEAD)
            power = (t - n // 2) / (WINDOW // 2)
            scale = base_scale[None, :] ** power[:, None]
            scale = jnp.concatenate([scale, scale], -1)
            return (freqs, scale)

        def local_attention(q, k, v):
            b, h, n, d = q.shape
            w = WINDOW
            nw = n // w
            bq = q.reshape(b, h, nw, w, d)
            bk = k.reshape(b, h, nw, w, d)
            bv = v.reshape(b, h, nw, w, d)

            def look(t):
                p = jnp.pad(t, ((0, 0), (0, 0), (1, 0), (0, 0), (0, 0)))
                return jnp.concatenate([p[:, :, :nw], p[:, :, 1:]], axis=3)
            bk2, bv2 = (look(bk), look(bv))
            seq = jnp.arange(n).reshape(nw, w)
            seq_p = jnp.pad(seq, ((1, 0), (0, 0)), constant_values=-1)
            jt = jnp.concatenate([seq_p[:nw], seq_p[1:]], axis=1)
            it = seq[:, :, None]
            jb = jt[:, None, :]
            mask = (it < jb) | (it > jb + w) | (jb == -1)
            sim = jnp.einsum('bhwie,bhwje->bhwij', bq, bk2) * QK_SCALE
            sim = jnp.where(mask, -jnp.finfo(sim.dtype).max, sim)
            attn = jax.nn.softmax(sim, -1)
            out = jnp.einsum('bhwij,bhwje->bhwie', attn, bv2)
            return out.reshape(b, h, n, d)

        def attn_layer(x, Wqkv, qs, ksc, Wo):
            b, n, _ = x.shape
            qkv = x @ Wqkv
            q, k, v = jnp.split(qkv, 3, -1)
            sh = lambda t: t.reshape(b, n, HEADS, DIM_HEAD).transpose(0, 2, 1, 3)
            q, k, v = (sh(q), sh(k), sh(v))
            q = l2norm(q) * qs
            k = l2norm(k) * ksc
            freqs, scale = rotary_tables(n)
            cos, sin = (jnp.cos(freqs), jnp.sin(freqs))
            q = q * cos * scale + rotate_half(q) * sin * scale
            inv = 1.0 / scale
            k = k * cos * inv + rotate_half(k) * sin * inv
            out = local_attention(q, k, v)
            out = out.transpose(0, 2, 1, 3).reshape(b, n, INNER)
            return out @ Wo

        def ffn_layer(x, g, bln, W1, b1, W2, b2):
            mu = x.mean(-1, keepdims=True)
            var = ((x - mu) ** 2).mean(-1, keepdims=True)
            xn = (x - mu) / jnp.sqrt(var + 1e-05) * g + bln
            hg = xn @ W1 + b1
            a, gate = jnp.split(hg, 2, -1)
            return a * jax.nn.gelu(gate, approximate=False) @ W2 + b2
        key = jax.random.key(seed)
        ks = jax.random.split(key, 8)
        B, N = (2, 256)
        init = lambda k, shape: jax.random.normal(k, shape, jnp.float32) * 0.02
        return {'x': jax.random.normal(ks[0], (B, N, DIM), jnp.float32), 'Wqkv': init(ks[1], (DEPTH, DIM, 3 * INNER)), 'q_scale': jnp.ones((DEPTH, DIM_HEAD), jnp.float32), 'k_scale': jnp.ones((DEPTH, DIM_HEAD), jnp.float32), 'Wo': init(ks[2], (DEPTH, INNER, DIM)), 'ln_g': jnp.ones((DEPTH, DIM), jnp.float32), 'ln_b': jnp.zeros((DEPTH, DIM), jnp.float32), 'W1': init(ks[3], (DEPTH, DIM, 2 * DIM_INNER)), 'b1': jnp.zeros((DEPTH, 2 * DIM_INNER), jnp.float32), 'W2': init(ks[4], (DEPTH, DIM_INNER, DIM)), 'b2': jnp.zeros((DEPTH, DIM), jnp.float32)}
    _L0_ffn_in = _L0_ffn_setup()
    _d = {'L0_attn_x': _L0_attn_in['x'], 'L0_attn_q_w': _L0_attn_in['q_w'], 'L0_attn_q_b': _L0_attn_in['q_b'], 'L0_attn_k_w': _L0_attn_in['k_w'], 'L0_attn_k_b': _L0_attn_in['k_b'], 'L0_attn_v_w': _L0_attn_in['v_w'], 'L0_attn_v_b': _L0_attn_in['v_b'], 'L0_attn_l_w': _L0_attn_in['l_w'], 'L0_attn_l_b': _L0_attn_in['l_b'], 'L0_ffn_Wqkv': _L0_ffn_in['Wqkv'], 'L0_ffn_q_scale': _L0_ffn_in['q_scale'], 'L0_ffn_k_scale': _L0_ffn_in['k_scale'], 'L0_ffn_Wo': _L0_ffn_in['Wo'], 'L0_ffn_ln_g': _L0_ffn_in['ln_g'], 'L0_ffn_ln_b': _L0_ffn_in['ln_b'], 'L0_ffn_W1': _L0_ffn_in['W1'], 'L0_ffn_b1': _L0_ffn_in['b1'], 'L0_ffn_W2': _L0_ffn_in['W2'], 'L0_ffn_b2': _L0_ffn_in['b2']}
    _x0 = _d['L0_attn_x']
    _d['L0_attn_x'] = jax.random.normal(jax.random.fold_in(jax.random.key(seed), 1), (8, 256, 128), dtype=_x0.dtype)
    del _x0
    return _d

def reference(L0_attn_x, L0_attn_q_w, L0_attn_q_b, L0_attn_k_w, L0_attn_k_b, L0_attn_v_w, L0_attn_v_b, L0_attn_l_w, L0_attn_l_b, L0_ffn_Wqkv, L0_ffn_q_scale, L0_ffn_k_scale, L0_ffn_Wo, L0_ffn_ln_g, L0_ffn_ln_b, L0_ffn_W1, L0_ffn_b1, L0_ffn_W2, L0_ffn_b2):

    def _L0_attn_ref(x, q_w, q_b, k_w, k_b, v_w, v_b, l_w, l_b):
        import jax, jax.numpy as jnp
        import numpy as np
        B, S, D = (2, 256, 128)
        H, P = (16, 64)
        NUM_OUT = 128
        q = jnp.einsum('bsd,hpd->bhsp', x, q_w) + q_b
        k = jnp.einsum('bsd,hpd->bhsp', x, k_w) + k_b
        v = jnp.einsum('bsd,hpd->bhsp', x, v_w) + v_b
        scores = jnp.einsum('bhqp,bhkp->bhqk', q, k) / jnp.sqrt(jnp.float32(P))
        attn = jax.nn.softmax(scores, axis=2)
        ctx = jnp.einsum('bhqk,bhkp->bqhp', attn, v)
        concat = ctx.reshape(ctx.shape[0], ctx.shape[1], H * P)
        out = concat @ l_w.T + l_b
        return out

    def _L0_ffn_ref(x, Wqkv, q_scale, k_scale, Wo, ln_g, ln_b, W1, b1, W2, b2):
        import jax, jax.numpy as jnp
        import numpy as np
        DIM = 128
        DEPTH = 6
        HEADS = 16
        DIM_HEAD = 64
        WINDOW = 32
        INNER = HEADS * DIM_HEAD
        DIM_INNER = int(DIM * 4 * 2 / 3)
        QK_SCALE = 8.0

        def shift_tokens(t):
            a, s = jnp.split(t, 2, -1)
            s = jnp.pad(s, ((0, 0), (1, 0), (0, 0)))[:, :-1]
            return jnp.concatenate([a, s], -1)

        def l2norm(t):
            return t / jnp.maximum(jnp.linalg.norm(t, axis=-1, keepdims=True), 1e-12)

        def rotate_half(x):
            x1, x2 = jnp.split(x, 2, -1)
            return jnp.concatenate([-x2, x1], -1)

        def rotary_tables(n):
            half = jnp.arange(0, DIM_HEAD, 2, dtype=jnp.float32)
            inv_freq = 1.0 / 10000.0 ** (half / DIM_HEAD)
            t = jnp.arange(n, dtype=jnp.float32)
            freqs = t[:, None] * inv_freq[None, :]
            freqs = jnp.concatenate([freqs, freqs], -1)
            base_scale = (half + 0.4 * DIM_HEAD) / (1.4 * DIM_HEAD)
            power = (t - n // 2) / (WINDOW // 2)
            scale = base_scale[None, :] ** power[:, None]
            scale = jnp.concatenate([scale, scale], -1)
            return (freqs, scale)

        def local_attention(q, k, v):
            b, h, n, d = q.shape
            w = WINDOW
            nw = n // w
            bq = q.reshape(b, h, nw, w, d)
            bk = k.reshape(b, h, nw, w, d)
            bv = v.reshape(b, h, nw, w, d)

            def look(t):
                p = jnp.pad(t, ((0, 0), (0, 0), (1, 0), (0, 0), (0, 0)))
                return jnp.concatenate([p[:, :, :nw], p[:, :, 1:]], axis=3)
            bk2, bv2 = (look(bk), look(bv))
            seq = jnp.arange(n).reshape(nw, w)
            seq_p = jnp.pad(seq, ((1, 0), (0, 0)), constant_values=-1)
            jt = jnp.concatenate([seq_p[:nw], seq_p[1:]], axis=1)
            it = seq[:, :, None]
            jb = jt[:, None, :]
            mask = (it < jb) | (it > jb + w) | (jb == -1)
            sim = jnp.einsum('bhwie,bhwje->bhwij', bq, bk2) * QK_SCALE
            sim = jnp.where(mask, -jnp.finfo(sim.dtype).max, sim)
            attn = jax.nn.softmax(sim, -1)
            out = jnp.einsum('bhwij,bhwje->bhwie', attn, bv2)
            return out.reshape(b, h, n, d)

        def attn_layer(x, Wqkv, qs, ksc, Wo):
            b, n, _ = x.shape
            qkv = x @ Wqkv
            q, k, v = jnp.split(qkv, 3, -1)
            sh = lambda t: t.reshape(b, n, HEADS, DIM_HEAD).transpose(0, 2, 1, 3)
            q, k, v = (sh(q), sh(k), sh(v))
            q = l2norm(q) * qs
            k = l2norm(k) * ksc
            freqs, scale = rotary_tables(n)
            cos, sin = (jnp.cos(freqs), jnp.sin(freqs))
            q = q * cos * scale + rotate_half(q) * sin * scale
            inv = 1.0 / scale
            k = k * cos * inv + rotate_half(k) * sin * inv
            out = local_attention(q, k, v)
            out = out.transpose(0, 2, 1, 3).reshape(b, n, INNER)
            return out @ Wo

        def ffn_layer(x, g, bln, W1, b1, W2, b2):
            mu = x.mean(-1, keepdims=True)
            var = ((x - mu) ** 2).mean(-1, keepdims=True)
            xn = (x - mu) / jnp.sqrt(var + 1e-05) * g + bln
            hg = xn @ W1 + b1
            a, gate = jnp.split(hg, 2, -1)
            return a * jax.nn.gelu(gate, approximate=False) @ W2 + b2
        for i in range(DEPTH):
            x = attn_layer(shift_tokens(x), Wqkv[i], q_scale[i], k_scale[i], Wo[i]) + x
            x = ffn_layer(shift_tokens(x), ln_g[i], ln_b[i], W1[i], b1[i], W2[i], b2[i]) + x
        return x
    x = L0_attn_x
    x = _layernorm(x + _L0_attn_ref(x, L0_attn_q_w, L0_attn_q_b, L0_attn_k_w, L0_attn_k_b, L0_attn_v_w, L0_attn_v_b, L0_attn_l_w, L0_attn_l_b), axis=-1)
    x = _layernorm(x + _L0_ffn_ref(x, L0_ffn_Wqkv, L0_ffn_q_scale, L0_ffn_k_scale, L0_ffn_Wo, L0_ffn_ln_g, L0_ffn_ln_b, L0_ffn_W1, L0_ffn_b1, L0_ffn_W2, L0_ffn_b2), axis=-1)
    return x

_drawn_inputs = setup_inputs


def setup_inputs(seed=0):
    import zlib

    import numpy as np

    out = dict(_drawn_inputs(seed))
    spreads = {'L0_ffn_q_scale': (1.0, 0.6),
     'L0_ffn_k_scale': (1.0, 0.6),
     'L0_ffn_ln_g': (1.0, 0.6),
     'L0_ffn_ln_b': (0.0, 0.8),
     'L0_ffn_b1': (0.0, 0.8),
     'L0_ffn_b2': (0.0, 0.1)}
    factors = {'L0_attn_q_b': 8.0, 'L0_attn_k_b': 8.0, 'L0_ffn_W1': 3.668, 'L0_ffn_W2': 3.605}
    for name, (base, spread) in spreads.items():
        noise = np.random.default_rng([zlib.crc32(name.encode()), seed]).standard_normal(out[name].shape)
        drawn = base * np.exp(spread * noise) if base else spread * noise
        out[name] = jnp.asarray(drawn.astype(out[name].dtype))
    for name, factor in factors.items():
        out[name] = (out[name] * factor).astype(out[name].dtype)
    return out
```

```python
from contextlib import ExitStack

import numpy as np

import concourse.bass as bass
from concourse import mybir

F32 = mybir.dt.float32
BF16 = mybir.dt.bfloat16
ALU = mybir.AluOpType
ACT = mybir.ActivationFunctionType
AX = mybir.AxisListType

PARTS = 128
BATCHES, TOKENS, DIM = 8, 256, 128
HEADS, HEAD = 16, 64
INNER = HEADS * HEAD
PAIRS = HEADS // 2
LAYERS = 6
WINDOW = 32
TILES = TOKENS // PARTS
GROUPS = 4
PER_GROUP = HEADS // GROUPS
FF = int(DIM * 4 * 2 / 3)
FF_CHUNKS = [(0, 128), (128, 128), (256, FF - 256)]
UNITS = LAYERS * BATCHES
RING = 2 * BATCHES
EPS = 1e-5
QK_SCALE = 8.0
MASKED = -1e30
VW = HEAD + 1


def constants():
    ident = np.eye(PARTS, dtype=np.float32)
    mean = np.full((PARTS, PARTS), 1.0 / DIM, np.float32)
    q, k = np.arange(PARTS)[:, None], np.arange(PARTS)[None, :]
    band = np.where((q < k) | (q > k + WINDOW), np.float32(MASKED), np.float32(0))
    corner = np.zeros((PARTS, WINDOW), np.float32)
    corner[:WINDOW] = np.where(np.arange(WINDOW)[:, None] > np.arange(WINDOW)[None, :], MASKED, 0)
    half = np.arange(0, HEAD, 2, dtype=np.float32)
    inv_freq = (1.0 / 10000.0 ** (half / HEAD)).astype(np.float32)
    t = np.arange(TOKENS, dtype=np.float32)
    freqs = t[:, None] * inv_freq[None, :]
    freqs = np.concatenate([freqs, freqs], -1).astype(np.float64)
    base = ((half + 0.4 * HEAD) / (1.4 * HEAD)).astype(np.float32)
    scale = base[None, :].astype(np.float64) ** ((t - TOKENS // 2) / (WINDOW // 2))[:, None]
    scale = np.concatenate([scale, scale], -1)
    sign = np.where(np.arange(HEAD) < HEAD // 2, -1.0, 1.0)
    cos, sin = np.cos(freqs), np.sin(freqs) * sign
    tables = np.stack([cos * scale, sin * scale, cos / scale, sin / scale], 1).astype(np.float32)
    tables = tables.reshape(TILES, PARTS, 4, HEAD).transpose(1, 0, 2, 3)
    return {
        "ident": ident, "mean": mean, "centre": ident - mean, "band": band, "corner": corner,
        "rotary": np.ascontiguousarray(tables),
    }


class Unit:

    def __init__(self, n, par, count):
        self.n, self.par, self.count = n, par, count
        self.static = isinstance(n, int)
        self.live = not self.static or 0 <= n < count

    def back(self):
        return Unit(self.n - 1, 1 - self.par, self.count)


def lag(unit, s, k):
    return (unit, s - k) if s >= k else (unit.back(), s - k + 8)


def need(eng, sem, value):
    if not isinstance(value, int) or value > 0:
        eng.wait_ge(sem, value)


def over_units(eng, iteration, count, first, last):
    def at(i, par):
        iteration(Unit(i + 1, 1 - par, count), Unit(i, par, count), Unit(i - 1, 1 - par, count))

    for i in range(-1, first):
        at(i, i % 2)
    with eng.Fori(first, last, 2) as r:
        at(r, first % 2)
        at(r + 1, 1 - first % 2)
    for i in range(last, count + 2):
        at(i, i % 2)


def postln_kernel(nc, x, q_w, q_b, k_w, k_b, v_w, v_b, l_w, l_b, Wqkv, q_scale, k_scale, Wo,
                  ln_g, ln_b, W1, b1, W2, b2, ident_d, mean_d, centre_d, band_d, corner_d, rotary_d,
                  out):
    ctx = ExitStack()
    with ctx:
        def sb(name, shape, dt=F32):
            return ctx.enter_context(nc.sbuf_tensor(name, shape, dt))

        def sem(name):
            return ctx.enter_context(nc.semaphore(name))

        psA = [ctx.enter_context(nc.psum_tensor(f"psA{i}", [PARTS, 512], F32)) for i in range(2)]
        psS = [ctx.enter_context(nc.psum_tensor(f"psS{i}", [PARTS, 512], F32)) for i in range(2)]
        psT = [ctx.enter_context(nc.psum_tensor(f"psT{i}", [PARTS, 512], F32)) for i in range(2)]
        psX = ctx.enter_context(nc.psum_tensor("psX", [PARTS, 512], F32))
        psC = ctx.enter_context(nc.psum_tensor("psC", [PARTS, 512], F32))

        ident = sb("ident", [PARTS, PARTS])
        mean = sb("mean", [PARTS, PARTS])
        centre = sb("centre", [PARTS, PARTS])
        band = sb("band", [PARTS, PARTS])
        corner = sb("corner", [PARTS, WINDOW])
        rotary = sb("rotary", [PARTS, TILES * 4 * HEAD])
        ident_h = sb("ident_h", [PARTS, PARTS], BF16)
        band_h = sb("band_h", [PARTS, PER_GROUP, PARTS], BF16)
        corner_h = sb("corner_h", [PARTS, PAIRS, WINDOW], BF16)
        tables = sb("tables", [PARTS, LAYERS * TILES * 4 * HEAD])
        rows = sb("rows", [PARTS, PARTS])
        cols = sb("cols", [PARTS, PARTS])
        QB, KB, LB = 0, PAIRS, 2 * PAIRS
        LNG = LB + 1
        LNB, B2, B1 = LNG + LAYERS, LNG + 2 * LAYERS, LNG + 3 * LAYERS
        qb, kb, lb = cols[:, QB:QB + PAIRS], cols[:, KB:KB + PAIRS], cols[:, LB:LB + 1]
        wqkv = sb("wqkv", [PARTS, 2 * 3 * INNER])
        wo = sb("wo", [PARTS, PAIRS, DIM])
        w1 = sb("w1", [PARTS, 2 * FF])
        w2 = sb("w2", [PARTS, 3, DIM])
        X = sb("X", [PARTS, RING * TOKENS])
        x1 = sb("x1", [PARTS, BATCHES * TOKENS])
        arena = sb("arena", [PARTS, 8192])
        taken = [0]

        def part(columns, view=None, **sizes):
            ap = arena[:, taken[0]:taken[0] + columns]
            taken[0] += columns
            return ap.rearrange(view, **sizes) if view else ap

        wT = part(4 * INNER, "p (m n) -> p m n", m=4)
        xraw = part(BATCHES * TOKENS, "p (t d) -> p t d", d=DIM)
        raw_l = part(INNER, "p (c n) -> p c n", n=PARTS)
        vb = part(INNER)
        raw = [wqkv[:, (3 + i) * INNER:(4 + i) * INNER].rearrange("p (c n) -> p c n", n=PARTS) for i in range(3)] + [raw_l]
        taken[0] = 0
        sq, qn, qc, qs = ([part(512) for _ in range(2)] for _ in range(4))
        PT = [part(512) for _ in range(2)]
        gate, hid = (part(3 * TOKENS, "p (c t) -> p c t", c=3) for _ in range(2))
        Sc = part(HEADS * WINDOW, "p (h k) -> p h k", k=WINDOW)[0:WINDOW]
        cn = [part(PER_GROUP * HEAD) for _ in range(2)]
        xn, xg = part(TOKENS), part(TOKENS)
        xs1 = [sb(f"xs1_{i}", [PARTS, TOKENS]) for i in range(2)]
        xs = [sb(f"xs{i}", [PARTS, TOKENS]) for i in range(2)]
        qT = [sb(f"qT{i}", [PARTS, PAIRS, TOKENS]) for i in range(2)]
        kT = [sb(f"kT{i}", [PARTS, PAIRS, TOKENS]) for i in range(2)]
        V = sb("V", [PARTS, 2, TILES, HEADS, VW])
        Vc_all = sb("Vc", [PARTS, 2 * HEADS * VW])
        Vc = Vc_all[0:WINDOW, :].rearrange("p (a h e) -> p a h e", a=2, e=VW)
        scales = Vc_all[:, 0:LAYERS * 4 * HEAD].rearrange("p (l j d) -> p l j d", l=LAYERS, j=4)
        cT = [sb(f"cT{i}", [PARTS, PAIRS, TOKENS]) for i in range(2)]
        n2 = [sb(f"n2{i}", [PARTS, 8]) for i in range(2)]
        rn = [sb(f"rn{i}", [PARTS, 8]) for i in range(2)]
        E = [sb(f"E{i}", [PARTS, 512]) for i in range(4)]
        mx = [sb(f"mx{i}", [PARTS, PER_GROUP]) for i in range(2)]
        nm = [sb(f"nm{i}", [PARTS, 2]) for i in range(2)]
        sums = [sb(f"sums{i}", [PARTS, 2]) for i in range(4)]
        rinv = [sb(f"rinv{i}", [PARTS, 4]) for i in range(4)]
        Vs = [sb(f"Vs{i}", [PARTS, 2, HEAD]) for i in range(4)]
        mc = sb("mc", [WINDOW, HEADS])
        Ec = [sb(f"Ec{i}", [WINDOW, 128]) for i in range(2)]
        PcT = [sb(f"PcT{i}", [WINDOW, 128]) for i in range(2)]
        xr = [sb(f"xr{i}", [PARTS, TOKENS]) for i in range(2)]
        xsh = [sb(f"xsh{i}", [PARTS, TOKENS]) for i in range(2)]
        csq = sb("csq", [PARTS, 512])
        rstd = sb("rstd", [PARTS, 512])
        var_eps = sb("var_eps", [PARTS, 512])
        minus_half = sb("minus_half", [PARTS, 1])
        y = [qT[0][:, 2 * i:2 * i + 2, :].rearrange("p c t -> p (c t)") for i in range(2)]
        yn = [qT[1][:, 2 * i:2 * i + 2, :].rearrange("p c t -> p (c t)") for i in range(2)]
        yo = [kT[0][:, 2 * i:2 * i + 2, :].rearrange("p c t -> p (c t)") for i in range(2)]

        x_in = sem("x_in")
        raw_in = [sem(f"raw_in{i}") for i in range(4)]
        ident_in = sem("ident_in")
        const_in = sem("const_in")
        bias_in = sem("bias_in")
        param_in = sem("param_in")
        scale_in = sem("scale_in")
        wqkv_in = sem("wqkv_in")
        wo_in = sem("wo_in")
        w1_in = sem("w1_in")
        w2_in = sem("w2_in")
        vc_in = sem("vc_in")
        stored = [sem(f"stored{i}") for i in range(4)]
        sp_passed = sem("sp_passed")
        pool_passed = sem("pool_passed")
        halves_ready = sem("halves_ready")
        cleared = sem("cleared")
        tables_ready = sem("tables_ready")
        turned = sem("turned")
        turned_out = sem("turned_out")
        xs1_ready = sem("xs1_ready")
        proj1 = sem("proj1")
        qk1_stored = sem("qk1_stored")
        v1_stored = sem("v1_stored")
        score1 = sem("score1")
        max1 = sem("max1")
        nm1 = sem("nm1")
        exp1 = sem("exp1")
        rinv1 = sem("rinv1")
        vs1 = sem("vs1")
        pv1 = sem("pv1")
        ctx1 = sem("ctx1")
        wl_done = sem("wl_done")
        resid1 = sem("resid1")
        centred1 = sem("centred1")
        csq1 = sem("csq1")
        var1 = sem("var1")
        eps1 = sem("eps1")
        rstd1 = sem("rstd1")
        x_written = sem("x_written")
        x1_kept = sem("x1_kept")
        xs_ready = sem("xs_ready")
        proj_done = sem("proj_done")
        squared = sem("squared")
        summed = sem("summed")
        guarded = sem("guarded")
        rn_ready = sem("rn_ready")
        normed = sem("normed")
        cos_done = sem("cos_done")
        sin_done = sem("sin_done")
        rotated = sem("rotated")
        v_stored = sem("v_stored")
        a_turned = sem("a_turned")
        a_stored = sem("a_stored")
        scored = sem("scored")
        maxed = sem("maxed")
        shifted = sem("shifted")
        exped = sem("exped")
        p_turned = sem("p_turned")
        p_stored = sem("p_stored")
        corner_maxed = sem("corner_maxed")
        corner_stored = sem("corner_stored")
        corner_shifted = sem("corner_shifted")
        corner_exped = sem("corner_exped")
        corner_turned = sem("corner_turned")
        pv_done = sem("pv_done")
        recip_done = sem("recip_done")
        ctx_normed = sem("ctx_normed")
        ctx_turned = sem("ctx_turned")
        ctx_stored = sem("ctx_stored")
        wo_done = sem("wo_done")
        resid = sem("resid")
        xsh_ready = sem("xsh_ready")
        centred = sem("centred")
        csq_done = sem("csq_done")
        var_done = sem("var_done")
        eps_added = sem("eps_added")
        rstd_done = sem("rstd_done")
        xn_done = sem("xn_done")
        xg_done = sem("xg_done")
        gates_done = sem("gates_done")
        gate_stored = sem("gate_stored")
        gelu_done = sem("gelu_done")
        a_done = sem("a_done")
        hid_done = sem("hid_done")
        hid2_done = sem("hid2_done")
        w2_done = sem("w2_done")
        y_ready = sem("y_ready")
        y_centred = sem("y_centred")
        y_sq = sem("y_sq")
        y_var = sem("y_var")
        y_eps = sem("y_eps")
        y_rstd = sem("y_rstd")
        y_normed = sem("y_normed")
        y_turned = sem("y_turned")
        y_out = sem("y_out")

        def use_qk(s):
            return s + s // 2

        def use_v(w):
            return 3 * w + 2

        def use_s(s):
            return s + 2 * (s > 3)

        CORNER_USE = 4

        def chunk_of(g, k):
            return 4 * (g // 2) + g % 2 + 2 * k

        def head_of(g, j):
            return 2 * PER_GROUP * (g // 2) + 2 * j + g % 2

        def table(layer, tile, which):
            return bass.ds(((layer * TILES + tile) * 4 + which) * HEAD, HEAD)

        def layer_of(n):
            if isinstance(n, int):
                return n // BATCHES
            return nc.s_assert_within(n >> 3, 0, LAYERS - 1, skip_runtime_bounds_check_because="a unit's number is under UNITS")

        def slot(u, first=0, count=TOKENS):
            return bass.ds((u & (RING - 1)) * TOKENS + first, count)

        def heads8(ap):
            return ap.rearrange("p (h d) -> p h d", d=HEAD)

        block = ctx.enter_context(nc.Block())

        @block.sync
        def _(sp):
            sp.dma_start(ident[:, :], ident_d).then_inc(ident_in, 16)
            sp.dma_start(raw[0], q_w.rearrange("(c a) p d -> (a p) c d", a=2)).then_inc(raw_in[0], 16)
            sp.dma_start(xraw[:, :, :], x.rearrange("b (t p) d -> p (b t) d", p=PARTS)).then_inc(x_in, 16)
            sp.dma_start(raw[1], k_w.rearrange("(c a) p d -> (a p) c d", a=2)).then_inc(raw_in[1], 16)
            sp.dma_start(raw[2], v_w.rearrange("(c a) p d -> (a p) c d", a=2)).then_inc(raw_in[2], 16)
            sp.dma_start(raw[3], l_w.rearrange("o (c p) -> o c p", p=PARTS)).then_inc(raw_in[3], 16)
            sp.wait_ge(cleared, 1)
            for at, src in ((QB, q_b.rearrange("(c a) o p -> c (a o p)", a=2)), (KB, k_b.rearrange("(c a) o p -> c (a o p)", a=2)),
                            (LB, l_b), (LNG, ln_g), (LNB, ln_b), (B2, b2)):
                sp.dma_start(rows[at:at + src.shape[0], :], src).then_inc(param_in, 16)
            for c, (off, m) in enumerate(FF_CHUNKS):
                for k in range(2):
                    at = B1 + (3 * k + c) * LAYERS
                    sp.dma_start(rows[at:at + LAYERS, 0:m], b1[:, k * FF + off:k * FF + off + m]).then_inc(param_in, 16)
            sp.dma_start(vb[:, :], v_b.rearrange("h o p -> (o h p)").partition_broadcast(PARTS)).then_inc(bias_in, 16)
            for dst, src in ((mean, mean_d), (centre, centre_d), (band, band_d), (corner, corner_d), (rotary, rotary_d)):
                sp.dma_start(dst[:, :], src).then_inc(const_in, 16)
            for j, src in enumerate((q_scale, q_scale, k_scale, k_scale)):
                if j % 2 == 0:
                    sp.dma_start(scales[:, :, j, :], src.partition_broadcast(PARTS)).then_inc(scale_in, 16)
                    continue
                h = HEAD // 2
                sp.dma_start(scales[:, :, j, 0:h], src[:, h:HEAD].partition_broadcast(PARTS)).then_inc(scale_in, 16)
                sp.dma_start(scales[:, :, j, h:HEAD], src[:, 0:h].partition_broadcast(PARTS)).then_inc(scale_in, 16)

            def load_wqkv(layer):
                sp.dma_start(wqkv[:, bass.ds((layer & 1) * (3 * INNER), 3 * INNER)], Wqkv[bass.ds(layer, 1)].rearrange("o d n -> d (o n)")).then_inc(wqkv_in, 16)

            def load_wo(layer):
                heads = Wo[bass.ds(layer, 1)].rearrange("o (g a r p) d -> a p (o g) r d", g=GROUPS, a=2, r=2)
                for k in range(2):
                    for r in range(2):
                        sp.dma_start(wo[64 * k:64 * k + 64, r:PAIRS:2, :], heads[k][:, :, r, :]).then_inc(wo_in, 16)

            def load_w1(layer):
                sp.dma_start(w1[:, :], W1[bass.ds(layer, 1)].rearrange("o d n -> d (o n)")).then_inc(w1_in, 16)

            def load_w2(layer):
                sp.dma_start(w2[:, 0:2, :], W2[bass.ds(layer, 1), 0:256, :].rearrange("o (c p) d -> p (o c) d", p=PARTS)).then_inc(w2_in, 16)
                sp.dma_start(w2[0:FF - 256, 2, :], W2[bass.ds(layer, 1), 256:FF, :].rearrange("o p d -> p (o d)")).then_inc(w2_in, 16)

            load_wqkv(0)
            load_wo(0)
            load_w1(0)
            load_w2(0)

            def corner_values(u):
                sp.wait_ge(v_stored, 4 * u + 2)
                sp.sem_inc(sp_passed, 1)
                need(sp, pv_done, 8 * u - 3)
                sp.sem_inc(sp_passed, 1)
                sp.dma_start(Vc[:, bass.ds(u & 1, 1)], V[PARTS - WINDOW:PARTS, bass.ds(u & 1, 1), 0]).then_inc(vc_in, 16)

            corner_values(0)
            sp.wait_ge(proj_done, 12)
            load_wqkv(1)
            corner_values(1)
            with sp.Fori(2, 9) as u:
                corner_values(u)

            def next_layer(layer, units, two_ahead):
                sp.wait_ge(wo_done, layer * BATCHES)
                sp.sem_inc(sp_passed, 1)
                load_wo(layer)
                if two_ahead:
                    sp.wait_ge(proj_done, layer * (BATCHES * 12) + 12)
                    sp.sem_inc(sp_passed, 1)
                    load_wqkv(layer + 1)
                corner_values(layer * BATCHES + 1)
                sp.wait_ge(a_done, layer * BATCHES)
                sp.sem_inc(sp_passed, 1)
                load_w1(layer)
                sp.wait_ge(w2_done, layer * BATCHES)
                sp.sem_inc(sp_passed, 1)
                load_w2(layer)
                with sp.Fori(2, 2 + units) as k:
                    corner_values(layer * BATCHES + k)

            with sp.Fori(1, LAYERS - 1) as layer:
                next_layer(layer, 7, True)
            next_layer(LAYERS - 1, 6, False)

            for k in range(4):
                sp.wait_ge(y_out, k + 1)
                sp.dma_start(out.rearrange("b (t p) d -> p (b t) d", p=PARTS)[:, 4 * k:4 * k + 4, :],
                             yo[k % 2][:, :].rearrange("p (t d) -> p t d", d=DIM)).then_inc(stored[k], 16)
            for k in range(4):
                sp.wait_ge(stored[k], 16)

        @block.gpsimd
        def _(pool):
            nc.gpsimd.memset(rows[:, :], 0.0).then_inc(cleared, 1)
            nc.gpsimd.memset(minus_half[:, :], -0.5).then_inc(cleared, 1)
            nc.gpsimd.memset(V[:, :, :, :, :].rearrange("p a t h e -> p (a t h) e")[:, :, HEAD:VW], 1.0).then_inc(cleared, 1)
            pool.wait_ge(cleared, 2)
            pool.wait_ge(const_in, 16 * 5)
            pool.wait_ge(scale_in, 16 * 6)
            rot = rotary[:, :].rearrange("p (t n) -> p t n", t=TILES)
            tab = tables[:, :].rearrange("p (l t n) -> p l t n", l=LAYERS, t=TILES)
            for layer in range(LAYERS):
                for tile in range(TILES):
                    nc.gpsimd.tensor_tensor(tab[:, layer, tile, :], rot[:, tile, :],
                                            scales[:, layer].rearrange("p a d -> p (a d)"), ALU.mult).then_inc(tables_ready, 1)

            def rsqrt(dst, src):
                return nc.gpsimd.tensor_tensor(dst, src, minus_half[:, :].to_broadcast(list(src.shape)), ALU.pow)

            def first_attention(a, b, c):
                if c.live:
                    pool.wait_ge(eps1, c.n + 1)
                    rsqrt(rstd[:, 0:256], var_eps[:, 0:256]).then_inc(rstd1, 1)

            over_units(pool, first_attention, BATCHES, 2, BATCHES - 2)

            def iteration(a, b, c):
                c1 = c.back()
                for s in range(8):
                    if c1.live and s == 1:
                        m = FF_CHUNKS[2][1]
                        pool.wait_ge(gelu_done, 2 * c1.n + 1)
                        pool.wait_ge(gate_stored, 2 * c1.n + 2)
                        nc.gpsimd.tensor_tensor(hid[0:m, 2, :], hid[0:m, 2, :], gate[0:m, 2, :], ALU.mult).then_inc(hid2_done, 1)
                    if c.live and s == 5:
                        pool.wait_ge(eps_added, c.n + 1)
                        need(pool, xn_done, c.n)
                        rsqrt(rstd[:, 0:256], var_eps[:, 0:256]).then_inc(rstd_done, 1)
                    if a.live:
                        tile, which = s // 4, s % 2
                        pool.wait_ge(guarded, 8 * a.n + s + 1)
                        need(pool, normed, 8 * a.n + s - 1)
                        rsqrt(rn[s % 2][:, :], n2[s % 2][:, :]).then_inc(rn_ready, 1)
                        pool.wait_ge(normed, 8 * a.n + s + 1)
                        need(pool, a_turned, 8 * a.n + s - 1)
                        pool.sem_inc(pool_passed, 1)
                        nc.gpsimd.tensor_tensor(
                            heads8(qs[s % 2][:, :]).rearrange("p h (a d) -> p h a d", a=2),
                            heads8(qn[s % 2][:, :]).rearrange("p h (a d) -> p h a d", a=2)[:, :, ::-1, :],
                            tables[:, table(layer_of(a.n), tile, 2 * which + 1)].rearrange("p (o a d) -> p o a d", o=1, a=2)
                            .to_broadcast([PARTS, 8, 2, HEAD // 2]), ALU.mult).then_inc(sin_done, 1)
                        pool.wait_ge(sin_done, 8 * a.n + s + 1)
                        pool.wait_ge(cos_done, 8 * a.n + s + 1)
                        nc.gpsimd.tensor_tensor(qs[s % 2][:, :], qs[s % 2][:, :], qc[s % 2][:, :], ALU.add).then_inc(rotated, 1)

            pool.wait_ge(tables_ready, LAYERS * TILES)
            over_units(pool, iteration, UNITS, FIRST, LAST)

            for k in range(4):
                pool.wait_ge(y_eps, k + 1)
                need(pool, y_normed, k)
                rsqrt(rstd[:, :], var_eps[:, :]).then_inc(y_rstd, 1)

        @block.tensor
        def _(pe):
            pe.wait_ge(ident_in, 16)
            for n in range(12):
                if n < 4:
                    pe.wait_ge(x_in, 16)
                elif n % 2 == 0:
                    pe.wait_ge(raw_in[(n - 4) // 2], 16)
                need(pe, turned_out, n - 1)
                for j in range(4):
                    src = xraw[:, 4 * n + j, :] if n < 4 else raw[(n - 4) // 2][:, 4 * (n % 2) + j, :]
                    mm = nc.tensor.transpose(psT[n % 2][:, 128 * j:128 * j + 128], src, ident[:, :])
                mm.then_inc(turned, 1)
            pe.wait_ge(param_in, 16 * 12)
            pe.wait_ge(turned_out, 11)
            nc.tensor.transpose(psT[0][:, 0:128], rows[:, :], ident[:, :]).then_inc(turned, 1)
            pe.wait_ge(turned_out, 13)

            def first_attention(a, b, c):
                b1, c1 = b.back(), c.back()
                for s in range(8):
                    if b.live:
                        for j in range(2):
                            need(pe, exp1, 4 * (8 * b.n + s - 1) + 2 * j + 2)
                            if j == 0:
                                pe.wait_ge(qk1_stored, 8 * b.n + s + 1)
                            for t in range(2):
                                mm = nc.tensor.matmul(psS[j][:, 256 * t:256 * t + 256], kT[b.par][64 * j:64 * j + 64, s, 128 * t:128 * t + 128],
                                                      qT[b.par][64 * j:64 * j + 64, s, :], start=True, stop=True)
                            mm.then_inc(score1, 1)
                    if a.live:
                        n = use_qk(s)
                        if s == 0:
                            pe.wait_ge(xs1_ready, a.n + 1)
                        free1(pe, a, n)
                        nc.tensor.matmul(psA[n % 2][:, 0:256], wT[:, 0, 128 * s:128 * s + 128], xs1[a.par][:, :], start=True, stop=True)
                        nc.tensor.matmul(psA[n % 2][:, 256:512], wT[:, 1, 128 * s:128 * s + 128], xs1[a.par][:, :], start=True, stop=True).then_inc(proj1, 1)
                    ub, sb_ = lag(b, s, 1)
                    if ub.live:
                        need(pe, ctx1, 8 * ub.n + sb_)
                        for j in range(2):
                            pe.wait_ge(vs1, 2 * (8 * ub.n + sb_) + j + 1)
                            e = (sb_ % 2) * 2 + j
                            for t in range(2):
                                mm = nc.tensor.matmul(psX[64 * j:64 * j + 64, 0:256], Vs[e][:, t, :], E[e][:, 256 * t:256 * t + 256], start=t == 0, stop=t == 1)
                            mm.then_inc(pv1, 1)
                    if a.live and s % 2:
                        w = s // 2
                        n = use_v(w)
                        free1(pe, a, n)
                        nc.tensor.matmul(psA[n % 2][:, :], xs1[a.par][:, 128 * (w // 2):128 * (w // 2) + 128], wT[:, 2, 512 * (w % 2):512 * (w % 2) + 512],
                                         start=True, stop=True).then_inc(proj1, 1)
                    if c.live and s == 1:
                        pe.wait_ge(ctx1, 8 * c.n + 8)
                        need(pe, x_written, c.n)
                        for h in range(PAIRS):
                            mm = nc.tensor.matmul(psC[:, 0:256], wT[:, 3, 128 * h:128 * h + 128], cT[c.par][:, h, :], start=h == 0, stop=h == PAIRS - 1)
                        mm.then_inc(wl_done, 1)
                    if c.live and s == 2:
                        pe.wait_ge(resid1, c.n + 1)
                        nc.tensor.matmul(psC[:, 0:256], centre[:, :], xr[c.par][:, :], start=True, stop=True).then_inc(centred1, 1)
                    if c.live and s == 3:
                        pe.wait_ge(csq1, c.n + 1)
                        nc.tensor.matmul(psC[:, 256:512], mean[:, :], csq[:, 0:256], start=True, stop=True).then_inc(var1, 1)

            def free1(pe, a, n):
                u, k = (a.n, n - 2) if n >= 2 else (a.n - 1, n + 10)
                if k % 3 == 2:
                    need(pe, v1_stored, 4 * u + k // 3 + 1)
                else:
                    need(pe, qk1_stored, 8 * u + (k // 3) * 2 + k % 3 + 1)

            pe.wait_ge(const_in, 16 * 5)
            over_units(pe, first_attention, BATCHES, 2, BATCHES - 2)

            def free(a, n):
                u, k = (a.n, n - 2) if n >= 2 else (a.n - 1, n + 10)
                if k % 3 == 2:
                    need(pe, v_stored, 4 * u + k // 3 + 1)
                else:
                    need(pe, normed, 8 * u + (k // 3) * 2 + k % 3 + 1)

            def free_scores(b, k):
                u, k = (b.n, k - 2) if k >= 2 else (b.n - 1, k + 8)
                if CORNER_USE <= k < CORNER_USE + 2:
                    need(pe, corner_stored, 2 * u + k - CORNER_USE + 1)
                else:
                    need(pe, shifted, 8 * u + (k if k < CORNER_USE else k - 2) + 1)

            def free_turn(kinds):
                for s_, unit, slot in kinds:
                    if unit.live:
                        need(pe, s_, 8 * unit.n + slot + 1)

            def iteration(a, b, c):
                for s in range(8):
                    ap1, sa1 = lag(a, s, 3)
                    apa, sa = lag(a, s, 2)
                    bp1, sb1 = lag(b, s, 1)
                    bp2, sb2 = lag(b, s, 2)
                    bp3, sb3 = lag(b, s, 3)
                    bp4, sb4 = lag(b, s, 4)
                    if b.live and s == 4:
                        pe.wait_ge(a_stored, 8 * b.n + 8)
                        for r in range(2):
                            free_scores(b, CORNER_USE + r)
                            nc.tensor.matmul(psS[r][0:WINDOW, 0:256], ident_h[:, 0:WINDOW], corner_h[:, :, :].rearrange("p h k -> p (h k)"),
                                             start=True, stop=False, skip_group_check=True)
                            for h in range(PAIRS):
                                mm = nc.tensor.matmul(psS[r][0:WINDOW, WINDOW * h:WINDOW * h + WINDOW], qT[b.par][64 * r:64 * r + 64, h, PARTS:PARTS + WINDOW],
                                                      kT[b.par][64 * r:64 * r + 64, h, PARTS - WINDOW:PARTS], start=False, stop=h == PAIRS - 1, skip_group_check=True)
                            mm.then_inc(scored, 1)
                    if b.live:
                        tile, g = s // 4, s % 4
                        k = use_s(s) % 2
                        free_scores(b, use_s(s))
                        if s < 4:
                            pe.wait_ge(a_stored, 8 * b.n + (2 if g < 2 else 4))
                        nc.tensor.matmul(psS[k][:, :], ident_h[:, :], band_h[:, :, :].rearrange("p h k -> p (h k)"), start=True, stop=False, skip_group_check=True)
                        for j in range(PER_GROUP):
                            h = head_of(g, j)
                            r = 64 * (h % 2)
                            mm = nc.tensor.matmul(psS[k][:, 128 * j:128 * j + 128], qT[b.par][r:r + 64, h // 2, 128 * tile:128 * tile + 128],
                                                  kT[b.par][r:r + 64, h // 2, 128 * tile:128 * tile + 128], start=False, stop=j == PER_GROUP - 1, skip_group_check=True)
                        mm.then_inc(scored, 1)
                    if a.live:
                        tile, half, which = s // 4, (s // 2) % 2, s % 2
                        n = use_qk(s)
                        if s == 0:
                            pe.wait_ge(xs_ready, a.n + 1)
                            pe.wait_ge(wqkv_in, (layer_of(a.n) + 1) * 16)
                        free(a, n)
                        nc.tensor.matmul(psA[n % 2][:, :], xs[a.par][:, 128 * tile:128 * tile + 128],
                                         wqkv[:, bass.ds((layer_of(a.n) & 1) * (3 * INNER) + which * INNER + half * 512, 512)],
                                         start=True, stop=True).then_inc(proj_done, 1)
                    if bp1.live:
                        pe.wait_ge(exped, 8 * bp1.n + sb1 + 1)
                        free_turn([(a_stored, ap1, sa1)] + ([(p_stored, bp3, sb3), (ctx_stored, bp4, sb4)] if b.static else []))
                        for j in range(PER_GROUP):
                            mm = nc.tensor.transpose(psT[s % 2][:, 128 * j:128 * j + 128], E[sb1 % 2][:, 128 * j:128 * j + 128], ident[:, :])
                        mm.then_inc(p_turned, 1)
                    if a.live and s % 2:
                        w = s // 2
                        n = use_v(w)
                        free(a, n)
                        nc.tensor.matmul(psA[n % 2][:, :], xs[a.par][:, 128 * (w // 2):128 * (w // 2) + 128],
                                         wqkv[:, bass.ds((layer_of(a.n) & 1) * (3 * INNER) + 2 * INNER + (w % 2) * 512, 512)],
                                         start=True, stop=True).then_inc(proj_done, 1)
                    if apa.live:
                        apx, sax = lag(a, s, 4)
                        pe.wait_ge(rotated, 8 * apa.n + sa + 1)
                        free_turn([(ctx_stored, bp3, sb3)] + ([(a_stored, apx, sax), (p_stored, bp2, sb2)] if b.static else []))
                        for j in range(4):
                            mm = nc.tensor.transpose(psT[(s + 1) % 2][:, 128 * j:128 * j + 128], qs[sa % 2][:, 128 * j:128 * j + 128], ident[:, :])
                        mm.then_inc(a_turned, 1)
                    if bp1.live:
                        tile, g = sb1 // 4, sb1 % 4
                        pe.wait_ge(p_stored, 8 * bp1.n + sb1 + 1)
                        need(pe, ctx_normed, 8 * bp1.n + sb1)
                        pe.wait_ge(v_stored, 4 * bp1.n + 2 * tile + 2)
                        if tile == 1:
                            pe.wait_ge(corner_turned, 4 * bp1.n + g + 1)
                            pe.wait_ge(vc_in, (bp1.n + 1) * 16)
                        for j in range(PER_GROUP):
                            h = head_of(g, j)
                            mm = nc.tensor.matmul(psX[:, VW * j:VW * j + VW], PT[sb1 % 2][:, 128 * j:128 * j + 128], V[:, bp1.par, tile, h, :],
                                                  start=True, stop=tile == 0, skip_group_check=True)
                            if tile == 1:
                                mm = nc.tensor.matmul(psX[0:WINDOW, VW * j:VW * j + VW], PcT[sb1 % 2][:, 32 * j:32 * j + 32], Vc[:, bp1.par, h, :],
                                                      start=False, stop=True, skip_group_check=True)
                        mm.then_inc(pv_done, 1)
                    feed_forward(c, c.back(), s)
                    if bp2.live:
                        pe.wait_ge(ctx_normed, 8 * bp2.n + sb2 + 1)
                        free_turn([(p_stored, bp1, sb1)] + ([(a_stored, ap1, sa1), (ctx_stored, bp4, sb4)] if b.static else []))
                        for j in range(2):
                            mm = nc.tensor.transpose(psT[s % 2][:, 128 * j:128 * j + 128], cn[sb2 % 2][:, 128 * j:128 * j + 128], ident[:, :])
                        mm.then_inc(ctx_turned, 1)

            def feed_forward(c, c1, s):
                if c1.live and s == 0:
                    pe.wait_ge(gate_stored, 2 * c1.n + 2)
                    for k in range(2):
                        mm = nc.tensor.matmul(psC[:, 256 * k:256 * k + 256], w1[:, 128 * k:128 * k + 128], xg[:, :], start=True, stop=True)
                    mm.then_inc(a_done, 1)
                if c1.live and s == 1:
                    pe.wait_ge(hid_done, 2 * c1.n + 2)
                    pe.wait_ge(hid2_done, c1.n + 1)
                    pe.wait_ge(w2_in, (layer_of(c1.n) + 1) * 32)
                    for k, (off, m) in enumerate(FF_CHUNKS):
                        mm = nc.tensor.matmul(psC[:, 0:256], w2[0:m, k, :], hid[0:m, k, :], start=k == 0, stop=k == 2)
                    mm.then_inc(w2_done, 1)
                if not c.live:
                    return
                if s == 2:
                    pe.wait_ge(ctx_stored, 8 * c.n + 8)
                    pe.wait_ge(wo_in, (layer_of(c.n) + 1) * 64)
                    pe.wait_ge(x_written, c.n + BATCHES)
                    for h in range(PAIRS):
                        mm = nc.tensor.matmul(psC[:, 0:256], wo[:, h, :], cT[c.par][:, h, :], start=h == 0, stop=h == PAIRS - 1)
                    mm.then_inc(wo_done, 1)
                if s == 3:
                    pe.wait_ge(xsh_ready, c.n + 1)
                    nc.tensor.matmul(psC[:, 0:256], centre[:, :], xsh[c.par][:, :], start=True, stop=True).then_inc(centred, 1)
                if s == 4:
                    pe.wait_ge(csq_done, c.n + 1)
                    nc.tensor.matmul(psC[:, 256:512], mean[:, :], csq[:, 0:256], start=True, stop=True).then_inc(var_done, 1)
                if s == 6:
                    pe.wait_ge(xg_done, c.n + 1)
                    pe.wait_ge(w1_in, (layer_of(c.n) + 1) * 16)
                    for k in range(2):
                        mm = nc.tensor.matmul(psC[:, 256 * k:256 * k + 256], w1[:, FF + 128 * k:FF + 128 * k + 128], xg[:, :], start=True, stop=True)
                    mm.then_inc(gates_done, 1)
                if s == 7:
                    off, m = FF_CHUNKS[2]
                    pe.wait_ge(gate_stored, 2 * c.n + 1)
                    nc.tensor.matmul(psC[0:m, 0:256], w1[:, FF + off:FF + off + m], xg[:, :], start=True, stop=True)
                    nc.tensor.matmul(psC[0:m, 256:512], w1[:, off:off + m], xg[:, :], start=True, stop=True).then_inc(gates_done, 1)

            pe.wait_ge(x_written, BATCHES)
            pe.wait_ge(halves_ready, 7)
            over_units(pe, iteration, UNITS, FIRST, LAST)

            for k in range(6):
                if k < 4:
                    pe.wait_ge(y_ready, k + 1)
                    need(pe, y_normed, k - 1)
                    nc.tensor.matmul(psS[k % 2][:, :], centre[:, :], y[k % 2][:, :], start=True, stop=True).then_inc(y_centred, 1)
                if 1 <= k < 5:
                    pe.wait_ge(y_sq, k)
                    need(pe, y_rstd, k - 2)
                    nc.tensor.matmul(psA[(k - 1) % 2][:, :], mean[:, :], csq[:, :], start=True, stop=True).then_inc(y_var, 1)
                if k >= 2:
                    pe.wait_ge(y_normed, k - 1)
                    need(pe, y_out, k - 3)
                    for j in range(4):
                        mm = nc.tensor.transpose(psT[k % 2][:, 128 * j:128 * j + 128], yn[k % 2][:, 128 * j:128 * j + 128], ident[:, :])
                    mm.then_inc(y_turned, 1)

        @block.scalar
        def _(act):
            for n in range(12):
                act.wait_ge(turned, n + 1)
                dst = X[:, BATCHES * TOKENS + 512 * n:BATCHES * TOKENS + 512 * n + 512] if n < 4 else wT[:, (n - 4) // 2, 512 * (n % 2):512 * (n % 2) + 512]
                nc.scalar.copy(dst, psT[n % 2][:, :]).then_inc(turned_out, 1)

            act.wait_ge(turned, 13)
            nc.scalar.copy(cols[:, :], psT[0][:, 0:128]).then_inc(turned_out, 1)
            act.wait_ge(turned_out, 13)

            def first_attention(a, b, c):
                for s in range(8):
                    if a.live:
                        n = use_qk(s)
                        act.wait_ge(proj1, 12 * a.n + n + 1)
                        need(act, score1, 2 * (8 * (a.n - 2) + s) + 2)
                        nc.scalar.activation(qT[a.par][:, s, :], psA[n % 2][:, 0:256], ACT.Identity, bias=qb[:, s:s + 1])
                        nc.scalar.activation(kT[a.par][:, s, :], psA[n % 2][:, 256:512], ACT.Identity, bias=kb[:, s:s + 1]).then_inc(qk1_stored, 1)
                    ub, sb_ = lag(b, s, 1)
                    if ub.live and ub is not b or (ub.live and s):
                        act.wait_ge(pv1, 2 * (8 * ub.n + sb_) + 2)
                        need(act, wl_done, ub.n - 1)
                        nc.scalar.copy(cT[ub.par][:, sb_, :], psX[:, 0:256]).then_inc(ctx1, 1)
                    if b.live:
                        for j in range(2):
                            e = (s % 2) * 2 + j
                            act.wait_ge(nm1, 2 * (8 * b.n + s) + j + 1)
                            need(act, pv1, 2 * (8 * b.n + s - 2) + j + 1)
                            for t in range(2):
                                nc.scalar.activation(E[e][:, 256 * t:256 * t + 256], psS[j][:, 256 * t:256 * t + 256], ACT.Exp, bias=nm[j][:, t:t + 1],
                                                     scale=HEAD ** -0.5, accum_out=sums[e][:, t:t + 1]).then_inc(exp1, 1)
                    if c.live and s == 2:
                        act.wait_ge(centred1, c.n + 1)
                        need(act, var1, c.n)
                        nc.scalar.activation(csq[:, 0:256], psC[:, 0:256], ACT.Square).then_inc(csq1, 1)

            over_units(act, first_attention, BATCHES, 2, BATCHES - 2)

            def iteration(a, b, c):
                for s in range(8):
                    if b.live and s == 4:
                        need(act, corner_shifted, 4 * b.n)
                        for r in range(2):
                            act.wait_ge(corner_maxed, 2 * b.n + r + 1)
                            nc.scalar.copy(Sc[:, PAIRS * r:PAIRS * r + PAIRS, :].rearrange("p h k -> p (h k)"), psS[r][0:WINDOW, 0:256]).then_inc(corner_stored, 1)
                    if a.live:
                        n = use_qk(s)
                        act.wait_ge(proj_done, 12 * a.n + n + 1)
                        need(act, summed, 8 * a.n + s - 1)
                        nc.scalar.activation(sq[s % 2][:, :], psA[n % 2][:, :], ACT.Square).then_inc(squared, 1)
                    bp1, sb1 = lag(b, s, 1)
                    if bp1.live:
                        act.wait_ge(p_turned, 8 * bp1.n + sb1 + 1)
                        need(act, pv_done, 8 * bp1.n + sb1 - 1)
                        nc.scalar.copy(PT[sb1 % 2][:, :], psT[s % 2][:, :]).then_inc(p_stored, 1)
                    if b.live:
                        act.wait_ge(shifted, 8 * b.n + s + 1)
                        nc.scalar.activation(E[s % 2][:, :], E[s % 2][:, :], ACT.Exp, scale=QK_SCALE).then_inc(exped, 1)
                        if s >= 4:
                            act.wait_ge(corner_shifted, 4 * b.n + s - 3)
                            nc.scalar.activation(Ec[s % 2][:, :], Ec[s % 2][:, :], ACT.Exp, scale=QK_SCALE).then_inc(corner_exped, 1)
                    if a.live and s % 2:
                        w = s // 2
                        act.wait_ge(proj_done, 12 * a.n + use_v(w) + 1)
                        need(act, pv_done, 8 * (a.n - 1))
                        nc.scalar.copy(V[:, a.par, w // 2, 8 * (w % 2):8 * (w % 2) + 8, 0:HEAD], heads8(psA[use_v(w) % 2][:, :])).then_inc(v_stored, 1)
                    apa, sa = lag(a, s, 2)
                    if apa.live:
                        tile, half, which = sa // 4, (sa // 2) % 2, sa % 2
                        act.wait_ge(a_turned, 8 * apa.n + sa + 1)
                        need(act, scored, 10 * (apa.n - 1))
                        dst = (kT if which else qT)[apa.par]
                        nc.scalar.copy(dst[:, 4 * half:4 * half + 4, 128 * tile:128 * tile + 128],
                                       psT[(s + 1) % 2][:, :].rearrange("p (c t) -> p c t", c=4)).then_inc(a_stored, 1)
                    if c.live and s == 3:
                        act.wait_ge(centred, c.n + 1)
                        need(act, var_done, c.n)
                        nc.scalar.activation(csq[:, 0:256], psC[:, 0:256], ACT.Square).then_inc(csq_done, 1)
                    c1 = c.back()
                    if c1.live and s == 0:
                        m = FF_CHUNKS[2][1]
                        act.wait_ge(gate_stored, 2 * c1.n + 2)
                        nc.scalar.activation(gate[0:m, 2, :], gate[0:m, 2, :], ACT.Gelu).then_inc(gelu_done, 1)
                        nc.scalar.activation(gate[:, 0:2, :], gate[:, 0:2, :], ACT.Gelu).then_inc(gelu_done, 1)
                    bp2, sb2 = lag(b, s, 2)
                    if bp2.live:
                        tile, g = sb2 // 4, sb2 % 4
                        act.wait_ge(ctx_turned, 8 * bp2.n + sb2 + 1)
                        need(act, wo_done, bp2.n - 1)
                        nc.scalar.copy(cT[bp2.par][:, chunk_of(g, 0):chunk_of(g, 1) + 1:2, 128 * tile:128 * tile + 128],
                                       psT[s % 2][:, 0:256].rearrange("p (c t) -> p c t", c=2)).then_inc(ctx_stored, 1)

            act.wait_ge(x_written, BATCHES)
            nc.scalar.copy(x1[:, :], X[:, 0:BATCHES * TOKENS]).then_inc(x1_kept, 1)
            over_units(act, iteration, UNITS, FIRST, LAST)

            for k in range(6):
                if k < 4:
                    act.wait_ge(y_centred, k + 1)
                    need(act, y_var, k)
                    nc.scalar.activation(csq[:, :], psS[k % 2][:, :], ACT.Square).then_inc(y_sq, 1)
                if k >= 2:
                    act.wait_ge(y_turned, k - 1)
                    if k >= 4:
                        act.wait_ge(stored[k - 4], 16)
                    nc.scalar.copy(yo[k % 2][:, :], psT[k % 2][:, :]).then_inc(y_out, 1)

        @block.vector
        def _(dve):
            dve.wait_ge(ident_in, 16)
            dve.wait_ge(const_in, 16 * 5)
            nc.vector.tensor_copy(ident_h[:, :], ident[:, :]).then_inc(halves_ready, 1)
            nc.vector.tensor_copy(band_h[:, :, :], band[:, :].unsqueeze(1).to_broadcast([PARTS, PER_GROUP, PARTS])).then_inc(halves_ready, 1)
            nc.vector.tensor_copy(corner_h[:, :, :], corner[:, :].unsqueeze(1).to_broadcast([PARTS, PAIRS, WINDOW])).then_inc(halves_ready, 1)

            for t in (xs[0], xs[1], xsh[0], xsh[1]):
                nc.vector.memset(t[64:128, 0:1], 0.0).then_inc(halves_ready, 1)

            def first_input(u, par):
                need(dve, proj1, 12 * (u - 1))
                nc.vector.tensor_copy(xs1[par][:, :], X[:, slot(u + BATCHES)]).then_inc(xs1_ready, 1)

            def first_attention(a, b, c):
                for s in range(8):
                    if c.live and s == 2:
                        dve.wait_ge(wl_done, c.n + 1)
                        nc.vector.scalar_tensor_tensor(out=xr[c.par][:, :], in0=psC[:, 0:256], scalar=lb[:, :], in1=X[:, slot(c.n + BATCHES)],
                                                       op0=ALU.add, op1=ALU.add).then_inc(resid1, 1)
                    if c.live and s == 4:
                        dve.wait_ge(var1, c.n + 1)
                        nc.vector.tensor_scalar(var_eps[:, 0:256], psC[:, 256:512], EPS, None, ALU.add).then_inc(eps1, 1)
                    if c.live and s == 5:
                        dve.wait_ge(rstd1, c.n + 1)
                        nc.vector.tensor_tensor(X[:, slot(c.n)], psC[:, 0:256], rstd[:, 0:256], ALU.mult).then_inc(x_written, 1)
                    if b.live:
                        for j in range(2):
                            i = 2 * (8 * b.n + s) + j
                            dve.wait_ge(score1, i + 1)
                            nc.vector.tensor_reduce(mx[j][:, 0:2], psS[j][:, :].rearrange("p (t q) -> p t q", t=2), AX.X, ALU.max).then_inc(max1, 1)
                            dve.wait_ge(max1, i + 1)
                            need(dve, exp1, 4 * (8 * b.n + s - 1) + 2 * j + 2)
                            nc.vector.tensor_scalar(nm[j][:, :], mx[j][:, 0:2], -(HEAD ** -0.5), None, ALU.mult).then_inc(nm1, 1)
                    if a.live and s % 2:
                        w = s // 2
                        dve.wait_ge(proj1, 12 * a.n + use_v(w) + 1)
                        dve.wait_ge(bias_in, 16)
                        nc.vector.tensor_tensor(V[:, a.par, w // 2, 8 * (w % 2):8 * (w % 2) + 8, 0:HEAD], heads8(psA[use_v(w) % 2][:, :]),
                                                heads8(vb[:, 512 * (w % 2):512 * (w % 2) + 512]), ALU.add).then_inc(v1_stored, 1)
                    if b.live:
                        for j in range(2):
                            i = 2 * (8 * b.n + s) + j
                            e = (s % 2) * 2 + j
                            dve.wait_ge(exp1, 2 * i + 2)
                            nc.vector.reciprocal(rinv[e][:, 0:2], sums[e][:, :]).then_inc(rinv1, 1)
                            dve.wait_ge(rinv1, i + 1)
                            dve.wait_ge(v1_stored, 4 * b.n + 4)
                            need(dve, pv1, i - 3)
                            nc.vector.tensor_tensor(Vs[e][:, :, :], V[:, b.par, :, 2 * s + j, 0:HEAD], rinv[e][:, 0:2].unsqueeze(2).to_broadcast([PARTS, 2, HEAD]),
                                                    ALU.mult).then_inc(vs1, 1)
                    if s == 6 and (not a.static or 0 < a.n + 1 < BATCHES):
                        first_input(a.n + 1, 1 - a.par)

            dve.wait_ge(turned_out, 13)
            first_input(0, 0)
            over_units(dve, first_attention, BATCHES, 2, BATCHES - 2)

            def unit_input(u, par):
                need(dve, proj_done, 12 * (u - 1))
                dve.wait_ge(x_written, u + 1)
                nc.vector.tensor_copy(xs[par][0:64, :], X[0:64, slot(u)])
                nc.vector.tensor_copy(xs[par][64:128, 1:TOKENS], X[64:128, slot(u, 0, TOKENS - 1)]).then_inc(xs_ready, 1)

            def feed_forward(c, c1, s):
                if c1.live and s == 0:
                    off, m = FF_CHUNKS[2]
                    layer = layer_of(c1.n)
                    dve.wait_ge(gates_done, 2 * c1.n + 2)
                    need(dve, w2_done, c1.n)
                    nc.vector.tensor_scalar(gate[0:m, 2, :], psC[0:m, 0:256], cols[0:m, bass.ds(layer + B1 + 5 * LAYERS, 1)], None, ALU.add)
                    nc.vector.tensor_scalar(hid[0:m, 2, :], psC[0:m, 256:512], cols[0:m, bass.ds(layer + B1 + 2 * LAYERS, 1)], None, ALU.add).then_inc(gate_stored, 1)
                if c1.live and s == 1:
                    for k in range(2):
                        dve.wait_ge(a_done, c1.n + 1)
                        dve.wait_ge(gelu_done, 2 * c1.n + 2)
                        nc.vector.scalar_tensor_tensor(out=hid[:, k, :], in0=psC[:, 256 * k:256 * k + 256], scalar=cols[:, bass.ds(layer_of(c1.n) + B1 + k * LAYERS, 1)],
                                                       in1=gate[:, k, :], op0=ALU.add, op1=ALU.mult).then_inc(hid_done, 1)
                if c1.live and s == 2:
                    dve.wait_ge(w2_done, c1.n + 1)
                    nc.vector.scalar_tensor_tensor(out=X[:, slot(c1.n + BATCHES)], in0=psC[:, 0:256],
                                                   scalar=cols[:, bass.ds(layer_of(c1.n) + B2, 1)], in1=xr[c1.par][:, :], op0=ALU.add, op1=ALU.add).then_inc(x_written, 1)
                if not c.live:
                    return
                if s == 3:
                    dve.wait_ge(wo_done, c.n + 1)
                    nc.vector.tensor_tensor(xr[c.par][:, :], psC[:, 0:256], X[:, slot(c.n)], ALU.add).then_inc(resid, 1)
                    dve.wait_ge(resid, c.n + 1)
                    nc.vector.tensor_copy(xsh[c.par][0:64, :], xr[c.par][0:64, :])
                    nc.vector.tensor_copy(xsh[c.par][64:128, 1:TOKENS], xr[c.par][64:128, 0:TOKENS - 1]).then_inc(xsh_ready, 1)
                if s == 5:
                    dve.wait_ge(var_done, c.n + 1)
                    nc.vector.tensor_scalar(var_eps[:, 0:256], psC[:, 256:512], EPS, None, ALU.add).then_inc(eps_added, 1)
                if s == 7:
                    dve.wait_ge(gates_done, 2 * c.n + 1)
                    need(dve, hid_done, 2 * c.n)
                    for k in range(2):
                        ins = nc.vector.tensor_scalar(gate[:, k, :], psC[:, 256 * k:256 * k + 256], cols[:, bass.ds(layer_of(c.n) + B1 + (3 + k) * LAYERS, 1)], None, ALU.add)
                    ins.then_inc(gate_stored, 1)

            def normalise(c):
                dve.wait_ge(rstd_done, c.n + 1)
                nc.vector.tensor_tensor(xn[:, :], psC[:, 0:256], rstd[:, 0:256], ALU.mult).then_inc(xn_done, 1)
                dve.wait_ge(xn_done, c.n + 1)
                need(dve, a_done, c.n)
                nc.vector.tensor_scalar(xg[:, :], xn[:, :], cols[:, bass.ds(layer_of(c.n) + LNG, 1)], cols[:, bass.ds(layer_of(c.n) + LNB, 1)], ALU.mult, ALU.add).then_inc(xg_done, 1)

            def iteration(a, b, c):
                for s in range(8):
                    feed_forward(c, c.back(), s)
                    if b.live and s == 4:
                        for r in range(2):
                            dve.wait_ge(scored, 10 * b.n + CORNER_USE + r + 1)
                            nc.vector.tensor_reduce(mc[:, PAIRS * r:PAIRS * r + PAIRS], psS[r][0:WINDOW, 0:256].rearrange("p (h k) -> p h k", k=WINDOW),
                                                    AX.X, ALU.max).then_inc(corner_maxed, 1)
                    if b.live:
                        k = use_s(s) % 2
                        m, e, g = mx[s % 2], E[s % 2], s % 4
                        dve.wait_ge(scored, 10 * b.n + use_s(s) + 1)
                        nc.vector.tensor_reduce(m[:, :], heads4(psS[k][:, :]), AX.X, ALU.max).then_inc(maxed, 1)
                        if s >= 4:
                            dve.wait_ge(maxed, 12 * b.n + s + 1 + (s - 4))
                            dve.wait_ge(corner_maxed, 2 * b.n + 2)
                            nc.vector.tensor_tensor(m[0:WINDOW, :], m[0:WINDOW, :], mc[:, kept(g)], ALU.max).then_inc(maxed, 1)
                        dve.wait_ge(maxed, 12 * b.n + s + 1 + (s - 3 if s >= 4 else 0))
                        need(dve, p_turned, 8 * b.n + s - 1)
                        nc.vector.tensor_tensor(heads4(e[:, :]), heads4(psS[k][:, :]), m[:, :].unsqueeze(2).to_broadcast([PARTS, PER_GROUP, PARTS]),
                                                ALU.subtract).then_inc(shifted, 1)
                        if s >= 4:
                            dve.wait_ge(corner_stored, 2 * b.n + 2)
                            need(dve, corner_turned, 4 * b.n + s - 5)
                            nc.vector.tensor_tensor(Ec[s % 2][:, :].rearrange("p (h k) -> p h k", k=WINDOW), Sc[:, kept(g), :],
                                                    m[0:WINDOW, :].unsqueeze(2).to_broadcast([WINDOW, PER_GROUP, WINDOW]), ALU.subtract).then_inc(corner_shifted, 1)
                    if a.live:
                        i = 8 * a.n + s
                        dve.wait_ge(squared, i + 1)
                        need(dve, rn_ready, i - 1)
                        nc.vector.tensor_reduce(n2[s % 2][:, :], heads8(sq[s % 2][:, :]), AX.X, ALU.add).then_inc(summed, 1)
                        dve.wait_ge(summed, i + 1)
                        nc.vector.tensor_scalar(n2[s % 2][:, :], n2[s % 2][:, :], 1e-24, None, ALU.max).then_inc(guarded, 1)
                    if b.live and s >= 4:
                        dve.wait_ge(corner_exped, 4 * b.n + s - 3)
                        need(dve, pv_done, 8 * b.n + s - 1)
                        nc.vector.transpose(PcT[s % 2][:, :], Ec[s % 2][:, :]).then_inc(corner_turned, 1)
                    bp1, sb1 = lag(b, s, 1)
                    if bp1.live:
                        i = 8 * bp1.n + sb1
                        px = psX[:, 0:PER_GROUP * VW].rearrange("p (h e) -> p h e", e=VW)
                        dve.wait_ge(pv_done, i + 1)
                        nc.vector.reciprocal(rinv[sb1 % 2][:, :].unsqueeze(2), px[:, :, HEAD:VW]).then_inc(recip_done, 1)
                        dve.wait_ge(recip_done, i + 1)
                        need(dve, ctx_turned, i - 1)
                        nc.vector.tensor_tensor(cn[sb1 % 2][:, :].rearrange("p (h d) -> p h d", d=HEAD), px[:, :, 0:HEAD],
                                                rinv[sb1 % 2][:, :].unsqueeze(2).to_broadcast([PARTS, PER_GROUP, HEAD]), ALU.mult).then_inc(ctx_normed, 1)
                    if a.live:
                        tile, which = s // 4, s % 2
                        n = use_qk(s)
                        i = 8 * a.n + s
                        dve.wait_ge(rn_ready, i + 1)
                        need(dve, sin_done, i - 1)
                        nc.vector.tensor_tensor(heads8(qn[s % 2][:, :]), heads8(psA[n % 2][:, :]), rn[s % 2][:, :].unsqueeze(2).to_broadcast([PARTS, 8, HEAD]),
                                                ALU.mult).then_inc(normed, 1)
                        dve.wait_ge(normed, i + 1)
                        need(dve, rotated, i - 1)
                        nc.vector.tensor_tensor(heads8(qc[s % 2][:, :]), heads8(qn[s % 2][:, :]),
                                                tables[:, table(layer_of(a.n), tile, 2 * which)].unsqueeze(1).to_broadcast([PARTS, 8, HEAD]), ALU.mult).then_inc(cos_done, 1)
                    if c.live and s == 5:
                        normalise(c)
                    if s == 6 and (not a.static or 0 < a.n + 1 < UNITS):
                        unit_input(a.n + 1, 1 - a.par)

            def kept(g):
                at = PAIRS * (g % 2) + PER_GROUP * (g // 2)
                return slice(at, at + PER_GROUP)

            def heads4(ap):
                return ap.rearrange("p (h k) -> p h k", k=PARTS)

            dve.wait_ge(x_written, BATCHES)
            dve.wait_ge(x1_kept, 1)
            dve.wait_ge(cleared, 3)
            dve.wait_ge(tables_ready, LAYERS * TILES)
            unit_input(0, 0)
            over_units(dve, iteration, UNITS, FIRST, LAST)

            for k in range(6):
                if k < 4:
                    dve.wait_ge(x_written, UNITS + BATCHES)
                    need(dve, y_centred, k - 1)
                    nc.vector.tensor_tensor(y[k % 2][:, :], X[:, 512 * k:512 * k + 512], x1[:, 512 * k:512 * k + 512],
                                            ALU.add).then_inc(y_ready, 1)
                if 1 <= k < 5:
                    dve.wait_ge(y_var, k)
                    nc.vector.tensor_scalar(var_eps[:, :], psA[(k - 1) % 2][:, :], EPS, None, ALU.add).then_inc(y_eps, 1)
                    dve.wait_ge(y_rstd, k)
                    need(dve, y_turned, k - 2)
                    nc.vector.tensor_tensor(yn[(k - 1) % 2][:, :], psS[(k - 1) % 2][:, :], rstd[:, :], ALU.mult).then_inc(y_normed, 1)


FIRST, LAST = 2, UNITS - 2

_INS = ["L0_attn_x", "L0_attn_q_w", "L0_attn_q_b", "L0_attn_k_w", "L0_attn_k_b", "L0_attn_v_w", "L0_attn_v_b", "L0_attn_l_w", "L0_attn_l_b",
        "L0_ffn_Wqkv", "L0_ffn_q_scale", "L0_ffn_k_scale", "L0_ffn_Wo", "L0_ffn_ln_g", "L0_ffn_ln_b", "L0_ffn_W1", "L0_ffn_b1", "L0_ffn_W2", "L0_ffn_b2"]


def kernel(**inputs):
    import concourse.bacc as _bacc
    from concourse.bass_utils import run_bass_kernel_spmd as _run

    nc = _bacc.Bacc("TRN2", target_bir_lowering=False, num_devices=1)
    arrays, args = {}, []
    given = [(f"in_{n}_dram", np.ascontiguousarray(inputs[n])) for n in _INS]
    for name, a in given + [(f"const_{n}_dram", a) for n, a in constants().items()]:
        if name == "const_rotary_dram":
            a = a.reshape(PARTS, -1)
        arrays[name] = a
        args.append(nc.dram_tensor(name, a.shape, mybir.dt.from_np(a.dtype), kind="ExternalInput").ap())
    args.append(nc.dram_tensor("out_0_dram", (BATCHES, TOKENS, DIM), F32, kind="ExternalOutput").ap())
    postln_kernel(nc, *args)
    r = _run(nc, [arrays], core_ids=[0])
    return r.results[0]["out_0_dram"]
```

```python
from contextlib import ExitStack

import numpy as np

import concourse.bass as bass
from concourse import mybir

F32 = mybir.dt.float32
BF16 = mybir.dt.bfloat16
I32 = mybir.dt.int32
ALU = mybir.AluOpType
ACT = mybir.ActivationFunctionType
AX = mybir.AxisListType

PARTS = 128
BATCHES, TOKENS, DIM = 8, 256, 128
HEADS, HEAD = 16, 64
INNER = HEADS * HEAD
PAIRS = HEADS // 2
LAYERS = 6
WINDOW = 32
TILES = TOKENS // PARTS
GROUPS = 4
PER_GROUP = HEADS // GROUPS
FF = int(DIM * 4 * 2 / 3)
FF_CHUNKS = [(0, 128), (128, 128), (256, FF - 256)]
UNITS = LAYERS * BATCHES
RING = 2 * BATCHES
EPS = 1e-5
RSQRT_BITS = 0x5F3759DF
QK_SCALE = 8.0
MASKED = -1e30
VW = HEAD + 1


def constants():
    ident = np.eye(PARTS, dtype=np.float32)
    mean = np.full((PARTS, PARTS), 1.0 / DIM, np.float32)
    q, k = np.arange(PARTS)[:, None], np.arange(PARTS)[None, :]
    band = np.where((q < k) | (q > k + WINDOW), np.float32(MASKED), np.float32(0))
    corner = np.zeros((PARTS, WINDOW), np.float32)
    corner[:WINDOW] = np.where(np.arange(WINDOW)[:, None] > np.arange(WINDOW)[None, :], MASKED, 0)
    half = np.arange(0, HEAD, 2, dtype=np.float32)
    inv_freq = (1.0 / 10000.0 ** (half / HEAD)).astype(np.float32)
    t = np.arange(TOKENS, dtype=np.float32)
    freqs = t[:, None] * inv_freq[None, :]
    freqs = np.concatenate([freqs, freqs], -1).astype(np.float64)
    base = ((half + 0.4 * HEAD) / (1.4 * HEAD)).astype(np.float32)
    scale = base[None, :].astype(np.float64) ** ((t - TOKENS // 2) / (WINDOW // 2))[:, None]
    scale = np.concatenate([scale, scale], -1)
    sign = np.where(np.arange(HEAD) < HEAD // 2, -1.0, 1.0)
    cos, sin = np.cos(freqs), np.sin(freqs) * sign
    tables = np.stack([cos * scale, sin * scale, cos / scale, sin / scale], 1).astype(np.float32)
    tables = tables.reshape(TILES, PARTS, 4, HEAD).transpose(1, 0, 2, 3)
    return {
        "ident": ident, "mean": mean, "centre": ident - mean, "band": band, "corner": corner,
        "rotary": np.ascontiguousarray(tables),
    }


class Unit:

    def __init__(self, n, par, count):
        self.n, self.par, self.count = n, par, count
        self.static = isinstance(n, int)
        self.live = not self.static or 0 <= n < count

    def back(self):
        return Unit(self.n - 1, 1 - self.par, self.count)


def lag(unit, s, k):
    return (unit, s - k) if s >= k else (unit.back(), s - k + 8)


def need(eng, sem, value):
    if not isinstance(value, int) or value > 0:
        eng.wait_ge(sem, value)


def over_units(eng, iteration, count, first, last):
    def at(i, par):
        iteration(Unit(i + 1, 1 - par, count), Unit(i, par, count), Unit(i - 1, 1 - par, count))

    for i in range(-1, first):
        at(i, i % 2)
    with eng.Fori(first, last, 2) as r:
        at(r, first % 2)
        at(r + 1, 1 - first % 2)
    for i in range(last, count + 2):
        at(i, i % 2)


def postln_kernel(nc, x, q_w, q_b, k_w, k_b, v_w, v_b, l_w, l_b, Wqkv, q_scale, k_scale, Wo,
                  ln_g, ln_b, W1, b1, W2, b2, ident_d, mean_d, centre_d, band_d, corner_d, rotary_d,
                  out):
    ctx = ExitStack()
    with ctx:
        def sb(name, shape, dt=F32):
            return ctx.enter_context(nc.sbuf_tensor(name, shape, dt))

        def sem(name):
            return ctx.enter_context(nc.semaphore(name))

        psA = [ctx.enter_context(nc.psum_tensor(f"psA{i}", [PARTS, 512], F32)) for i in range(2)]
        psS = [ctx.enter_context(nc.psum_tensor(f"psS{i}", [PARTS, 512], F32)) for i in range(2)]
        psT = [ctx.enter_context(nc.psum_tensor(f"psT{i}", [PARTS, 512], F32)) for i in range(2)]
        psX = ctx.enter_context(nc.psum_tensor("psX", [PARTS, 512], F32))
        psC = ctx.enter_context(nc.psum_tensor("psC", [PARTS, 512], F32))

        ident = sb("ident", [PARTS, PARTS])
        mean = sb("mean", [PARTS, PARTS])
        centre = sb("centre", [PARTS, PARTS])
        band = sb("band", [PARTS, PARTS])
        corner = sb("corner", [PARTS, WINDOW])
        rotary = sb("rotary", [PARTS, TILES * 4 * HEAD])
        ident_h = sb("ident_h", [PARTS, PARTS], BF16)
        band_h = sb("band_h", [PARTS, PER_GROUP, PARTS], BF16)
        corner_h = sb("corner_h", [PARTS, PAIRS, WINDOW], BF16)
        tables = sb("tables", [PARTS, LAYERS * TILES * 4 * HEAD])
        rows = sb("rows", [PARTS, PARTS])
        cols = sb("cols", [PARTS, PARTS])
        QB, KB, LB = 0, PAIRS, 2 * PAIRS
        LNG = LB + 1
        LNB, B2, B1 = LNG + LAYERS, LNG + 2 * LAYERS, LNG + 3 * LAYERS
        qb, kb, lb = cols[:, QB:QB + PAIRS], cols[:, KB:KB + PAIRS], cols[:, LB:LB + 1]
        wqkv = sb("wqkv", [PARTS, 2 * 3 * INNER])
        wo = sb("wo", [PARTS, PAIRS, DIM])
        w1 = sb("w1", [PARTS, 2 * FF])
        w2 = sb("w2", [PARTS, 3, DIM])
        X = sb("X", [PARTS, RING * TOKENS])
        x1 = sb("x1", [PARTS, BATCHES * TOKENS])
        arena = sb("arena", [PARTS, 8192])
        taken = [0]

        def part(columns, view=None, **sizes):
            ap = arena[:, taken[0]:taken[0] + columns]
            taken[0] += columns
            return ap.rearrange(view, **sizes) if view else ap

        wT = part(4 * INNER, "p (m n) -> p m n", m=4)
        xraw = part(BATCHES * TOKENS, "p (t d) -> p t d", d=DIM)
        raw_l = part(INNER, "p (c n) -> p c n", n=PARTS)
        vb = part(INNER)
        raw = [wqkv[:, (3 + i) * INNER:(4 + i) * INNER].rearrange("p (c n) -> p c n", n=PARTS) for i in range(3)] + [raw_l]
        taken[0] = 0
        sq, qc = ([part(512) for _ in range(2)] for _ in range(2))
        qs = [part(512) for _ in range(4)]
        PT = [part(512) for _ in range(2)]
        gate, hid = (part(3 * TOKENS, "p (c t) -> p c t", c=3) for _ in range(2))
        Sc = part(HEADS * WINDOW, "p (h k) -> p h k", k=WINDOW)[0:WINDOW]
        cn = [part(PER_GROUP * HEAD) for _ in range(2)]
        xn, xg = part(TOKENS), part(TOKENS)
        xs1 = [sb(f"xs1_{i}", [PARTS, TOKENS]) for i in range(2)]
        xs = [sb(f"xs{i}", [PARTS, TOKENS]) for i in range(2)]
        qT = [sb(f"qT{i}", [PARTS, PAIRS, TOKENS]) for i in range(2)]
        kT = [sb(f"kT{i}", [PARTS, PAIRS, TOKENS]) for i in range(2)]
        V = sb("V", [PARTS, 2, TILES, HEADS, VW])
        Vc_all = sb("Vc", [PARTS, 2 * HEADS * VW])
        Vc = Vc_all[0:WINDOW, :].rearrange("p (a h e) -> p a h e", a=2, e=VW)
        scales = Vc_all[:, 0:LAYERS * 4 * HEAD].rearrange("p (l j d) -> p l j d", l=LAYERS, j=4)
        cT = [sb(f"cT{i}", [PARTS, PAIRS, TOKENS]) for i in range(2)]
        n2 = [sb(f"n2{i}", [PARTS, 16]) for i in range(2)]
        rn = [sb(f"rn{i}", [PARTS, 16]) for i in range(2)]
        E = [sb(f"E{i}", [PARTS, 512]) for i in range(4)]
        mx = [sb(f"mx{i}", [PARTS, PER_GROUP]) for i in range(2)]
        nm = [sb(f"nm{i}", [PARTS, 2]) for i in range(2)]
        sums = [sb(f"sums{i}", [PARTS, 2]) for i in range(4)]
        rinv = [sb(f"rinv{i}", [PARTS, 4]) for i in range(4)]
        Vs = [sb(f"Vs{i}", [PARTS, 2, HEAD]) for i in range(4)]
        mc = sb("mc", [WINDOW, HEADS])
        Ec = [sb(f"Ec{i}", [WINDOW, 128]) for i in range(2)]
        PcT = [sb(f"PcT{i}", [WINDOW, 128]) for i in range(2)]
        xr = [sb(f"xr{i}", [PARTS, TOKENS]) for i in range(2)]
        xsh = [sb(f"xsh{i}", [PARTS, TOKENS]) for i in range(2)]
        csq = sb("csq", [PARTS, 512])
        rstd = sb("rstd", [PARTS, 512])
        var = sb("var", [PARTS, 4])
        rdev = sb("rdev", [PARTS, 4])
        guess = [sb(f"guess{i}", [PARTS, 16]) for i in range(2)]
        y = [qT[0][:, 2 * i:2 * i + 2, :].rearrange("p c t -> p (c t)") for i in range(2)]
        yn = [qT[1][:, 2 * i:2 * i + 2, :].rearrange("p c t -> p (c t)") for i in range(2)]
        yo = [kT[0][:, 2 * i:2 * i + 2, :].rearrange("p c t -> p (c t)") for i in range(2)]

        x_in = sem("x_in")
        raw_in = [sem(f"raw_in{i}") for i in range(4)]
        ident_in = sem("ident_in")
        const_in = sem("const_in")
        bias_in = sem("bias_in")
        param_in = sem("param_in")
        scale_in = sem("scale_in")
        wqkv_in = sem("wqkv_in")
        wo_in = sem("wo_in")
        w1_in = sem("w1_in")
        w2_in = sem("w2_in")
        vc_in = sem("vc_in")
        stored = [sem(f"stored{i}") for i in range(4)]
        sp_passed = sem("sp_passed")
        pool_passed = sem("pool_passed")
        halves_ready = sem("halves_ready")
        cleared = sem("cleared")
        tables_ready = sem("tables_ready")
        turned = sem("turned")
        turned_out = sem("turned_out")
        xs1_ready = sem("xs1_ready")
        proj1 = sem("proj1")
        qk1_stored = sem("qk1_stored")
        v1_stored = sem("v1_stored")
        score1 = sem("score1")
        max1 = sem("max1")
        nm1 = sem("nm1")
        exp1 = sem("exp1")
        rinv1 = sem("rinv1")
        vs1 = sem("vs1")
        pv1 = sem("pv1")
        ctx1 = sem("ctx1")
        wl_done = sem("wl_done")
        resid1 = sem("resid1")
        centred1 = sem("centred1")
        csq1 = sem("csq1")
        var1 = sem("var1")
        eps1 = sem("eps1")
        rdev1 = sem("rdev1")
        spread1 = sem("spread1")
        rstd1 = sem("rstd1")
        x_written = sem("x_written")
        x1_kept = sem("x1_kept")
        xs_ready = sem("xs_ready")
        proj_done = sem("proj_done")
        squared = sem("squared")
        summed = sem("summed")
        guarded = sem("guarded")
        cos_done = sem("cos_done")
        sin_done = sem("sin_done")
        added = sem("added")
        rotated = sem("rotated")
        v_stored = sem("v_stored")
        a_turned = sem("a_turned")
        a_stored = sem("a_stored")
        scored = sem("scored")
        maxed = sem("maxed")
        shifted = sem("shifted")
        exped = sem("exped")
        p_turned = sem("p_turned")
        p_stored = sem("p_stored")
        corner_maxed = sem("corner_maxed")
        corner_stored = sem("corner_stored")
        corner_shifted = sem("corner_shifted")
        corner_exped = sem("corner_exped")
        corner_turned = sem("corner_turned")
        pv_done = sem("pv_done")
        recip_done = sem("recip_done")
        ctx_normed = sem("ctx_normed")
        ctx_turned = sem("ctx_turned")
        ctx_stored = sem("ctx_stored")
        wo_done = sem("wo_done")
        resid = sem("resid")
        xsh_ready = sem("xsh_ready")
        centred = sem("centred")
        csq_done = sem("csq_done")
        var_done = sem("var_done")
        eps_added = sem("eps_added")
        rdev_done = sem("rdev_done")
        spread = sem("spread")
        rstd_done = sem("rstd_done")
        xn_done = sem("xn_done")
        xg_done = sem("xg_done")
        gates_done = sem("gates_done")
        gate_stored = sem("gate_stored")
        gelu_done = sem("gelu_done")
        a_done = sem("a_done")
        hid_done = sem("hid_done")
        hid2_done = sem("hid2_done")
        w2_done = sem("w2_done")
        y_ready = sem("y_ready")
        y_centred = sem("y_centred")
        y_sq = sem("y_sq")
        y_var = sem("y_var")
        y_eps = sem("y_eps")
        y_rdev = sem("y_rdev")
        y_spread = sem("y_spread")
        y_rstd = sem("y_rstd")
        y_normed = sem("y_normed")
        y_turned = sem("y_turned")
        y_out = sem("y_out")

        def use_s(s):
            return s + 2 * (s > 3)

        CORNER_USE = 4

        def chunk_of(g, k):
            return 4 * (g // 2) + g % 2 + 2 * k

        def head_of(g, j):
            return 2 * PER_GROUP * (g // 2) + 2 * j + g % 2

        def table(layer, tile, which):
            return bass.ds(((layer * TILES + tile) * 4 + which) * HEAD, HEAD)

        def layer_of(n):
            if isinstance(n, int):
                return n // BATCHES
            return nc.s_assert_within(n >> 3, 0, LAYERS - 1, skip_runtime_bounds_check_because="a unit's number is under UNITS")

        def slot(u, first=0, count=TOKENS):
            return bass.ds((u & (RING - 1)) * TOKENS + first, count)

        def heads8(ap):
            return ap.rearrange("p (h d) -> p h d", d=HEAD)

        block = ctx.enter_context(nc.Block())

        @block.sync
        def _(sp):
            sp.dma_start(ident[:, :], ident_d).then_inc(ident_in, 16)
            sp.dma_start(raw[0], q_w.rearrange("(c a) p d -> (a p) c d", a=2)).then_inc(raw_in[0], 16)
            sp.dma_start(xraw[:, :, :], x.rearrange("b (t p) d -> p (b t) d", p=PARTS)).then_inc(x_in, 16)
            sp.dma_start(raw[1], k_w.rearrange("(c a) p d -> (a p) c d", a=2)).then_inc(raw_in[1], 16)
            sp.dma_start(raw[2], v_w.rearrange("(c a) p d -> (a p) c d", a=2)).then_inc(raw_in[2], 16)
            sp.dma_start(raw[3], l_w.rearrange("o (c p) -> o c p", p=PARTS)).then_inc(raw_in[3], 16)
            sp.wait_ge(cleared, 1)
            for at, src in ((QB, q_b.rearrange("(c a) o p -> c (a o p)", a=2)), (KB, k_b.rearrange("(c a) o p -> c (a o p)", a=2)),
                            (LB, l_b), (LNG, ln_g), (LNB, ln_b), (B2, b2)):
                sp.dma_start(rows[at:at + src.shape[0], :], src).then_inc(param_in, 16)
            for c, (off, m) in enumerate(FF_CHUNKS):
                for k in range(2):
                    at = B1 + (3 * k + c) * LAYERS
                    sp.dma_start(rows[at:at + LAYERS, 0:m], b1[:, k * FF + off:k * FF + off + m]).then_inc(param_in, 16)
            sp.dma_start(vb[:, :], v_b.rearrange("h o p -> (o h p)").partition_broadcast(PARTS)).then_inc(bias_in, 16)
            for dst, src in ((mean, mean_d), (centre, centre_d), (band, band_d), (corner, corner_d), (rotary, rotary_d)):
                sp.dma_start(dst[:, :], src).then_inc(const_in, 16)
            for j, src in enumerate((q_scale, q_scale, k_scale, k_scale)):
                if j % 2 == 0:
                    sp.dma_start(scales[:, :, j, :], src.partition_broadcast(PARTS)).then_inc(scale_in, 16)
                    continue
                h = HEAD // 2
                sp.dma_start(scales[:, :, j, 0:h], src[:, h:HEAD].partition_broadcast(PARTS)).then_inc(scale_in, 16)
                sp.dma_start(scales[:, :, j, h:HEAD], src[:, 0:h].partition_broadcast(PARTS)).then_inc(scale_in, 16)

            def load_wqkv(layer):
                sp.dma_start(wqkv[:, bass.ds((layer & 1) * (3 * INNER), 3 * INNER)], Wqkv[bass.ds(layer, 1)].rearrange("o d n -> d (o n)")).then_inc(wqkv_in, 16)

            def load_wo(layer):
                heads = Wo[bass.ds(layer, 1)].rearrange("o (g a r p) d -> a p (o g) r d", g=GROUPS, a=2, r=2)
                for k in range(2):
                    for r in range(2):
                        sp.dma_start(wo[64 * k:64 * k + 64, r:PAIRS:2, :], heads[k][:, :, r, :]).then_inc(wo_in, 16)

            def load_w1(layer):
                sp.dma_start(w1[:, :], W1[bass.ds(layer, 1)].rearrange("o d n -> d (o n)")).then_inc(w1_in, 16)

            def load_w2(layer):
                sp.dma_start(w2[:, 0:2, :], W2[bass.ds(layer, 1), 0:256, :].rearrange("o (c p) d -> p (o c) d", p=PARTS)).then_inc(w2_in, 16)
                sp.dma_start(w2[0:FF - 256, 2, :], W2[bass.ds(layer, 1), 256:FF, :].rearrange("o p d -> p (o d)")).then_inc(w2_in, 16)

            load_wqkv(0)
            load_wo(0)
            load_w1(0)
            load_w2(0)

            def corner_values(u):
                sp.wait_ge(v_stored, 4 * u + 2)
                sp.sem_inc(sp_passed, 1)
                need(sp, pv_done, 8 * u - 3)
                sp.sem_inc(sp_passed, 1)
                sp.dma_start(Vc[:, bass.ds(u & 1, 1)], V[PARTS - WINDOW:PARTS, bass.ds(u & 1, 1), 0]).then_inc(vc_in, 16)

            corner_values(0)
            sp.wait_ge(proj_done, 12)
            load_wqkv(1)
            corner_values(1)
            with sp.Fori(2, 9) as u:
                corner_values(u)

            def next_layer(layer, units, two_ahead):
                sp.wait_ge(wo_done, layer * BATCHES)
                sp.sem_inc(sp_passed, 1)
                load_wo(layer)
                if two_ahead:
                    sp.wait_ge(proj_done, layer * (BATCHES * 12) + 12)
                    sp.sem_inc(sp_passed, 1)
                    load_wqkv(layer + 1)
                corner_values(layer * BATCHES + 1)
                sp.wait_ge(a_done, layer * BATCHES)
                sp.sem_inc(sp_passed, 1)
                load_w1(layer)
                sp.wait_ge(w2_done, layer * BATCHES)
                sp.sem_inc(sp_passed, 1)
                load_w2(layer)
                with sp.Fori(2, 2 + units) as k:
                    corner_values(layer * BATCHES + k)

            with sp.Fori(1, LAYERS - 1) as layer:
                next_layer(layer, 7, True)
            next_layer(LAYERS - 1, 6, False)

            for k in range(4):
                sp.wait_ge(y_out, k + 1)
                sp.dma_start(out.rearrange("b (t p) d -> p (b t) d", p=PARTS)[:, 4 * k:4 * k + 4, :],
                             yo[k % 2][:, :].rearrange("p (t d) -> p t d", d=DIM)).then_inc(stored[k], 16)
            for k in range(4):
                sp.wait_ge(stored[k], 16)

        @block.gpsimd
        def _(pool):
            nc.gpsimd.memset(rows[:, :], 0.0).then_inc(cleared, 1)
            nc.gpsimd.memset(V[:, :, :, :, :].rearrange("p a t h e -> p (a t h) e")[:, :, HEAD:VW], 1.0).then_inc(cleared, 1)
            pool.wait_ge(const_in, 16 * 5)
            pool.wait_ge(scale_in, 16 * 6)
            rot = rotary[:, :].rearrange("p (t n) -> p t n", t=TILES)
            tab = tables[:, :].rearrange("p (l t n) -> p l t n", l=LAYERS, t=TILES)
            for layer in range(LAYERS):
                for tile in range(TILES):
                    nc.gpsimd.tensor_tensor(tab[:, layer, tile, :], rot[:, tile, :],
                                            scales[:, layer].rearrange("p a d -> p (a d)"), ALU.mult).then_inc(tables_ready, 1)

            def rsqrt(dst, src, t):
                pool.sem_inc(pool_passed, 1)
                nc.gpsimd.tensor_scalar(dst.bitcast(I32), src.bitcast(I32), -0.5, float(RSQRT_BITS), ALU.mult, ALU.add)
                for _ in range(3):
                    pool.drain()
                    nc.gpsimd.tensor_tensor(t, dst, dst, ALU.mult)
                    pool.drain()
                    nc.gpsimd.tensor_tensor(t, t, src, ALU.mult)
                    pool.drain()
                    nc.gpsimd.tensor_scalar(t, t, -0.5, 1.5, ALU.mult, ALU.add)
                    pool.drain()
                    last = nc.gpsimd.tensor_tensor(dst, dst, t, ALU.mult)
                return last

            def first_attention(a, b, c):
                if c.live:
                    pool.wait_ge(eps1, c.n + 1)
                    rsqrt(rdev[:, 0:2], var[:, 0:2], guess[0][:, 0:2]).then_inc(rdev1, 1)

            over_units(pool, first_attention, BATCHES, 2, BATCHES - 2)

            def iteration(a, b, c):
                for s in range(8):
                    if a.live:
                        pool.wait_ge(sin_done, 8 * a.n + s + 1)
                        nc.gpsimd.tensor_tensor(qs[s % 4][:, :], qs[s % 4][:, :], qc[s % 2][:, :], ALU.add).then_inc(added, 1)
                    if c.live and s == 5:
                        pool.wait_ge(eps_added, c.n + 1)
                        need(pool, spread, c.n)
                        rsqrt(rdev[:, 0:2], var[:, 0:2], guess[0][:, 0:2]).then_inc(rdev_done, 1)
                    if a.live and s % 2:
                        k = (s // 2) % 2
                        pool.wait_ge(guarded, 4 * a.n + s // 2 + 1)
                        rsqrt(rn[k][:, :], n2[k][:, :], guess[1][:, :])
                        pool.drain()
                        for j in range(2):
                            t = qs[(s - 1 + j) % 4]
                            nc.gpsimd.tensor_tensor(heads8(t[:, :]), heads8(t[:, :]), rn[k][:, 8 * j:8 * j + 8].unsqueeze(2).to_broadcast([PARTS, 8, HEAD]),
                                                    ALU.mult).then_inc(rotated, 1)

            pool.wait_ge(tables_ready, LAYERS * TILES)
            over_units(pool, iteration, UNITS, FIRST, LAST)

            for k in range(4):
                pool.wait_ge(y_eps, k + 1)
                rsqrt(rdev[:, :], var[:, :], guess[0][:, 0:4]).then_inc(y_rdev, 1)

        @block.tensor
        def _(pe):
            pe.wait_ge(ident_in, 16)
            for n in range(12):
                if n < 4:
                    pe.wait_ge(x_in, 16)
                elif n % 2 == 0:
                    pe.wait_ge(raw_in[(n - 4) // 2], 16)
                need(pe, turned_out, n - 1)
                for j in range(4):
                    src = xraw[:, 4 * n + j, :] if n < 4 else raw[(n - 4) // 2][:, 4 * (n % 2) + j, :]
                    mm = nc.tensor.transpose(psT[n % 2][:, 128 * j:128 * j + 128], src, ident[:, :])
                mm.then_inc(turned, 1)
            pe.wait_ge(param_in, 16 * 12)
            pe.wait_ge(turned_out, 11)
            nc.tensor.transpose(psT[0][:, 0:128], rows[:, :], ident[:, :]).then_inc(turned, 1)
            pe.wait_ge(turned_out, 13)

            def variances(bank, at, tiles):
                for t in range(tiles):
                    mm = nc.tensor.matmul(bank[:, at + t:at + t + 1], csq[:, 128 * t:128 * t + 128], mean[:, 0:1], start=True, stop=True)
                return mm

            def spread_out(bank, at, tiles):
                for t in range(tiles):
                    mm = nc.tensor.matmul(bank[:, at + 128 * t:at + 128 * t + 128], rdev[:, t:t + 1].to_broadcast([PARTS, PARTS]), ident[:, :], start=True, stop=True)
                return mm

            def first_attention(a, b, c):
                for s in range(8):
                    if b.live:
                        for j in range(2):
                            need(pe, exp1, 4 * (8 * b.n + s - 1) + 2 * j + 2)
                            if j == 0:
                                pe.wait_ge(qk1_stored, 8 * b.n + s + 1)
                            for t in range(2):
                                mm = nc.tensor.matmul(psS[j][:, 256 * t:256 * t + 256], kT[b.par][64 * j:64 * j + 64, s, 128 * t:128 * t + 128],
                                                      qT[b.par][64 * j:64 * j + 64, s, :], start=True, stop=True)
                            mm.then_inc(score1, 1)
                    if a.live:
                        if s == 0:
                            pe.wait_ge(xs1_ready, a.n + 1)
                        need(pe, qk1_stored, 8 * a.n + s)
                        nc.tensor.matmul(psA[0][:, 0:256], wT[:, 0, 128 * s:128 * s + 128], xs1[a.par][:, :], start=True, stop=True)
                        nc.tensor.matmul(psA[0][:, 256:512], wT[:, 1, 128 * s:128 * s + 128], xs1[a.par][:, :], start=True, stop=True).then_inc(proj1, 1)
                    ub, sb_ = lag(b, s, 1)
                    if ub.live:
                        need(pe, ctx1, 8 * ub.n + sb_)
                        for j in range(2):
                            pe.wait_ge(vs1, 2 * (8 * ub.n + sb_) + j + 1)
                            e = (sb_ % 2) * 2 + j
                            for t in range(2):
                                mm = nc.tensor.matmul(psX[64 * j:64 * j + 64, 0:256], Vs[e][:, t, :], E[e][:, 256 * t:256 * t + 256], start=t == 0, stop=t == 1)
                            mm.then_inc(pv1, 1)
                    if a.live and s % 2:
                        w = s // 2
                        need(pe, v1_stored, 4 * a.n + w)
                        nc.tensor.matmul(psA[1][:, :], xs1[a.par][:, 128 * (w // 2):128 * (w // 2) + 128], wT[:, 2, 512 * (w % 2):512 * (w % 2) + 512],
                                         start=True, stop=True).then_inc(proj1, 1)
                    if c.live and s == 1:
                        pe.wait_ge(ctx1, 8 * c.n + 8)
                        need(pe, x_written, c.n)
                        for h in range(PAIRS):
                            mm = nc.tensor.matmul(psC[:, 0:256], wT[:, 3, 128 * h:128 * h + 128], cT[c.par][:, h, :], start=h == 0, stop=h == PAIRS - 1)
                        mm.then_inc(wl_done, 1)
                    if c.live and s == 2:
                        pe.wait_ge(resid1, c.n + 1)
                        nc.tensor.matmul(psC[:, 0:256], centre[:, :], xr[c.par][:, :], start=True, stop=True).then_inc(centred1, 1)
                    if c.live and s == 3:
                        pe.wait_ge(csq1, c.n + 1)
                        variances(psC, 256, 2).then_inc(var1, 1)
                    if c.live and s == 5:
                        pe.wait_ge(rdev1, c.n + 1)
                        spread_out(psC, 256, 2).then_inc(spread1, 1)

            pe.wait_ge(const_in, 16 * 5)
            over_units(pe, first_attention, BATCHES, 2, BATCHES - 2)

            def free_scores(b, k):
                u, k = (b.n, k - 2) if k >= 2 else (b.n - 1, k + 8)
                if CORNER_USE <= k < CORNER_USE + 2:
                    need(pe, corner_stored, 2 * u + k - CORNER_USE + 1)
                else:
                    need(pe, shifted, 8 * u + (k if k < CORNER_USE else k - 2) + 1)

            def free_turn(kinds):
                for s_, unit, slot in kinds:
                    if unit.live:
                        need(pe, s_, 8 * unit.n + slot + 1)

            def iteration(a, b, c):
                for s in range(8):
                    ap1, sa1 = lag(a, s, 4)
                    apa, sa = lag(a, s, 3)
                    bp1, sb1 = lag(b, s, 1)
                    bp2, sb2 = lag(b, s, 2)
                    bp3, sb3 = lag(b, s, 3)
                    bp4, sb4 = lag(b, s, 4)
                    if b.live and s == 4:
                        pe.wait_ge(a_stored, 8 * b.n + 8)
                        for r in range(2):
                            free_scores(b, CORNER_USE + r)
                            nc.tensor.matmul(psS[r][0:WINDOW, 0:256], ident_h[:, 0:WINDOW], corner_h[:, :, :].rearrange("p h k -> p (h k)"),
                                             start=True, stop=False, skip_group_check=True)
                            for h in range(PAIRS):
                                mm = nc.tensor.matmul(psS[r][0:WINDOW, WINDOW * h:WINDOW * h + WINDOW], qT[b.par][64 * r:64 * r + 64, h, PARTS:PARTS + WINDOW],
                                                      kT[b.par][64 * r:64 * r + 64, h, PARTS - WINDOW:PARTS], start=False, stop=h == PAIRS - 1, skip_group_check=True)
                            mm.then_inc(scored, 1)
                    if b.live:
                        tile, g = s // 4, s % 4
                        k = use_s(s) % 2
                        free_scores(b, use_s(s))
                        if s < 4:
                            pe.wait_ge(a_stored, 8 * b.n + (2 if g < 2 else 4))
                        nc.tensor.matmul(psS[k][:, :], ident_h[:, :], band_h[:, :, :].rearrange("p h k -> p (h k)"), start=True, stop=False, skip_group_check=True)
                        for j in range(PER_GROUP):
                            h = head_of(g, j)
                            r = 64 * (h % 2)
                            mm = nc.tensor.matmul(psS[k][:, 128 * j:128 * j + 128], qT[b.par][r:r + 64, h // 2, 128 * tile:128 * tile + 128],
                                                  kT[b.par][r:r + 64, h // 2, 128 * tile:128 * tile + 128], start=False, stop=j == PER_GROUP - 1, skip_group_check=True)
                        mm.then_inc(scored, 1)
                    if bp1.live:
                        pe.wait_ge(exped, 8 * bp1.n + sb1 + 1)
                        free_turn([(a_stored, ap1, sa1)] + ([(p_stored, bp3, sb3), (ctx_stored, bp4, sb4)] if b.static else []))
                        for j in range(PER_GROUP):
                            mm = nc.tensor.transpose(psT[s % 2][:, 128 * j:128 * j + 128], E[sb1 % 2][:, 128 * j:128 * j + 128], ident[:, :])
                        mm.then_inc(p_turned, 1)
                    if a.live:
                        tile, half, which = s // 4, (s // 2) % 2, s % 2
                        if s == 0:
                            pe.wait_ge(xs_ready, a.n + 1)
                            pe.wait_ge(wqkv_in, (layer_of(a.n) + 1) * 16)
                        need(pe, sin_done, 8 * a.n + s)
                        nc.tensor.matmul(psA[0][:, :], xs[a.par][:, 128 * tile:128 * tile + 128],
                                         wqkv[:, bass.ds((layer_of(a.n) & 1) * (3 * INNER) + which * INNER + half * 512, 512)],
                                         start=True, stop=True).then_inc(proj_done, 1)
                    if c.live and s == 5:
                        pe.wait_ge(csq_done, c.n + 1)
                        variances(psC, 256, 2).then_inc(var_done, 1)
                    if a.live and s % 2:
                        w = s // 2
                        c1 = c.back()
                        need(pe, v_stored, 4 * a.n + w)
                        if c1.live and w == 0:
                            pe.wait_ge(gate_stored, 2 * c1.n + 2)
                        if c1.live and w == 1:
                            pe.wait_ge(x_written, c1.n + BATCHES + 1)
                        nc.tensor.matmul(psA[1][:, :], xs[a.par][:, 128 * (w // 2):128 * (w // 2) + 128],
                                         wqkv[:, bass.ds((layer_of(a.n) & 1) * (3 * INNER) + 2 * INNER + (w % 2) * 512, 512)],
                                         start=True, stop=True).then_inc(proj_done, 1)
                    if apa.live:
                        apx, sax = lag(a, s, 5)
                        pe.wait_ge(rotated, 8 * apa.n + sa + 1)
                        free_turn([(ctx_stored, bp3, sb3)] + ([(a_stored, apx, sax), (p_stored, bp2, sb2)] if b.static else []))
                        for j in range(4):
                            mm = nc.tensor.transpose(psT[(s + 1) % 2][:, 128 * j:128 * j + 128], qs[sa % 4][:, 128 * j:128 * j + 128], ident[:, :])
                        mm.then_inc(a_turned, 1)
                    if bp1.live:
                        tile, g = sb1 // 4, sb1 % 4
                        pe.wait_ge(p_stored, 8 * bp1.n + sb1 + 1)
                        need(pe, ctx_normed, 8 * bp1.n + sb1)
                        pe.wait_ge(v_stored, 4 * bp1.n + 2 * tile + 2)
                        if tile == 1:
                            pe.wait_ge(corner_turned, 4 * bp1.n + g + 1)
                            pe.wait_ge(vc_in, (bp1.n + 1) * 16)
                        for j in range(PER_GROUP):
                            h = head_of(g, j)
                            mm = nc.tensor.matmul(psX[:, VW * j:VW * j + VW], PT[sb1 % 2][:, 128 * j:128 * j + 128], V[:, bp1.par, tile, h, :],
                                                  start=True, stop=tile == 0, skip_group_check=True)
                            if tile == 1:
                                mm = nc.tensor.matmul(psX[0:WINDOW, VW * j:VW * j + VW], PcT[sb1 % 2][:, 32 * j:32 * j + 32], Vc[:, bp1.par, h, :],
                                                      start=False, stop=True, skip_group_check=True)
                        mm.then_inc(pv_done, 1)
                    feed_forward(a, c, c.back(), s)
                    if bp2.live:
                        pe.wait_ge(ctx_normed, 8 * bp2.n + sb2 + 1)
                        free_turn([(p_stored, bp1, sb1)] + ([(a_stored, ap1, sa1), (ctx_stored, bp4, sb4)] if b.static else []))
                        for j in range(2):
                            mm = nc.tensor.transpose(psT[s % 2][:, 128 * j:128 * j + 128], cn[sb2 % 2][:, 128 * j:128 * j + 128], ident[:, :])
                        mm.then_inc(ctx_turned, 1)

            def feed_forward(a, c, c1, s):
                if c1.live and s == 0:
                    off, m = FF_CHUNKS[2]
                    need(pe, v_stored, 4 * a.n if not a.static else 4 * min(a.n, UNITS))
                    nc.tensor.matmul(psA[1][0:m, 0:256], w1[:, FF + off:FF + off + m], xg[:, :], start=True, stop=True)
                    nc.tensor.matmul(psA[1][0:m, 256:512], w1[:, off:off + m], xg[:, :], start=True, stop=True).then_inc(gates_done, 1)
                if c1.live and s == 1:
                    pe.wait_ge(gate_stored, 2 * c1.n + 1)
                    for k in range(2):
                        mm = nc.tensor.matmul(psC[:, 256 * k:256 * k + 256], w1[:, 128 * k:128 * k + 128], xg[:, :], start=True, stop=True)
                    mm.then_inc(a_done, 1)
                if c1.live and s == 2:
                    pe.wait_ge(hid_done, 2 * c1.n + 2)
                    pe.wait_ge(hid2_done, c1.n + 1)
                    pe.wait_ge(w2_in, (layer_of(c1.n) + 1) * 32)
                    if a.live:
                        pe.wait_ge(v_stored, 4 * a.n + 1)
                    for k, (off, m) in enumerate(FF_CHUNKS):
                        mm = nc.tensor.matmul(psA[1][:, 0:256], w2[0:m, k, :], hid[0:m, k, :], start=k == 0, stop=k == 2)
                    mm.then_inc(w2_done, 1)
                if not c.live:
                    return
                if s == 2:
                    pe.wait_ge(ctx_stored, 8 * c.n + 8)
                    pe.wait_ge(wo_in, (layer_of(c.n) + 1) * 64)
                    need(pe, hid_done, 2 * c.n)
                if s == 2 or s == 3:
                    for h in range(4 * (s - 2), 4 * (s - 2) + 4):
                        mm = nc.tensor.matmul(psC[:, 0:256], wo[:, h, :], cT[c.par][:, h, :], start=h == 0, stop=h == PAIRS - 1)
                if s == 3:
                    mm.then_inc(wo_done, 1)
                if s == 4:
                    pe.wait_ge(xsh_ready, c.n + 1)
                    nc.tensor.matmul(psC[:, 0:256], centre[:, :], xsh[c.par][:, :], start=True, stop=True).then_inc(centred, 1)
                if s == 6:
                    pe.wait_ge(rdev_done, c.n + 1)
                    spread_out(psC, 256, 2).then_inc(spread, 1)
                if s == 7:
                    pe.wait_ge(xg_done, c.n + 1)
                    pe.wait_ge(w1_in, (layer_of(c.n) + 1) * 16)
                    for k in range(2):
                        mm = nc.tensor.matmul(psC[:, 256 * k:256 * k + 256], w1[:, FF + 128 * k:FF + 128 * k + 128], xg[:, :], start=True, stop=True)
                    mm.then_inc(gates_done, 1)

            pe.wait_ge(x_written, BATCHES)
            pe.wait_ge(halves_ready, 7)
            over_units(pe, iteration, UNITS, FIRST, LAST)

            for k in range(4):
                pe.wait_ge(y_ready, k + 1)
                nc.tensor.matmul(psS[k % 2][:, :], centre[:, :], y[k % 2][:, :], start=True, stop=True).then_inc(y_centred, 1)
                pe.wait_ge(y_sq, k + 1)
                variances(psC, 0, 4).then_inc(y_var, 1)
                pe.wait_ge(y_rdev, k + 1)
                spread_out(psA[k % 2], 0, 4).then_inc(y_spread, 1)
                pe.wait_ge(y_normed, k + 1)
                for j in range(4):
                    mm = nc.tensor.transpose(psT[k % 2][:, 128 * j:128 * j + 128], yn[k % 2][:, 128 * j:128 * j + 128], ident[:, :])
                mm.then_inc(y_turned, 1)

        @block.scalar
        def _(act):
            for n in range(12):
                act.wait_ge(turned, n + 1)
                dst = X[:, BATCHES * TOKENS + 512 * n:BATCHES * TOKENS + 512 * n + 512] if n < 4 else wT[:, (n - 4) // 2, 512 * (n % 2):512 * (n % 2) + 512]
                nc.scalar.copy(dst, psT[n % 2][:, :]).then_inc(turned_out, 1)

            act.wait_ge(turned, 13)
            nc.scalar.copy(cols[:, :], psT[0][:, 0:128]).then_inc(turned_out, 1)
            act.wait_ge(turned_out, 13)

            def first_attention(a, b, c):
                for s in range(8):
                    if a.live:
                        act.wait_ge(proj1, 12 * a.n + s + s // 2 + 1)
                        need(act, score1, 2 * (8 * (a.n - 2) + s) + 2)
                        nc.scalar.activation(qT[a.par][:, s, :], psA[0][:, 0:256], ACT.Identity, bias=qb[:, s:s + 1])
                        nc.scalar.activation(kT[a.par][:, s, :], psA[0][:, 256:512], ACT.Identity, bias=kb[:, s:s + 1]).then_inc(qk1_stored, 1)
                    ub, sb_ = lag(b, s, 1)
                    if ub.live and ub is not b or (ub.live and s):
                        act.wait_ge(pv1, 2 * (8 * ub.n + sb_) + 2)
                        need(act, wl_done, ub.n - 1)
                        nc.scalar.copy(cT[ub.par][:, sb_, :], psX[:, 0:256]).then_inc(ctx1, 1)
                    if b.live:
                        for j in range(2):
                            e = (s % 2) * 2 + j
                            act.wait_ge(nm1, 2 * (8 * b.n + s) + j + 1)
                            need(act, pv1, 2 * (8 * b.n + s - 2) + j + 1)
                            for t in range(2):
                                nc.scalar.activation(E[e][:, 256 * t:256 * t + 256], psS[j][:, 256 * t:256 * t + 256], ACT.Exp, bias=nm[j][:, t:t + 1],
                                                     scale=HEAD ** -0.5, accum_out=sums[e][:, t:t + 1]).then_inc(exp1, 1)
                    if c.live and s == 2:
                        act.wait_ge(centred1, c.n + 1)
                        need(act, var1, c.n)
                        nc.scalar.activation(csq[:, 0:256], psC[:, 0:256], ACT.Square).then_inc(csq1, 1)
                    if c.live and s == 6:
                        act.wait_ge(spread1, c.n + 1)
                        need(act, x_written, c.n)
                        nc.scalar.copy(rstd[:, 0:256], psC[:, 256:512]).then_inc(rstd1, 1)

            over_units(act, first_attention, BATCHES, 2, BATCHES - 2)

            def iteration(a, b, c):
                for s in range(8):
                    if b.live and s == 4:
                        need(act, corner_shifted, 4 * b.n)
                        for r in range(2):
                            act.wait_ge(corner_maxed, 2 * b.n + r + 1)
                            nc.scalar.copy(Sc[:, PAIRS * r:PAIRS * r + PAIRS, :].rearrange("p h k -> p (h k)"), psS[r][0:WINDOW, 0:256]).then_inc(corner_stored, 1)
                    bp1, sb1 = lag(b, s, 1)
                    if bp1.live:
                        act.wait_ge(p_turned, 8 * bp1.n + sb1 + 1)
                        need(act, pv_done, 8 * bp1.n + sb1 - 1)
                        nc.scalar.copy(PT[sb1 % 2][:, :], psT[s % 2][:, :]).then_inc(p_stored, 1)
                    if a.live:
                        act.wait_ge(proj_done, 12 * a.n + s + s // 2 + 1)
                        need(act, summed, 8 * a.n + s - 1)
                        nc.scalar.activation(sq[s % 2][:, :], psA[0][:, :], ACT.Square).then_inc(squared, 1)
                    if b.live:
                        act.wait_ge(shifted, 8 * b.n + s + 1)
                        nc.scalar.activation(E[s % 2][:, :], E[s % 2][:, :], ACT.Exp, scale=QK_SCALE).then_inc(exped, 1)
                        if s >= 4:
                            act.wait_ge(corner_shifted, 4 * b.n + s - 3)
                            nc.scalar.activation(Ec[s % 2][:, :], Ec[s % 2][:, :], ACT.Exp, scale=QK_SCALE).then_inc(corner_exped, 1)
                    c1 = c.back()
                    if c1.live and s == 1:
                        m = FF_CHUNKS[2][1]
                        act.wait_ge(gate_stored, 2 * c1.n + 2)
                        nc.scalar.activation(gate[0:m, 2, :], gate[0:m, 2, :], ACT.Gelu).then_inc(gelu_done, 1)
                        nc.scalar.activation(gate[:, 0:2, :], gate[:, 0:2, :], ACT.Gelu).then_inc(gelu_done, 1)
                    if a.live and s % 2:
                        w = s // 2
                        act.wait_ge(proj_done, 12 * a.n + 3 * w + 3)
                        need(act, pv_done, 8 * (a.n - 1))
                        nc.scalar.copy(V[:, a.par, w // 2, 8 * (w % 2):8 * (w % 2) + 8, 0:HEAD], heads8(psA[1][:, :])).then_inc(v_stored, 1)
                    apa, sa = lag(a, s, 3)
                    if apa.live:
                        tile, half, which = sa // 4, (sa // 2) % 2, sa % 2
                        act.wait_ge(a_turned, 8 * apa.n + sa + 1)
                        need(act, scored, 10 * (apa.n - 1))
                        dst = (kT if which else qT)[apa.par]
                        nc.scalar.copy(dst[:, 4 * half:4 * half + 4, 128 * tile:128 * tile + 128],
                                       psT[(s + 1) % 2][:, :].rearrange("p (c t) -> p c t", c=4)).then_inc(a_stored, 1)
                    if c.live and s == 4:
                        act.wait_ge(centred, c.n + 1)
                        need(act, var_done, c.n)
                        nc.scalar.activation(csq[:, 0:256], psC[:, 0:256], ACT.Square).then_inc(csq_done, 1)
                    if c.live and s == 6:
                        act.wait_ge(spread, c.n + 1)
                        need(act, xn_done, c.n)
                        nc.scalar.copy(rstd[:, 0:256], psC[:, 256:512]).then_inc(rstd_done, 1)
                    bp2, sb2 = lag(b, s, 2)
                    if bp2.live:
                        tile, g = sb2 // 4, sb2 % 4
                        act.wait_ge(ctx_turned, 8 * bp2.n + sb2 + 1)
                        need(act, wo_done, bp2.n - 1)
                        nc.scalar.copy(cT[bp2.par][:, chunk_of(g, 0):chunk_of(g, 1) + 1:2, 128 * tile:128 * tile + 128],
                                       psT[s % 2][:, 0:256].rearrange("p (c t) -> p c t", c=2)).then_inc(ctx_stored, 1)

            act.wait_ge(x_written, BATCHES)
            nc.scalar.copy(x1[:, :], X[:, 0:BATCHES * TOKENS]).then_inc(x1_kept, 1)
            over_units(act, iteration, UNITS, FIRST, LAST)

            for k in range(4):
                act.wait_ge(y_centred, k + 1)
                nc.scalar.activation(csq[:, :], psS[k % 2][:, :], ACT.Square).then_inc(y_sq, 1)
                act.wait_ge(y_spread, k + 1)
                nc.scalar.copy(rstd[:, :], psA[k % 2][:, :]).then_inc(y_rstd, 1)
                act.wait_ge(y_turned, k + 1)
                if k >= 2:
                    act.wait_ge(stored[k - 2], 16)
                nc.scalar.copy(yo[k % 2][:, :], psT[k % 2][:, :]).then_inc(y_out, 1)

        @block.vector
        def _(dve):
            dve.wait_ge(ident_in, 16)
            dve.wait_ge(const_in, 16 * 5)
            nc.vector.tensor_copy(ident_h[:, :], ident[:, :]).then_inc(halves_ready, 1)
            nc.vector.tensor_copy(band_h[:, :, :], band[:, :].unsqueeze(1).to_broadcast([PARTS, PER_GROUP, PARTS])).then_inc(halves_ready, 1)
            nc.vector.tensor_copy(corner_h[:, :, :], corner[:, :].unsqueeze(1).to_broadcast([PARTS, PAIRS, WINDOW])).then_inc(halves_ready, 1)

            for t in (xs[0], xs[1], xsh[0], xsh[1]):
                nc.vector.memset(t[64:128, 0:1], 0.0).then_inc(halves_ready, 1)

            def first_input(u, par):
                need(dve, proj1, 12 * (u - 1))
                nc.vector.tensor_copy(xs1[par][:, :], X[:, slot(u + BATCHES)]).then_inc(xs1_ready, 1)

            def first_attention(a, b, c):
                for s in range(8):
                    if c.live and s == 2:
                        dve.wait_ge(wl_done, c.n + 1)
                        nc.vector.scalar_tensor_tensor(out=xr[c.par][:, :], in0=psC[:, 0:256], scalar=lb[:, :], in1=X[:, slot(c.n + BATCHES)],
                                                       op0=ALU.add, op1=ALU.add).then_inc(resid1, 1)
                    if c.live and s == 4:
                        dve.wait_ge(var1, c.n + 1)
                        nc.vector.tensor_scalar(var[:, 0:2], psC[:, 256:258], EPS, None, ALU.add).then_inc(eps1, 1)
                    if c.live and s == 7:
                        dve.wait_ge(rstd1, c.n + 1)
                        nc.vector.tensor_tensor(X[:, slot(c.n)], psC[:, 0:256], rstd[:, 0:256], ALU.mult).then_inc(x_written, 1)
                    if b.live:
                        for j in range(2):
                            i = 2 * (8 * b.n + s) + j
                            dve.wait_ge(score1, i + 1)
                            nc.vector.tensor_reduce(mx[j][:, 0:2], psS[j][:, :].rearrange("p (t q) -> p t q", t=2), AX.X, ALU.max).then_inc(max1, 1)
                            dve.wait_ge(max1, i + 1)
                            need(dve, exp1, 4 * (8 * b.n + s - 1) + 2 * j + 2)
                            nc.vector.tensor_scalar(nm[j][:, :], mx[j][:, 0:2], -(HEAD ** -0.5), None, ALU.mult).then_inc(nm1, 1)
                    if a.live and s % 2:
                        w = s // 2
                        dve.wait_ge(proj1, 12 * a.n + 3 * w + 3)
                        dve.wait_ge(bias_in, 16)
                        nc.vector.tensor_tensor(V[:, a.par, w // 2, 8 * (w % 2):8 * (w % 2) + 8, 0:HEAD], heads8(psA[1][:, :]),
                                                heads8(vb[:, 512 * (w % 2):512 * (w % 2) + 512]), ALU.add).then_inc(v1_stored, 1)
                    if b.live:
                        for j in range(2):
                            i = 2 * (8 * b.n + s) + j
                            e = (s % 2) * 2 + j
                            dve.wait_ge(exp1, 2 * i + 2)
                            nc.vector.reciprocal(rinv[e][:, 0:2], sums[e][:, :]).then_inc(rinv1, 1)
                            dve.wait_ge(rinv1, i + 1)
                            dve.wait_ge(v1_stored, 4 * b.n + 4)
                            need(dve, pv1, i - 3)
                            nc.vector.tensor_tensor(Vs[e][:, :, :], V[:, b.par, :, 2 * s + j, 0:HEAD], rinv[e][:, 0:2].unsqueeze(2).to_broadcast([PARTS, 2, HEAD]),
                                                    ALU.mult).then_inc(vs1, 1)
                    if s == 6 and (not a.static or 0 < a.n + 1 < BATCHES):
                        first_input(a.n + 1, 1 - a.par)

            dve.wait_ge(turned_out, 13)
            first_input(0, 0)
            over_units(dve, first_attention, BATCHES, 2, BATCHES - 2)

            def unit_input(u, par):
                need(dve, proj_done, 12 * (u - 1))
                dve.wait_ge(x_written, u + 1)
                nc.vector.tensor_copy(xs[par][0:64, :], X[0:64, slot(u)])
                nc.vector.tensor_copy(xs[par][64:128, 1:TOKENS], X[64:128, slot(u, 0, TOKENS - 1)]).then_inc(xs_ready, 1)

            def feed_forward(c, c1, s):
                if c1.live and s == 0:
                    dve.wait_ge(gates_done, 2 * c1.n + 1)
                    need(dve, hid_done, 2 * c1.n)
                    for k in range(2):
                        ins = nc.vector.tensor_scalar(gate[:, k, :], psC[:, 256 * k:256 * k + 256], cols[:, bass.ds(layer_of(c1.n) + B1 + (3 + k) * LAYERS, 1)], None, ALU.add)
                    ins.then_inc(gate_stored, 1)
                if c1.live and s == 1:
                    m = FF_CHUNKS[2][1]
                    dve.wait_ge(gates_done, 2 * c1.n + 2)
                    need(dve, w2_done, c1.n)
                    nc.vector.tensor_scalar(gate[0:m, 2, :], psA[1][0:m, 0:256], cols[0:m, bass.ds(layer_of(c1.n) + B1 + 5 * LAYERS, 1)], None, ALU.add)
                    nc.vector.tensor_scalar(hid[0:m, 2, :], psA[1][0:m, 256:512], cols[0:m, bass.ds(layer_of(c1.n) + B1 + 2 * LAYERS, 1)], None, ALU.add).then_inc(gate_stored, 1)
                if c1.live and s == 2:
                    m = FF_CHUNKS[2][1]
                    dve.wait_ge(gelu_done, 2 * c1.n + 1)
                    nc.vector.tensor_tensor(hid[0:m, 2, :], hid[0:m, 2, :], gate[0:m, 2, :], ALU.mult).then_inc(hid2_done, 1)
                    for k in range(2):
                        dve.wait_ge(a_done, c1.n + 1)
                        dve.wait_ge(gelu_done, 2 * c1.n + 2)
                        nc.vector.scalar_tensor_tensor(out=hid[:, k, :], in0=psC[:, 256 * k:256 * k + 256], scalar=cols[:, bass.ds(layer_of(c1.n) + B1 + k * LAYERS, 1)],
                                                       in1=gate[:, k, :], op0=ALU.add, op1=ALU.mult).then_inc(hid_done, 1)
                if c1.live and s == 3:
                    dve.wait_ge(w2_done, c1.n + 1)
                    nc.vector.scalar_tensor_tensor(out=X[:, slot(c1.n + BATCHES)], in0=psA[1][:, 0:256],
                                                   scalar=cols[:, bass.ds(layer_of(c1.n) + B2, 1)], in1=xr[c1.par][:, :], op0=ALU.add, op1=ALU.add).then_inc(x_written, 1)
                if not c.live:
                    return
                if s == 4:
                    dve.wait_ge(wo_done, c.n + 1)
                    nc.vector.tensor_tensor(xr[c.par][:, :], psC[:, 0:256], X[:, slot(c.n)], ALU.add).then_inc(resid, 1)
                    dve.wait_ge(resid, c.n + 1)
                    nc.vector.tensor_copy(xsh[c.par][0:64, :], xr[c.par][0:64, :])
                    nc.vector.tensor_copy(xsh[c.par][64:128, 1:TOKENS], xr[c.par][64:128, 0:TOKENS - 1]).then_inc(xsh_ready, 1)
                if s == 7:
                    normalise(c)

            def normalise(c):
                dve.wait_ge(rstd_done, c.n + 1)
                nc.vector.tensor_tensor(xn[:, :], psC[:, 0:256], rstd[:, 0:256], ALU.mult).then_inc(xn_done, 1)
                dve.wait_ge(xn_done, c.n + 1)
                need(dve, a_done, c.n)
                nc.vector.tensor_scalar(xg[:, :], xn[:, :], cols[:, bass.ds(layer_of(c.n) + LNG, 1)], cols[:, bass.ds(layer_of(c.n) + LNB, 1)], ALU.mult, ALU.add).then_inc(xg_done, 1)

            def iteration(a, b, c):
                for s in range(8):
                    feed_forward(c, c.back(), s)
                    if b.live and s == 4:
                        for r in range(2):
                            dve.wait_ge(scored, 10 * b.n + CORNER_USE + r + 1)
                            nc.vector.tensor_reduce(mc[:, PAIRS * r:PAIRS * r + PAIRS], psS[r][0:WINDOW, 0:256].rearrange("p (h k) -> p h k", k=WINDOW),
                                                    AX.X, ALU.max).then_inc(corner_maxed, 1)
                    if b.live:
                        k = use_s(s) % 2
                        m, e, g = mx[s % 2], E[s % 2], s % 4
                        dve.wait_ge(scored, 10 * b.n + use_s(s) + 1)
                        nc.vector.tensor_reduce(m[:, :], heads4(psS[k][:, :]), AX.X, ALU.max).then_inc(maxed, 1)
                        if s >= 4:
                            dve.wait_ge(maxed, 12 * b.n + s + 1 + (s - 4))
                            dve.wait_ge(corner_maxed, 2 * b.n + 2)
                            nc.vector.tensor_tensor(m[0:WINDOW, :], m[0:WINDOW, :], mc[:, kept(g)], ALU.max).then_inc(maxed, 1)
                        dve.wait_ge(maxed, 12 * b.n + s + 1 + (s - 3 if s >= 4 else 0))
                        need(dve, p_turned, 8 * b.n + s - 1)
                        nc.vector.tensor_tensor(heads4(e[:, :]), heads4(psS[k][:, :]), m[:, :].unsqueeze(2).to_broadcast([PARTS, PER_GROUP, PARTS]),
                                                ALU.subtract).then_inc(shifted, 1)
                        if s >= 4:
                            dve.wait_ge(corner_stored, 2 * b.n + 2)
                            need(dve, corner_turned, 4 * b.n + s - 5)
                            nc.vector.tensor_tensor(Ec[s % 2][:, :].rearrange("p (h k) -> p h k", k=WINDOW), Sc[:, kept(g), :],
                                                    m[0:WINDOW, :].unsqueeze(2).to_broadcast([WINDOW, PER_GROUP, WINDOW]), ALU.subtract).then_inc(corner_shifted, 1)
                    if c.live and s == 5:
                        dve.wait_ge(var_done, c.n + 1)
                        need(dve, rdev_done, c.n)
                        nc.vector.tensor_scalar(var[:, 0:2], psC[:, 256:258], EPS, None, ALU.add).then_inc(eps_added, 1)
                    if a.live:
                        tile, which = s // 4, s % 2
                        i = 8 * a.n + s
                        rotated_half = heads8(psA[0][:, :]).rearrange("p h (a d) -> p h a d", a=2)[:, :, ::-1, :]
                        dve.wait_ge(squared, i + 1)
                        need(dve, added, i - 1)
                        nc.vector.tensor_tensor(heads8(qc[s % 2][:, :]), heads8(psA[0][:, :]),
                                                tables[:, table(layer_of(a.n), tile, 2 * which)].unsqueeze(1).to_broadcast([PARTS, 8, HEAD]), ALU.mult).then_inc(cos_done, 1)
                        need(dve, a_turned, i - 3)
                        nc.vector.tensor_tensor(heads8(qs[s % 4][:, :]).rearrange("p h (a d) -> p h a d", a=2), rotated_half,
                                                tables[:, table(layer_of(a.n), tile, 2 * which + 1)].rearrange("p (o a d) -> p o a d", o=1, a=2)
                                                .to_broadcast([PARTS, 8, 2, HEAD // 2]), ALU.mult).then_inc(sin_done, 1)
                        norms = n2[(s // 2) % 2]
                        need(dve, rotated, i - 3 - s % 2)
                        nc.vector.tensor_reduce(norms[:, 8 * which:8 * which + 8], heads8(sq[s % 2][:, :]), AX.X, ALU.add).then_inc(summed, 1)
                        if which:
                            dve.wait_ge(summed, i + 1)
                            nc.vector.tensor_scalar(norms[:, :], norms[:, :], 1e-24, None, ALU.max).then_inc(guarded, 1)
                    if b.live and s >= 4:
                        dve.wait_ge(corner_exped, 4 * b.n + s - 3)
                        need(dve, pv_done, 8 * b.n + s - 1)
                        nc.vector.transpose(PcT[s % 2][:, :], Ec[s % 2][:, :]).then_inc(corner_turned, 1)
                    bp1, sb1 = lag(b, s, 1)
                    if bp1.live:
                        i = 8 * bp1.n + sb1
                        px = psX[:, 0:PER_GROUP * VW].rearrange("p (h e) -> p h e", e=VW)
                        dve.wait_ge(pv_done, i + 1)
                        nc.vector.reciprocal(rinv[sb1 % 2][:, :].unsqueeze(2), px[:, :, HEAD:VW]).then_inc(recip_done, 1)
                        dve.wait_ge(recip_done, i + 1)
                        need(dve, ctx_turned, i - 1)
                        nc.vector.tensor_tensor(cn[sb1 % 2][:, :].rearrange("p (h d) -> p h d", d=HEAD), px[:, :, 0:HEAD],
                                                rinv[sb1 % 2][:, :].unsqueeze(2).to_broadcast([PARTS, PER_GROUP, HEAD]), ALU.mult).then_inc(ctx_normed, 1)
                    if s == 6 and (not a.static or 0 < a.n + 1 < UNITS):
                        unit_input(a.n + 1, 1 - a.par)

            def kept(g):
                at = PAIRS * (g % 2) + PER_GROUP * (g // 2)
                return slice(at, at + PER_GROUP)

            def heads4(ap):
                return ap.rearrange("p (h k) -> p h k", k=PARTS)

            dve.wait_ge(x_written, BATCHES)
            dve.wait_ge(x1_kept, 1)
            dve.wait_ge(cleared, 2)
            dve.wait_ge(tables_ready, LAYERS * TILES)
            unit_input(0, 0)
            over_units(dve, iteration, UNITS, FIRST, LAST)

            dve.wait_ge(x_written, UNITS + BATCHES)
            for k in range(4):
                nc.vector.tensor_tensor(y[k % 2][:, :], X[:, 512 * k:512 * k + 512], x1[:, 512 * k:512 * k + 512], ALU.add).then_inc(y_ready, 1)
                dve.wait_ge(y_var, k + 1)
                nc.vector.tensor_scalar(var[:, :], psC[:, 0:4], EPS, None, ALU.add).then_inc(y_eps, 1)
                dve.wait_ge(y_rstd, k + 1)
                nc.vector.tensor_tensor(yn[k % 2][:, :], psS[k % 2][:, :], rstd[:, :], ALU.mult).then_inc(y_normed, 1)


FIRST, LAST = 2, UNITS - 2

_INS = ["L0_attn_x", "L0_attn_q_w", "L0_attn_q_b", "L0_attn_k_w", "L0_attn_k_b", "L0_attn_v_w", "L0_attn_v_b", "L0_attn_l_w", "L0_attn_l_b",
        "L0_ffn_Wqkv", "L0_ffn_q_scale", "L0_ffn_k_scale", "L0_ffn_Wo", "L0_ffn_ln_g", "L0_ffn_ln_b", "L0_ffn_W1", "L0_ffn_b1", "L0_ffn_W2", "L0_ffn_b2"]


def kernel(**inputs):
    import concourse.bacc as _bacc
    from concourse.bass_utils import run_bass_kernel_spmd as _run

    nc = _bacc.Bacc("TRN2", target_bir_lowering=False, num_devices=1)
    arrays, args = {}, []
    given = [(f"in_{n}_dram", np.ascontiguousarray(inputs[n])) for n in _INS]
    for name, a in given + [(f"const_{n}_dram", a) for n, a in constants().items()]:
        if name == "const_rotary_dram":
            a = a.reshape(PARTS, -1)
        arrays[name] = a
        args.append(nc.dram_tensor(name, a.shape, mybir.dt.from_np(a.dtype), kind="ExternalInput").ap())
    args.append(nc.dram_tensor("out_0_dram", (BATCHES, TOKENS, DIM), F32, kind="ExternalOutput").ap())
    postln_kernel(nc, *args)
    r = _run(nc, [arrays], core_ids=[0])
    return r.results[0]["out_0_dram"]
```

```python
from contextlib import ExitStack

import numpy as np

import concourse.bass as bass
from concourse import mybir

F32 = mybir.dt.float32
BF16 = mybir.dt.bfloat16
I32 = mybir.dt.int32
ALU = mybir.AluOpType
ACT = mybir.ActivationFunctionType
AX = mybir.AxisListType

PARTS = 128
BATCHES, TOKENS, DIM = 8, 256, 128
HEADS, HEAD = 16, 64
INNER = HEADS * HEAD
PAIRS = HEADS // 2
LAYERS = 6
WINDOW = 32
TILES = TOKENS // PARTS
GROUPS = 4
PER_GROUP = HEADS // GROUPS
FF = int(DIM * 4 * 2 / 3)
FF_CHUNKS = [(0, 128), (128, 128), (256, FF - 256)]
UNITS = LAYERS * BATCHES
RING = 2 * BATCHES
EPS = 1e-5
RSQRT_BITS = 0x5F3759DF
QK_SCALE = 8.0
MASKED = -1e30


def constants():
    ident = np.eye(PARTS, dtype=np.float32)
    mean = np.full((PARTS, PARTS), 1.0 / DIM, np.float32)
    q, k = np.arange(PARTS)[:, None], np.arange(PARTS)[None, :]
    band = np.where((q < k) | (q > k + WINDOW), np.float32(MASKED), np.float32(0))
    corner = np.zeros((PARTS, WINDOW), np.float32)
    corner[:WINDOW] = np.where(np.arange(WINDOW)[:, None] > np.arange(WINDOW)[None, :], MASKED, 0)
    half = np.arange(0, HEAD, 2, dtype=np.float32)
    inv_freq = (1.0 / 10000.0 ** (half / HEAD)).astype(np.float32)
    t = np.arange(TOKENS, dtype=np.float32)
    freqs = t[:, None] * inv_freq[None, :]
    freqs = np.concatenate([freqs, freqs], -1).astype(np.float64)
    base = ((half + 0.4 * HEAD) / (1.4 * HEAD)).astype(np.float32)
    scale = base[None, :].astype(np.float64) ** ((t - TOKENS // 2) / (WINDOW // 2))[:, None]
    scale = np.concatenate([scale, scale], -1)
    sign = np.where(np.arange(HEAD) < HEAD // 2, -1.0, 1.0)
    cos, sin = np.cos(freqs), np.sin(freqs) * sign
    tables = np.stack([cos * scale * QK_SCALE, sin * scale * QK_SCALE, cos / scale, sin / scale], 1).astype(np.float32)
    tables = tables.reshape(TILES, PARTS, 4, HEAD).transpose(1, 0, 2, 3)
    return {
        "ident": ident, "mean": mean, "centre": ident - mean, "band": band, "corner": corner,
        "rotary": np.ascontiguousarray(tables),
    }


class Unit:

    def __init__(self, n, par, count):
        self.n, self.par, self.count = n, par, count
        self.static = isinstance(n, int)
        self.live = not self.static or 0 <= n < count

    def back(self):
        return Unit(self.n - 1, 1 - self.par, self.count)


def lag(unit, s, k):
    return (unit, s - k) if s >= k else (unit.back(), s - k + 8)


def need(eng, sem, value):
    if not isinstance(value, int) or value > 0:
        eng.wait_ge(sem, value)


def over_units(eng, slot_of, count, first, last, begin, end):
    def at(i, par):
        for s in range(8):
            slot_of(Unit(i + 1, 1 - par, count), Unit(i, par, count), Unit(i - 1, 1 - par, count), s)

    for i in range(begin, first):
        at(i, i % 2)
    with eng.Fori(first, last, 2) as r:
        at(r, first % 2)
        at(r + 1, 1 - first % 2)
    for i in range(last, end):
        at(i, i % 2)


def change_over(first_slot, slot_of):
    for s in range(8):
        first_slot(Unit(BATCHES + 1, 1, BATCHES), Unit(BATCHES, 0, BATCHES), Unit(BATCHES - 1, 1, BATCHES), s)
        slot_of(Unit(0, 0, UNITS), Unit(-1, 1, UNITS), Unit(-2, 0, UNITS), s)


def postln_kernel(nc, x, q_w, q_b, k_w, k_b, v_w, v_b, l_w, l_b, Wqkv, q_scale, k_scale, Wo,
                  ln_g, ln_b, W1, b1, W2, b2, ident_d, mean_d, centre_d, band_d, corner_d, rotary_d,
                  out):
    ctx = ExitStack()
    with ctx:
        def sb(name, shape, dt=F32):
            return ctx.enter_context(nc.sbuf_tensor(name, shape, dt))

        def sem(name):
            return ctx.enter_context(nc.semaphore(name))

        psA = [ctx.enter_context(nc.psum_tensor(f"psA{i}", [PARTS, 512], F32)) for i in range(2)]
        psS = [ctx.enter_context(nc.psum_tensor(f"psS{i}", [PARTS, 512], F32)) for i in range(2)]
        psT = [ctx.enter_context(nc.psum_tensor(f"psT{i}", [PARTS, 512], F32)) for i in range(2)]
        psX = ctx.enter_context(nc.psum_tensor("psX", [PARTS, 512], F32))
        psC = ctx.enter_context(nc.psum_tensor("psC", [PARTS, 512], F32))

        ident = sb("ident", [PARTS, PARTS])
        mean = sb("mean", [PARTS, PARTS])
        centre = sb("centre", [PARTS, PARTS])
        band = sb("band", [PARTS, PARTS])
        corner = sb("corner", [PARTS, WINDOW])
        rotary = sb("rotary", [PARTS, TILES * 4 * HEAD])
        ident_h = sb("ident_h", [PARTS, PARTS], BF16)
        band_h = sb("band_h", [PARTS, PER_GROUP, PARTS], BF16)
        corner_h = sb("corner_h", [PARTS, PAIRS, WINDOW], BF16)
        tables = sb("tables", [PARTS, LAYERS * TILES * 4 * HEAD])
        rows = sb("rows", [PARTS, PARTS])
        cols = sb("cols", [PARTS, PARTS])
        QB, KB, LB = 0, PAIRS, 2 * PAIRS
        LNG = LB + 1
        LNB, B2, B1 = LNG + LAYERS, LNG + 2 * LAYERS, LNG + 3 * LAYERS
        qb, kb, lb = cols[:, QB:QB + PAIRS], cols[:, KB:KB + PAIRS], cols[:, LB:LB + 1]
        wqkv = sb("wqkv", [PARTS, 2 * 3 * INNER])
        wo = sb("wo", [PARTS, PAIRS, DIM])
        w1 = sb("w1", [PARTS, 2 * FF])
        w2 = sb("w2", [PARTS, 3, DIM])
        X = sb("X", [PARTS, RING * TOKENS])
        x1 = sb("x1", [PARTS, BATCHES * TOKENS])
        arena = sb("arena", [PARTS, 8192])
        taken = [0]

        def part(columns, view=None, **sizes):
            ap = arena[:, taken[0]:taken[0] + columns]
            taken[0] += columns
            return ap.rearrange(view, **sizes) if view else ap

        wT = part(4 * INNER, "p (m n) -> p m n", m=4)
        xraw = part(BATCHES * TOKENS, "p (t d) -> p t d", d=DIM)
        raw_l = part(INNER, "p (c n) -> p c n", n=PARTS)
        vb = part(INNER)
        raw = [wqkv[:, (3 + i) * INNER:(4 + i) * INNER].rearrange("p (c n) -> p c n", n=PARTS) for i in range(3)] + [raw_l]
        taken[0] = 0
        sq, qc = ([part(512) for _ in range(2)] for _ in range(2))
        qs = [part(512) for _ in range(4)]
        PT = [part(512) for _ in range(2)]
        gate, hid = (part(3 * TOKENS, "p (c t) -> p c t", c=3) for _ in range(2))
        Sc = part(HEADS * WINDOW, "p (h k) -> p h k", k=WINDOW)[0:WINDOW]
        xn, xg = part(TOKENS), part(TOKENS)
        xs1 = [sb(f"xs1_{i}", [PARTS, TOKENS]) for i in range(2)]
        xs = [sb(f"xs{i}", [PARTS, TOKENS]) for i in range(2)]
        qT = [sb(f"qT{i}", [PARTS, PAIRS, TOKENS]) for i in range(2)]
        kT = [sb(f"kT{i}", [PARTS, PAIRS, TOKENS]) for i in range(2)]
        V = sb("V", [PARTS, 2, TILES, HEADS, HEAD])
        Vc_all = sb("Vc", [PARTS, 2 * HEADS * HEAD])
        Vc = Vc_all[0:WINDOW, :].rearrange("p (a h e) -> p a h e", a=2, e=HEAD)
        scales = Vc_all[:, 0:LAYERS * 4 * HEAD].rearrange("p (l j d) -> p l j d", l=LAYERS, j=4)
        cT = [sb(f"cT{i}", [PARTS, PAIRS, TOKENS]) for i in range(2)]
        n2 = [sb(f"n2{i}", [PARTS, HEADS + TILES]) for i in range(2)]
        rn = [sb(f"rn{i}", [PARTS, HEADS + TILES]) for i in range(2)]
        E = [sb(f"E{i}", [PARTS, 512]) for i in range(4)]
        mx = [sb(f"mx{i}", [PARTS, PER_GROUP]) for i in range(2)]
        nm = [sb(f"nm{i}", [PARTS, PER_GROUP]) for i in range(4)]
        sums = [sb(f"sums{i}", [PARTS, PER_GROUP]) for i in range(4)]
        corner_sums = sb("corner_sums", [WINDOW, PER_GROUP])
        rinv = [sb(f"rinv{i}", [PARTS, 4]) for i in range(4)]
        Vs = [sb(f"Vs{i}", [PARTS, 2, HEAD]) for i in range(4)]
        mc = sb("mc", [WINDOW, HEADS])
        Ec = [sb(f"Ec{i}", [WINDOW, 128]) for i in range(2)]
        PcT = [sb(f"PcT{i}", [WINDOW, 128]) for i in range(2)]
        xr = [sb(f"xr{i}", [PARTS, TOKENS]) for i in range(2)]
        xsh = [sb(f"xsh{i}", [PARTS, TOKENS]) for i in range(2)]
        csq = sb("csq", [PARTS, TOKENS])
        rstd = sb("rstd", [PARTS, TOKENS])
        var = sb("var", [PARTS, 16])
        rdev = sb("rdev", [PARTS, 16])
        guess = [sb(f"guess{i}", [PARTS, HEADS + TILES]) for i in range(2)]
        def quarters(t):
            return [t[:, 2 * k:2 * k + 2, :].rearrange("p c t -> p (c t)") for k in range(4)]

        y, y_squares, y_dev, yn, yo = (quarters(t) for t in (qT[0], kT[1], cT[0], qT[1], kT[0]))
        centred_y, spread_y = psS + psT, psA + [psX, psC]

        x_in = sem("x_in")
        raw_in = [sem(f"raw_in{i}") for i in range(4)]
        ident_in = sem("ident_in")
        const_in = sem("const_in")
        bias_in = sem("bias_in")
        param_in = sem("param_in")
        scale_in = sem("scale_in")
        wqkv_in = sem("wqkv_in")
        wo_in = sem("wo_in")
        w1_in = sem("w1_in")
        w2_in = sem("w2_in")
        vc_in = sem("vc_in")
        stored = [sem(f"stored{i}") for i in range(4)]
        sp_passed = sem("sp_passed")
        pool_passed = sem("pool_passed")
        act_passed = sem("act_passed")
        halves_ready = sem("halves_ready")
        cleared = sem("cleared")
        tables_ready = sem("tables_ready")
        turned = sem("turned")
        turned_out = sem("turned_out")
        xs1_ready = sem("xs1_ready")
        proj1 = sem("proj1")
        qk1_stored = sem("qk1_stored")
        v1_stored = sem("v1_stored")
        score1 = sem("score1")
        max1 = sem("max1")
        nm1 = sem("nm1")
        exp1 = sem("exp1")
        rinv1 = sem("rinv1")
        vs1 = sem("vs1")
        pv1 = sem("pv1")
        ctx1 = sem("ctx1")
        wl_done = sem("wl_done")
        resid1 = sem("resid1")
        centred1 = sem("centred1")
        csq1 = sem("csq1")
        var1 = sem("var1")
        eps1 = sem("eps1")
        rdev1 = sem("rdev1")
        spread1 = sem("spread1")
        rstd1 = sem("rstd1")
        x_written = sem("x_written")
        x1_kept = sem("x1_kept")
        xs_ready = sem("xs_ready")
        proj_done = sem("proj_done")
        squared = sem("squared")
        summed = sem("summed")
        guarded = sem("guarded")
        cos_done = sem("cos_done")
        sin_done = sem("sin_done")
        added = sem("added")
        rotated = sem("rotated")
        v_stored = sem("v_stored")
        a_turned = sem("a_turned")
        a_stored = sem("a_stored")
        scored = sem("scored")
        maxed = sem("maxed")
        exped = sem("exped")
        p_turned = sem("p_turned")
        p_stored = sem("p_stored")
        corner_maxed = sem("corner_maxed")
        corner_stored = sem("corner_stored")
        corner_shifted = sem("corner_shifted")
        corner_exped = sem("corner_exped")
        corner_turned = sem("corner_turned")
        pv_done = sem("pv_done")
        recip_done = sem("recip_done")
        corner_summed = sem("corner_summed")
        sums_whole = sem("sums_whole")
        weighted = sem("weighted")
        corner_weighted = sem("corner_weighted")
        ctx_stored = sem("ctx_stored")
        wo_done = sem("wo_done")
        resid = sem("resid")
        xsh_ready = sem("xsh_ready")
        centred = sem("centred")
        csq_done = sem("csq_done")
        var_done = sem("var_done")
        eps_added = sem("eps_added")
        rdev_done = sem("rdev_done")
        spread = sem("spread")
        rstd_done = sem("rstd_done")
        xn_done = sem("xn_done")
        xg_done = sem("xg_done")
        gates_done = sem("gates_done")
        gate_stored = sem("gate_stored")
        gelu_done = sem("gelu_done")
        a_done = sem("a_done")
        hid_done = sem("hid_done")
        hid2_done = sem("hid2_done")
        w2_done = sem("w2_done")
        y_ready = sem("y_ready")
        y_centred = sem("y_centred")
        y_sq = sem("y_sq")
        y_var = sem("y_var")
        y_eps = sem("y_eps")
        y_rdev = sem("y_rdev")
        y_spread = sem("y_spread")
        y_rstd = sem("y_rstd")
        y_normed = sem("y_normed")
        y_turned = sem("y_turned")
        y_out = sem("y_out")

        def bank1(s, j):
            return (psS, psT)[s % 2][j]

        def use_s(s):
            return s + 2 * (s > 3)

        CORNER_USE = 4

        def chunk_of(g, k):
            return 4 * (g // 2) + g % 2 + 2 * k

        def head_of(g, j):
            return 2 * PER_GROUP * (g // 2) + 2 * j + g % 2

        def table(layer, tile, which):
            return bass.ds(((layer * TILES + tile) * 4 + which) * HEAD, HEAD)

        def layer_of(n):
            if isinstance(n, int):
                return n // BATCHES
            return nc.s_assert_within(n >> 3, 0, LAYERS - 1, skip_runtime_bounds_check_because="a unit's number is under UNITS")

        def slot(u, first=0, count=TOKENS):
            return bass.ds((u & (RING - 1)) * TOKENS + first, count)

        def heads8(ap):
            return ap.rearrange("p (h d) -> p h d", d=HEAD)

        block = ctx.enter_context(nc.Block())

        @block.sync
        def _(sp):
            sp.dma_start(ident[:, :], ident_d).then_inc(ident_in, 16)
            sp.dma_start(raw[0], q_w.rearrange("(c a) p d -> (a p) c d", a=2)).then_inc(raw_in[0], 16)
            sp.dma_start(xraw[:, :, :], x.rearrange("b (t p) d -> p (b t) d", p=PARTS)).then_inc(x_in, 16)
            sp.dma_start(raw[1], k_w.rearrange("(c a) p d -> (a p) c d", a=2)).then_inc(raw_in[1], 16)
            sp.dma_start(raw[2], v_w.rearrange("(c a) p d -> (a p) c d", a=2)).then_inc(raw_in[2], 16)
            sp.dma_start(raw[3], l_w.rearrange("o (c p) -> o c p", p=PARTS)).then_inc(raw_in[3], 16)
            sp.wait_ge(cleared, 1)
            for at, src in ((QB, q_b.rearrange("(c a) o p -> c (a o p)", a=2)), (KB, k_b.rearrange("(c a) o p -> c (a o p)", a=2)),
                            (LB, l_b), (LNG, ln_g), (LNB, ln_b), (B2, b2)):
                sp.dma_start(rows[at:at + src.shape[0], :], src).then_inc(param_in, 16)
            for c, (off, m) in enumerate(FF_CHUNKS):
                for k in range(2):
                    at = B1 + (3 * k + c) * LAYERS
                    sp.dma_start(rows[at:at + LAYERS, 0:m], b1[:, k * FF + off:k * FF + off + m]).then_inc(param_in, 16)
            sp.dma_start(vb[:, :], v_b.rearrange("h o p -> (o h p)").partition_broadcast(PARTS)).then_inc(bias_in, 16)
            for dst, src in ((mean, mean_d), (centre, centre_d), (band, band_d), (corner, corner_d), (rotary, rotary_d)):
                sp.dma_start(dst[:, :], src).then_inc(const_in, 16)
            for j, src in enumerate((q_scale, q_scale, k_scale, k_scale)):
                if j % 2 == 0:
                    sp.dma_start(scales[:, :, j, :], src.partition_broadcast(PARTS)).then_inc(scale_in, 16)
                    continue
                h = HEAD // 2
                sp.dma_start(scales[:, :, j, 0:h], src[:, h:HEAD].partition_broadcast(PARTS)).then_inc(scale_in, 16)
                sp.dma_start(scales[:, :, j, h:HEAD], src[:, 0:h].partition_broadcast(PARTS)).then_inc(scale_in, 16)

            def load_wqkv(layer):
                sp.dma_start(wqkv[:, bass.ds((layer & 1) * (3 * INNER), 3 * INNER)], Wqkv[bass.ds(layer, 1)].rearrange("o d n -> d (o n)")).then_inc(wqkv_in, 16)

            def load_wo(layer):
                heads = Wo[bass.ds(layer, 1)].rearrange("o (g a r p) d -> a p (o g) r d", g=GROUPS, a=2, r=2)
                for k in range(2):
                    for r in range(2):
                        sp.dma_start(wo[64 * k:64 * k + 64, r:PAIRS:2, :], heads[k][:, :, r, :]).then_inc(wo_in, 16)

            def load_w1(layer):
                sp.dma_start(w1[:, :], W1[bass.ds(layer, 1)].rearrange("o d n -> d (o n)")).then_inc(w1_in, 16)

            def load_w2(layer):
                sp.dma_start(w2[:, 0:2, :], W2[bass.ds(layer, 1), 0:256, :].rearrange("o (c p) d -> p (o c) d", p=PARTS)).then_inc(w2_in, 16)
                sp.dma_start(w2[0:FF - 256, 2, :], W2[bass.ds(layer, 1), 256:FF, :].rearrange("o p d -> p (o d)")).then_inc(w2_in, 16)

            load_wqkv(0)
            load_wo(0)
            load_w1(0)
            load_w2(0)

            def corner_values(u):
                sp.wait_ge(v_stored, 4 * u + 2)
                sp.sem_inc(sp_passed, 1)
                need(sp, pv_done, 8 * u - 3)
                sp.sem_inc(sp_passed, 1)
                sp.dma_start(Vc[:, bass.ds(u & 1, 1)], V[PARTS - WINDOW:PARTS, bass.ds(u & 1, 1), 0]).then_inc(vc_in, 16)

            corner_values(0)
            sp.wait_ge(proj_done, 12)
            load_wqkv(1)
            corner_values(1)
            with sp.Fori(2, 9) as u:
                corner_values(u)

            def next_layer(layer, units, two_ahead):
                sp.wait_ge(wo_done, layer * BATCHES)
                sp.sem_inc(sp_passed, 1)
                load_wo(layer)
                if two_ahead:
                    sp.wait_ge(proj_done, layer * (BATCHES * 12) + 12)
                    sp.sem_inc(sp_passed, 1)
                    load_wqkv(layer + 1)
                corner_values(layer * BATCHES + 1)
                sp.wait_ge(a_done, layer * BATCHES)
                sp.sem_inc(sp_passed, 1)
                load_w1(layer)
                sp.wait_ge(w2_done, layer * BATCHES)
                sp.sem_inc(sp_passed, 1)
                load_w2(layer)
                with sp.Fori(2, 2 + units) as k:
                    corner_values(layer * BATCHES + k)

            with sp.Fori(1, LAYERS - 1) as layer:
                next_layer(layer, 7, True)
            next_layer(LAYERS - 1, 6, False)

            for k in range(4):
                sp.wait_ge(y_out, k + 1)
                sp.dma_start(out.rearrange("b (t p) d -> p (b t) d", p=PARTS)[:, 4 * k:4 * k + 4, :],
                             yo[k].rearrange("p (t d) -> p t d", d=DIM)).then_inc(stored[k], 16)
            for k in range(4):
                sp.wait_ge(stored[k], 16)

        @block.gpsimd
        def _(pool):
            nc.gpsimd.memset(rows[:, :], 0.0).then_inc(cleared, 1)
            pool.wait_ge(const_in, 16 * 5)
            pool.wait_ge(scale_in, 16 * 6)
            rot = rotary[:, :].rearrange("p (t n) -> p t n", t=TILES)
            tab = tables[:, :].rearrange("p (l t n) -> p l t n", l=LAYERS, t=TILES)
            for layer in range(LAYERS):
                for tile in range(TILES):
                    nc.gpsimd.tensor_tensor(tab[:, layer, tile, :], rot[:, tile, :],
                                            scales[:, layer].rearrange("p a d -> p (a d)"), ALU.mult).then_inc(tables_ready, 1)

            def rsqrt(dst, src, t):
                pool.sem_inc(pool_passed, 1)
                nc.gpsimd.tensor_scalar(dst.bitcast(I32), src.bitcast(I32), -0.5, float(RSQRT_BITS), ALU.mult, ALU.add)
                for _ in range(3):
                    pool.drain()
                    nc.gpsimd.tensor_tensor(t, dst, dst, ALU.mult)
                    pool.drain()
                    nc.gpsimd.tensor_tensor(t, t, src, ALU.mult)
                    pool.drain()
                    nc.gpsimd.tensor_scalar(t, t, -0.5, 1.5, ALU.mult, ALU.add)
                    pool.drain()
                    last = nc.gpsimd.tensor_tensor(dst, dst, t, ALU.mult)
                return last

            def first_slot(a, b, c, s):
                if c.live and s == 4:
                    pool.wait_ge(eps1, c.n + 1)
                    rsqrt(rdev[:, 0:2], var[:, 0:2], guess[0][:, 0:2]).then_inc(rdev1, 1)


            def slot_of(a, b, c, s):
                if a.live and s % 2:
                    k, joint = (s // 2) % 2, c.live and s == 5
                    if joint:
                        pool.wait_ge(eps_added, c.n + 1)
                        pool.sem_inc(pool_passed, 1)
                        need(pool, spread, c.n)
                        pool.sem_inc(pool_passed, 1)
                    n = HEADS + TILES if joint else HEADS
                    pool.wait_ge(guarded, 4 * a.n + s // 2 + 1)
                    last = rsqrt(rn[k][:, 0:n], n2[k][:, 0:n], guess[1][:, 0:n])
                    if joint:
                        last.then_inc(rdev_done, 1)
                elif c.live and s == 5:
                    pool.wait_ge(eps_added, c.n + 1)
                    need(pool, spread, c.n)
                    rsqrt(rdev[:, 0:2], var[:, 0:2], guess[0][:, 0:2]).then_inc(rdev_done, 1)
                if a.live:
                    pool.wait_ge(sin_done, 8 * a.n + s + 1)
                    nc.gpsimd.tensor_tensor(qs[s % 4][:, :], qs[s % 4][:, :], qc[s % 2][:, :], ALU.add).then_inc(added, 1)
                if a.live and s % 2:
                    pool.drain()
                    for j in range(2):
                        t = qs[(s - 1 + j) % 4]
                        nc.gpsimd.tensor_tensor(heads8(t[:, :]), heads8(t[:, :]), rn[k][:, 8 * j:8 * j + 8].unsqueeze(2).to_broadcast([PARTS, 8, HEAD]),
                                                ALU.mult).then_inc(rotated, 1)

            over_units(pool, first_slot, BATCHES, 2, BATCHES - 2, -1, BATCHES)
            pool.wait_ge(tables_ready, LAYERS * TILES)
            change_over(first_slot, slot_of)
            over_units(pool, slot_of, UNITS, FIRST, LAST, 0, UNITS + 2)

            pool.wait_ge(y_eps, 1)
            rsqrt(rdev[:, :], var[:, :], guess[0][:, 0:16]).then_inc(y_rdev, 1)

        @block.tensor
        def _(pe):
            pe.wait_ge(ident_in, 16)
            for n in range(12):
                if n < 4:
                    pe.wait_ge(x_in, 16)
                elif n % 2 == 0:
                    pe.wait_ge(raw_in[(n - 4) // 2], 16)
                need(pe, turned_out, n - 1)
                for j in range(4):
                    src = xraw[:, 4 * n + j, :] if n < 4 else raw[(n - 4) // 2][:, 4 * (n % 2) + j, :]
                    mm = nc.tensor.transpose(psT[n % 2][:, 128 * j:128 * j + 128], src, ident[:, :])
                mm.then_inc(turned, 1)
            pe.wait_ge(param_in, 16 * 12)
            pe.wait_ge(turned_out, 11)
            nc.tensor.transpose(psT[0][:, 0:128], rows[:, :], ident[:, :]).then_inc(turned, 1)
            pe.wait_ge(turned_out, 13)

            def variances(bank, at, tiles, squares=csq):
                for t in range(tiles):
                    mm = nc.tensor.matmul(bank[:, at + t:at + t + 1], squares[:, 128 * t:128 * t + 128], mean[:, 0:1], start=True, stop=True)
                return mm

            def spread_out(bank, at, tiles, first=0, rdev=rdev):
                for t in range(tiles):
                    mm = nc.tensor.matmul(bank[:, at + 128 * t:at + 128 * t + 128], rdev[:, first + t:first + t + 1].to_broadcast([PARTS, PARTS]), ident[:, :], start=True, stop=True)
                return mm

            def first_slot(a, b, c, s):
                if b.live:
                    for j in range(2):
                        need(pe, exp1, 4 * (8 * b.n + s - 2) + 2 * j + 2)
                        if j == 0:
                            pe.wait_ge(qk1_stored, 8 * b.n + s + 1)
                        for t in range(2):
                            mm = nc.tensor.matmul(bank1(s, j)[:, 256 * t:256 * t + 256], kT[b.par][64 * j:64 * j + 64, s, 128 * t:128 * t + 128],
                                                  qT[b.par][64 * j:64 * j + 64, s, :], start=True, stop=True)
                        mm.then_inc(score1, 1)
                if a.live:
                    if s == 0:
                        pe.wait_ge(xs1_ready, a.n + 1)
                    need(pe, qk1_stored, 8 * a.n + s)
                    nc.tensor.matmul(psA[0][:, 0:256], wT[:, 0, 128 * s:128 * s + 128], xs1[a.par][:, :], start=True, stop=True)
                    nc.tensor.matmul(psA[0][:, 256:512], wT[:, 1, 128 * s:128 * s + 128], xs1[a.par][:, :], start=True, stop=True).then_inc(proj1, 1)
                ub, sb_ = lag(b, s, 1)
                if ub.live:
                    need(pe, ctx1, 8 * ub.n + sb_)
                    for j in range(2):
                        pe.wait_ge(vs1, 2 * (8 * ub.n + sb_) + j + 1)
                        e = (sb_ % 2) * 2 + j
                        for t in range(2):
                            mm = nc.tensor.matmul(psX[64 * j:64 * j + 64, 0:256], Vs[e][:, t, :], E[e][:, 256 * t:256 * t + 256], start=t == 0, stop=t == 1)
                        mm.then_inc(pv1, 1)
                if a.live and s % 2:
                    w = s // 2
                    need(pe, v1_stored, 4 * a.n + w)
                    nc.tensor.matmul(psA[1][:, :], xs1[a.par][:, 128 * (w // 2):128 * (w // 2) + 128], wT[:, 2, 512 * (w % 2):512 * (w % 2) + 512],
                                     start=True, stop=True).then_inc(proj1, 1)
                if c.live and s == 1:
                    pe.wait_ge(ctx1, 8 * c.n + 8)
                    need(pe, x_written, c.n)
                    for h in range(PAIRS):
                        mm = nc.tensor.matmul(psC[:, 0:256], wT[:, 3, 128 * h:128 * h + 128], cT[c.par][:, h, :], start=h == 0, stop=h == PAIRS - 1)
                    mm.then_inc(wl_done, 1)
                if c.live and s == 2:
                    pe.wait_ge(resid1, c.n + 1)
                    nc.tensor.matmul(psC[:, 0:256], centre[:, :], xr[c.par][:, :], start=True, stop=True).then_inc(centred1, 1)
                if c.live and s == 3:
                    pe.wait_ge(csq1, c.n + 1)
                    variances(psC, 256, 2).then_inc(var1, 1)
                if c.live and s == 5:
                    pe.wait_ge(rdev1, c.n + 1)
                    spread_out(psC, 256, 2).then_inc(spread1, 1)


            def free_scores(b, k):
                u, k = (b.n, k - 2) if k >= 2 else (b.n - 1, k + 8)
                if CORNER_USE <= k < CORNER_USE + 2:
                    need(pe, corner_stored, 2 * u + k - CORNER_USE + 1)
                else:
                    need(pe, exped, 8 * u + (k if k < CORNER_USE else k - 2) + 1)

            def free_turn(kinds):
                for s_, unit, slot in kinds:
                    if unit.live:
                        need(pe, s_, 8 * unit.n + slot + 1)

            def slot_of(a, b, c, s):
                ap1, sa1 = lag(a, s, 4)
                apa, sa = lag(a, s, 3)
                bp2, sb2 = lag(b, s, 2)
                bp3, sb3 = lag(b, s, 3)
                bp4, sb4 = lag(b, s, 4)
                def turn_weights():
                    pe.wait_ge(weighted, 8 * bp2.n + sb2 + 1)
                    free_turn([(a_stored, ap1, sa1)] + ([(p_stored, bp4, sb4)] if b.static else []))
                    for j in range(PER_GROUP):
                        mm = nc.tensor.transpose(psT[s % 2][:, 128 * j:128 * j + 128], E[sb2 % 4][:, 128 * j:128 * j + 128], ident[:, :])
                    mm.then_inc(p_turned, 1)

                if b.live and s == 4:
                    pe.wait_ge(a_stored, 8 * b.n + 8)
                    for r in range(2):
                        free_scores(b, CORNER_USE + r)
                        nc.tensor.matmul(psS[r][0:WINDOW, 0:256], ident_h[:, 0:WINDOW], corner_h[:, :, :].rearrange("p h k -> p (h k)"),
                                         start=True, stop=False, skip_group_check=True)
                        for h in range(PAIRS):
                            mm = nc.tensor.matmul(psS[r][0:WINDOW, WINDOW * h:WINDOW * h + WINDOW], qT[b.par][64 * r:64 * r + 64, h, PARTS:PARTS + WINDOW],
                                                  kT[b.par][64 * r:64 * r + 64, h, PARTS - WINDOW:PARTS], start=False, stop=h == PAIRS - 1, skip_group_check=True)
                        mm.then_inc(scored, 1)
                if bp2.live and s == 4:
                    turn_weights()
                if b.live:
                    tile, g = s // 4, s % 4
                    k = use_s(s) % 2
                    free_scores(b, use_s(s))
                    if s < 4:
                        pe.wait_ge(a_stored, 8 * b.n + (2 if g < 2 else 4))
                    nc.tensor.matmul(psS[k][:, :], ident_h[:, :], band_h[:, :, :].rearrange("p h k -> p (h k)"), start=True, stop=False, skip_group_check=True)
                    for j in range(PER_GROUP):
                        h = head_of(g, j)
                        r = 64 * (h % 2)
                        mm = nc.tensor.matmul(psS[k][:, 128 * j:128 * j + 128], qT[b.par][r:r + 64, h // 2, 128 * tile:128 * tile + 128],
                                              kT[b.par][r:r + 64, h // 2, 128 * tile:128 * tile + 128], start=False, stop=j == PER_GROUP - 1, skip_group_check=True)
                    mm.then_inc(scored, 1)
                if bp2.live and s != 4:
                    turn_weights()
                c1 = c.back()
                if c1.live and s == 0:
                    pe.wait_ge(xg_done, c1.n + 1)
                    pe.wait_ge(w1_in, (layer_of(c1.n) + 1) * 16)
                    for k in range(2):
                        mm = nc.tensor.matmul(psC[:, 256 * k:256 * k + 256], w1[:, FF + 128 * k:FF + 128 * k + 128], xg[:, :], start=True, stop=True)
                    mm.then_inc(gates_done, 1)
                if c.live and s == 7:
                    pe.wait_ge(rdev_done, c.n + 1)
                    spread_out(psC, 256, 2, 0, rn[0][:, HEADS:HEADS + TILES] if a.live else rdev).then_inc(spread, 1)
                if a.live:
                    tile, half, which = s // 4, (s // 2) % 2, s % 2
                    if s == 0:
                        pe.wait_ge(xs_ready, a.n + 1)
                        pe.wait_ge(wqkv_in, (layer_of(a.n) + 1) * 16)
                    need(pe, sin_done, 8 * a.n + s)
                    nc.tensor.matmul(psA[0][:, :], xs[a.par][:, 128 * tile:128 * tile + 128],
                                     wqkv[:, bass.ds((layer_of(a.n) & 1) * (3 * INNER) + which * INNER + half * 512, 512)],
                                     start=True, stop=True).then_inc(proj_done, 1)
                if c.live and s == 5:
                    pe.wait_ge(csq_done, c.n + 1)
                    variances(psC, 256, 2).then_inc(var_done, 1)
                if a.live and s % 2:
                    w = s // 2
                    need(pe, v_stored, 4 * a.n + w)
                    if c1.live and w == 0:
                        pe.wait_ge(gate_stored, 2 * c1.n + 2)
                    if c1.live and w == 1:
                        pe.wait_ge(x_written, c1.n + BATCHES + 1)
                    nc.tensor.matmul(psA[1][:, :], xs[a.par][:, 128 * (w // 2):128 * (w // 2) + 128],
                                     wqkv[:, bass.ds((layer_of(a.n) & 1) * (3 * INNER) + 2 * INNER + (w % 2) * 512, 512)],
                                     start=True, stop=True).then_inc(proj_done, 1)
                if apa.live:
                    apx, sax = lag(a, s, 5)
                    pe.wait_ge(rotated, 8 * apa.n + sa + 1)
                    free_turn([(p_stored, bp3, sb3)] + ([(a_stored, apx, sax)] if b.static else []))
                    for j in range(4):
                        mm = nc.tensor.transpose(psT[(s + 1) % 2][:, 128 * j:128 * j + 128], qs[sa % 4][:, 128 * j:128 * j + 128], ident[:, :])
                    mm.then_inc(a_turned, 1)
                if bp2.live:
                    tile, g = sb2 // 4, sb2 % 4
                    pe.wait_ge(p_stored, 8 * bp2.n + sb2 + 1)
                    need(pe, ctx_stored, 8 * bp2.n + sb2)
                    pe.wait_ge(v_stored, 4 * bp2.n + 2 * tile + 2)
                    if tile == 1:
                        pe.wait_ge(corner_turned, 4 * bp2.n + g + 1)
                        pe.wait_ge(vc_in, (bp2.n + 1) * 16)
                    for j in range(PER_GROUP):
                        half, at = 64 * (j % 2), PARTS * (j // 2)
                        mm = nc.tensor.matmul(psX[half:half + 64, at:at + PARTS], V[:, bp2.par, tile, head_of(g, j), :], PT[sb2 % 2][:, 128 * j:128 * j + 128],
                                              start=True, stop=tile == 0, skip_group_check=True)
                        if tile == 1:
                            mm = nc.tensor.matmul(psX[half:half + 64, at:at + WINDOW], Vc[:, bp2.par, head_of(g, j), :], PcT[sb2 % 2][:, 32 * j:32 * j + 32],
                                                  start=False, stop=True, skip_group_check=True)
                    mm.then_inc(pv_done, 1)
                feed_forward(a, c, c.back(), s)

            def feed_forward(a, c, c1, s):
                if c1.live and s == 0:
                    off, m = FF_CHUNKS[2]
                    need(pe, v_stored, 4 * a.n if not a.static else 4 * min(a.n, UNITS))
                    nc.tensor.matmul(psA[1][0:m, 0:256], w1[:, FF + off:FF + off + m], xg[:, :], start=True, stop=True)
                    nc.tensor.matmul(psA[1][0:m, 256:512], w1[:, off:off + m], xg[:, :], start=True, stop=True).then_inc(gates_done, 1)
                if c1.live and s == 1:
                    pe.wait_ge(gate_stored, 2 * c1.n + 1)
                    for k in range(2):
                        mm = nc.tensor.matmul(psC[:, 256 * k:256 * k + 256], w1[:, 128 * k:128 * k + 128], xg[:, :], start=True, stop=True)
                    mm.then_inc(a_done, 1)
                if c1.live and s == 2:
                    pe.wait_ge(hid_done, 2 * c1.n + 2)
                    pe.wait_ge(hid2_done, c1.n + 1)
                    pe.wait_ge(w2_in, (layer_of(c1.n) + 1) * 32)
                    if a.live:
                        pe.wait_ge(v_stored, 4 * a.n + 1)
                    for k, (off, m) in enumerate(FF_CHUNKS):
                        mm = nc.tensor.matmul(psA[1][:, 0:256], w2[0:m, k, :], hid[0:m, k, :], start=k == 0, stop=k == 2)
                    mm.then_inc(w2_done, 1)
                if not c.live:
                    return
                if s == 2:
                    pe.wait_ge(ctx_stored, 8 * c.n + 8)
                    pe.wait_ge(wo_in, (layer_of(c.n) + 1) * 64)
                    need(pe, hid_done, 2 * c.n)
                if s == 2 or s == 3:
                    for h in range(4 * (s - 2), 4 * (s - 2) + 4):
                        mm = nc.tensor.matmul(psC[:, 0:256], wo[:, h, :], cT[c.par][:, h, :], start=h == 0, stop=h == PAIRS - 1)
                if s == 3:
                    mm.then_inc(wo_done, 1)
                if s == 4:
                    pe.wait_ge(xsh_ready, c.n + 1)
                    nc.tensor.matmul(psC[:, 0:256], centre[:, :], xsh[c.par][:, :], start=True, stop=True).then_inc(centred, 1)

            pe.wait_ge(const_in, 16 * 5)
            over_units(pe, first_slot, BATCHES, 2, BATCHES - 2, -1, BATCHES)
            pe.wait_ge(qk1_stored, BATCHES * 8)
            pe.wait_ge(v1_stored, BATCHES * 4)
            pe.wait_ge(exp1, BATCHES * 32)
            pe.wait_ge(halves_ready, 7)
            change_over(first_slot, slot_of)
            pe.wait_ge(x_written, BATCHES)
            over_units(pe, slot_of, UNITS, FIRST, LAST, 0, UNITS + 2)

            for k in range(4):
                pe.wait_ge(y_ready, k + 1)
                nc.tensor.matmul(centred_y[k][:, :], centre[:, :], y[k], start=True, stop=True).then_inc(y_centred, 1)
            for k in range(4):
                pe.wait_ge(y_sq, k + 1)
                variances(psC, 4 * k, 4, y_squares[k]).then_inc(y_var, 1)
            pe.wait_ge(y_rdev, 1)
            for k in range(4):
                spread_out(spread_y[k], 0, 4, 4 * k).then_inc(y_spread, 1)
            for k in range(4):
                pe.wait_ge(y_normed, k + 1)
                for j in range(4):
                    mm = nc.tensor.transpose(centred_y[k][:, 128 * j:128 * j + 128], yn[k][:, 128 * j:128 * j + 128], ident[:, :])
                mm.then_inc(y_turned, 1)

        @block.scalar
        def _(act):
            for n in range(12):
                act.wait_ge(turned, n + 1)
                dst = X[:, BATCHES * TOKENS + 512 * n:BATCHES * TOKENS + 512 * n + 512] if n < 4 else wT[:, (n - 4) // 2, 512 * (n % 2):512 * (n % 2) + 512]
                nc.scalar.copy(dst, psT[n % 2][:, :]).then_inc(turned_out, 1)

            act.wait_ge(turned, 13)
            nc.scalar.copy(cols[:, :], psT[0][:, 0:128]).then_inc(turned_out, 1)
            act.wait_ge(turned_out, 13)

            def first_slot(a, b, c, s):
                if a.live:
                    act.wait_ge(proj1, 12 * a.n + s + s // 2 + 1)
                    need(act, score1, 2 * (8 * (a.n - 2) + s) + 2)
                    nc.scalar.activation(qT[a.par][:, s, :], psA[0][:, 0:256], ACT.Identity, bias=qb[:, s:s + 1])
                    nc.scalar.activation(kT[a.par][:, s, :], psA[0][:, 256:512], ACT.Identity, bias=kb[:, s:s + 1]).then_inc(qk1_stored, 1)
                ub, sb_ = lag(b, s, 1)
                if ub.live and ub is not b or (ub.live and s):
                    act.wait_ge(pv1, 2 * (8 * ub.n + sb_) + 2)
                    need(act, wl_done, ub.n - 1)
                    nc.scalar.copy(cT[ub.par][:, sb_, :], psX[:, 0:256]).then_inc(ctx1, 1)
                if b.live:
                    for j in range(2):
                        e = (s % 2) * 2 + j
                        act.wait_ge(nm1, 2 * (8 * b.n + s) + j + 1)
                        need(act, pv1, 2 * (8 * b.n + s - 2) + j + 1)
                        for t in range(2):
                            nc.scalar.activation(E[e][:, 256 * t:256 * t + 256], bank1(s, j)[:, 256 * t:256 * t + 256], ACT.Exp, bias=nm[e][:, t:t + 1],
                                                 scale=HEAD ** -0.5, accum_out=sums[e][:, t:t + 1]).then_inc(exp1, 1)
                if c.live and s == 2:
                    act.wait_ge(centred1, c.n + 1)
                    need(act, var1, c.n)
                    nc.scalar.activation(csq[:, 0:256], psC[:, 0:256], ACT.Square).then_inc(csq1, 1)
                if c.live and s == 6:
                    act.wait_ge(spread1, c.n + 1)
                    need(act, x_written, c.n)
                    nc.scalar.copy(rstd[:, 0:256], psC[:, 256:512]).then_inc(rstd1, 1)


            def feed_forward(c, c1, s):
                if c1.live and s == 1:
                    m = FF_CHUNKS[2][1]
                    act.wait_ge(gates_done, 2 * c1.n + 2)
                    act.sem_inc(act_passed, 1)
                    need(act, w2_done, c1.n)
                    act.sem_inc(act_passed, 1)
                    nc.scalar.activation(gate[0:m, 2, :], psA[1][0:m, 0:256], ACT.Identity, bias=cols[0:m, bass.ds(layer_of(c1.n) + B1 + 5 * LAYERS, 1)])
                    nc.scalar.activation(hid[0:m, 2, :], psA[1][0:m, 256:512], ACT.Identity, bias=cols[0:m, bass.ds(layer_of(c1.n) + B1 + 2 * LAYERS, 1)]).then_inc(gate_stored, 1)
            def slot_of(a, b, c, s):
                feed_forward(c, c.back(), s)
                if b.live and s == 4:
                    need(act, corner_shifted, 4 * b.n)
                    for r in range(2):
                        act.wait_ge(corner_maxed, 2 * b.n + r + 1)
                        nc.scalar.copy(Sc[:, PAIRS * r:PAIRS * r + PAIRS, :].rearrange("p h k -> p (h k)"), psS[r][0:WINDOW, 0:256]).then_inc(corner_stored, 1)
                if c.live and s == 4:
                    act.wait_ge(resid, c.n + 1)
                    nc.scalar.copy(xsh[c.par][0:64, :], xr[c.par][0:64, :])
                    nc.scalar.copy(xsh[c.par][64:128, 1:TOKENS], xr[c.par][64:128, 0:TOKENS - 1]).then_inc(xsh_ready, 1)
                bp2, sb2 = lag(b, s, 2)
                if bp2.live:
                    act.wait_ge(p_turned, 8 * bp2.n + sb2 + 1)
                    need(act, pv_done, 8 * bp2.n + sb2 - 1)
                    nc.scalar.copy(PT[sb2 % 2][:, :], psT[s % 2][:, :]).then_inc(p_stored, 1)
                if a.live:
                    act.wait_ge(proj_done, 12 * a.n + s + s // 2 + 1)
                    need(act, summed, 8 * a.n + s - 1)
                    nc.scalar.activation(sq[s % 2][:, :], psA[0][:, :], ACT.Square).then_inc(squared, 1)
                apa, sa = lag(a, s, 3)

                def store_turned():
                    tile, half, which = sa // 4, (sa // 2) % 2, sa % 2
                    act.wait_ge(a_turned, 8 * apa.n + sa + 1)
                    need(act, scored, 10 * (apa.n - 1))
                    dst = (kT if which else qT)[apa.par]
                    nc.scalar.copy(dst[:, 4 * half:4 * half + 4, 128 * tile:128 * tile + 128],
                                   psT[(s + 1) % 2][:, :].rearrange("p (c t) -> p c t", c=4)).then_inc(a_stored, 1)

                if apa.live and s % 2 == 0:
                    store_turned()
                c1 = c.back()
                if c1.live and s == 0:
                    act.wait_ge(gates_done, 2 * c1.n + 1)
                    act.sem_inc(act_passed, 1)
                    need(act, hid_done, 2 * c1.n)
                    act.sem_inc(act_passed, 1)
                    for k in range(2):
                        ins = nc.scalar.activation(gate[:, k, :], psC[:, 256 * k:256 * k + 256], ACT.Identity, bias=cols[:, bass.ds(layer_of(c1.n) + B1 + (3 + k) * LAYERS, 1)])
                    ins.then_inc(gate_stored, 1)
                if c.live and s == 7:
                    act.wait_ge(spread, c.n + 1)
                    need(act, xn_done, c.n)
                    nc.scalar.copy(rstd[:, 0:256], psC[:, 256:512]).then_inc(rstd_done, 1)
                if b.live:
                    k = use_s(s) % 2
                    act.wait_ge(maxed, 12 * b.n + s + 1 + max(s - 3, 0))
                    for j in range(PER_GROUP):
                        ins = nc.scalar.activation(E[s % 4][:, 128 * j:128 * j + 128], psS[k][:, 128 * j:128 * j + 128], ACT.Exp, bias=mx[s % 2][:, j:j + 1],
                                                   accum_out=sums[s % 4][:, j:j + 1])
                    ins.then_inc(exped, 1)
                    if s >= 4:
                        act.wait_ge(corner_shifted, 4 * b.n + s - 3)
                        nc.scalar.activation(Ec[s % 2][:, :], Ec[s % 2][:, :], ACT.Exp).then_inc(corner_exped, 1)
                if a.live and s % 2:
                    w = s // 2
                    act.wait_ge(proj_done, 12 * a.n + 3 * w + 3)
                    need(act, pv_done, 8 * (a.n - 1))
                    nc.scalar.copy(V[:, a.par, w // 2, 8 * (w % 2):8 * (w % 2) + 8, 0:HEAD], heads8(psA[1][:, :])).then_inc(v_stored, 1)
                if apa.live and s % 2:
                    store_turned()
                if c.live and s == 4:
                    act.wait_ge(centred, c.n + 1)
                    need(act, var_done, c.n)
                    nc.scalar.activation(csq[:, 0:256], psC[:, 0:256], ACT.Square).then_inc(csq_done, 1)
                if bp2.live:
                    tile, g = sb2 // 4, sb2 % 4
                    act.wait_ge(pv_done, 8 * bp2.n + sb2 + 1)
                    need(act, wo_done, bp2.n - 1)
                    nc.scalar.copy(cT[bp2.par][:, chunk_of(g, 0):chunk_of(g, 1) + 1:2, 128 * tile:128 * tile + 128],
                                   psX[:, 0:256].rearrange("p (c t) -> p c t", c=2)).then_inc(ctx_stored, 1)
                c1 = c.back()
                if c1.live and s == 1:
                    m = FF_CHUNKS[2][1]
                    act.wait_ge(gate_stored, 2 * c1.n + 2)
                    nc.scalar.activation(gate[0:m, 2, :], gate[0:m, 2, :], ACT.Gelu).then_inc(gelu_done, 1)
                    nc.scalar.activation(gate[:, 0:2, :], gate[:, 0:2, :], ACT.Gelu).then_inc(gelu_done, 1)

            over_units(act, first_slot, BATCHES, 2, BATCHES - 2, -1, BATCHES)
            act.wait_ge(proj1, BATCHES * 12)
            act.wait_ge(score1, (BATCHES - 1) * 16)
            act.wait_ge(vs1, (BATCHES - 1) * 16)
            change_over(first_slot, slot_of)
            act.wait_ge(x_written, BATCHES)
            nc.scalar.copy(x1[:, :], X[:, 0:BATCHES * TOKENS]).then_inc(x1_kept, 1)
            over_units(act, slot_of, UNITS, FIRST, LAST, 0, UNITS + 2)

            for k in range(4):
                act.wait_ge(y_centred, k + 1)
                nc.scalar.activation(y_squares[k], centred_y[k][:, :], ACT.Square).then_inc(y_sq, 1)
            for k in range(4):
                act.wait_ge(y_spread, k + 1)
                nc.scalar.copy(y_dev[k], spread_y[k][:, :]).then_inc(y_rstd, 1)
            for k in range(4):
                act.wait_ge(y_turned, k + 1)
                nc.scalar.copy(yo[k], centred_y[k][:, :]).then_inc(y_out, 1)

        @block.vector
        def _(dve):
            dve.wait_ge(ident_in, 16)
            dve.wait_ge(const_in, 16 * 5)
            nc.vector.tensor_copy(ident_h[:, :], ident[:, :]).then_inc(halves_ready, 1)
            nc.vector.tensor_copy(band_h[:, :, :], band[:, :].unsqueeze(1).to_broadcast([PARTS, PER_GROUP, PARTS])).then_inc(halves_ready, 1)
            nc.vector.tensor_copy(corner_h[:, :, :], corner[:, :].unsqueeze(1).to_broadcast([PARTS, PAIRS, WINDOW])).then_inc(halves_ready, 1)

            for t in (xs[0], xs[1], xsh[0], xsh[1]):
                nc.vector.memset(t[64:128, 0:1], 0.0).then_inc(halves_ready, 1)

            def first_input(u, par):
                need(dve, proj1, 12 * (u - 1))
                nc.vector.tensor_copy(xs1[par][:, :], X[:, slot(u + BATCHES)]).then_inc(xs1_ready, 1)

            def first_slot(a, b, c, s):
                if c.live and s == 2:
                    dve.wait_ge(wl_done, c.n + 1)
                    nc.vector.scalar_tensor_tensor(out=xr[c.par][:, :], in0=psC[:, 0:256], scalar=lb[:, :], in1=X[:, slot(c.n + BATCHES)],
                                                   op0=ALU.add, op1=ALU.add).then_inc(resid1, 1)
                if c.live and s == 4:
                    dve.wait_ge(var1, c.n + 1)
                    nc.vector.tensor_scalar(var[:, 0:2], psC[:, 256:258], EPS, None, ALU.add).then_inc(eps1, 1)
                if c.live and s == 7:
                    dve.wait_ge(rstd1, c.n + 1)
                    nc.vector.tensor_tensor(X[:, slot(c.n)], psC[:, 0:256], rstd[:, 0:256], ALU.mult).then_inc(x_written, 1)
                if b.live:
                    for j in range(2):
                        i = 2 * (8 * b.n + s) + j
                        dve.wait_ge(score1, i + 1)
                        nc.vector.tensor_reduce(mx[j][:, 0:2], bank1(s, j)[:, :].rearrange("p (t q) -> p t q", t=2), AX.X, ALU.max).then_inc(max1, 1)
                        dve.wait_ge(max1, i + 1)
                        need(dve, exp1, 4 * (8 * b.n + s - 2) + 2 * j + 2)
                        nc.vector.tensor_scalar(nm[2 * (s % 2) + j][:, 0:2], mx[j][:, 0:2], -(HEAD ** -0.5), None, ALU.mult).then_inc(nm1, 1)
                if a.live and s % 2:
                    w = s // 2
                    dve.wait_ge(proj1, 12 * a.n + 3 * w + 3)
                    dve.wait_ge(bias_in, 16)
                    nc.vector.tensor_tensor(V[:, a.par, w // 2, 8 * (w % 2):8 * (w % 2) + 8, 0:HEAD], heads8(psA[1][:, :]),
                                            heads8(vb[:, 512 * (w % 2):512 * (w % 2) + 512]), ALU.add).then_inc(v1_stored, 1)
                if b.live:
                    for j in range(2):
                        i = 2 * (8 * b.n + s) + j
                        e = (s % 2) * 2 + j
                        dve.wait_ge(exp1, 2 * i + 2)
                        nc.vector.reciprocal(rinv[e][:, 0:2], sums[e][:, 0:2]).then_inc(rinv1, 1)
                        dve.wait_ge(rinv1, i + 1)
                        dve.wait_ge(v1_stored, 4 * b.n + 4)
                        need(dve, pv1, i - 3)
                        nc.vector.tensor_tensor(Vs[e][:, :, :], V[:, b.par, :, 2 * s + j, 0:HEAD], rinv[e][:, 0:2].unsqueeze(2).to_broadcast([PARTS, 2, HEAD]),
                                                ALU.mult).then_inc(vs1, 1)
                if s == 6 and (not a.static or 0 < a.n + 1 < BATCHES):
                    first_input(a.n + 1, 1 - a.par)

            dve.wait_ge(turned_out, 13)
            first_input(0, 0)

            def unit_input(u, par):
                need(dve, proj_done, 12 * (u - 1))
                dve.wait_ge(x_written, u + 1)
                nc.vector.tensor_copy(xs[par][0:64, :], X[0:64, slot(u)])
                nc.vector.tensor_copy(xs[par][64:128, 1:TOKENS], X[64:128, slot(u, 0, TOKENS - 1)]).then_inc(xs_ready, 1)

            def unit_output(c1, s):
                if c1.live and s == 3:
                    dve.wait_ge(w2_done, c1.n + 1)
                    nc.vector.scalar_tensor_tensor(out=X[:, slot(c1.n + BATCHES)], in0=psA[1][:, 0:256],
                                                   scalar=cols[:, bass.ds(layer_of(c1.n) + B2, 1)], in1=xr[c1.par][:, :], op0=ALU.add, op1=ALU.add).then_inc(x_written, 1)

            def normalise(c):
                dve.wait_ge(rstd_done, c.n + 1)
                nc.vector.tensor_tensor(xn[:, :], psC[:, 0:256], rstd[:, 0:256], ALU.mult).then_inc(xn_done, 1)
                dve.wait_ge(xn_done, c.n + 1)
                need(dve, a_done, c.n)
                nc.vector.tensor_scalar(xg[:, :], xn[:, :], cols[:, bass.ds(layer_of(c.n) + LNG, 1)], cols[:, bass.ds(layer_of(c.n) + LNB, 1)], ALU.mult, ALU.add).then_inc(xg_done, 1)

            def slot_of(a, b, c, s):
                unit_output(c.back(), s)
                if b.live and s == 4:
                    for r in range(2):
                        dve.wait_ge(scored, 10 * b.n + CORNER_USE + r + 1)
                        nc.vector.tensor_reduce(mc[:, PAIRS * r:PAIRS * r + PAIRS], psS[r][0:WINDOW, 0:256].rearrange("p (h k) -> p h k", k=WINDOW),
                                                AX.X, ALU.max, negate=True).then_inc(corner_maxed, 1)
                bp1, sb1 = lag(b, s, 1)
                e, ec = E[sb1 % 4], Ec[sb1 % 2][:, :].rearrange("p (h k) -> p h k", k=WINDOW)
                i1, ci = 8 * bp1.n + sb1, 4 * bp1.n + sb1 - 4
                if bp1.live and sb1 >= 4:
                    dve.wait_ge(corner_exped, ci + 1)
                    nc.vector.tensor_reduce(corner_sums[:, :], ec, AX.X, ALU.add).then_inc(corner_summed, 1)
                if c.live and s == 4:
                    dve.wait_ge(wo_done, c.n + 1)
                    nc.vector.tensor_tensor(xr[c.par][:, :], psC[:, 0:256], X[:, slot(c.n)], ALU.add).then_inc(resid, 1)
                if b.live:
                    m, g = mx[s % 2], s % 4
                    dve.wait_ge(scored, 10 * b.n + use_s(s) + 1)
                    nc.vector.tensor_reduce(m[:, :], heads4(psS[use_s(s) % 2][:, :]), AX.X, ALU.max, negate=True).then_inc(maxed, 1)
                if bp1.live:
                    dve.wait_ge(exped, i1 + 1)
                    if sb1 >= 4:
                        dve.wait_ge(corner_summed, ci + 1)
                        nc.vector.tensor_tensor(sums[sb1 % 4][0:WINDOW, :], sums[sb1 % 4][0:WINDOW, :], corner_sums[:, :], ALU.add).then_inc(sums_whole, 1)
                if b.live and s >= 4:
                    dve.wait_ge(maxed, 12 * b.n + 2 * s - 3)
                    dve.wait_ge(corner_maxed, 2 * b.n + 2)
                    nc.vector.tensor_tensor(m[0:WINDOW, :], m[0:WINDOW, :], mc[:, kept(g)], ALU.min).then_inc(maxed, 1)
                if bp1.live:
                    if sb1 >= 4:
                        dve.wait_ge(sums_whole, ci + 1)
                    nc.vector.reciprocal(rinv[sb1 % 2][:, :], sums[sb1 % 4][:, :]).then_inc(recip_done, 1)
                if b.live and s >= 4:
                    dve.wait_ge(maxed, 12 * b.n + 2 * s - 2)
                    dve.wait_ge(corner_stored, 2 * b.n + 2)
                    need(dve, corner_turned, 4 * b.n + s - 5)
                    nc.vector.tensor_tensor(Ec[s % 2][:, :].rearrange("p (h k) -> p h k", k=WINDOW), Sc[:, kept(g), :],
                                            m[0:WINDOW, :].unsqueeze(2).to_broadcast([WINDOW, PER_GROUP, WINDOW]), ALU.add).then_inc(corner_shifted, 1)
                if bp1.live:
                    dve.wait_ge(recip_done, i1 + 1)
                    if sb1 >= 4:
                        nc.vector.tensor_tensor(ec, ec, rinv[sb1 % 2][0:WINDOW, :].unsqueeze(2).to_broadcast([WINDOW, PER_GROUP, WINDOW]),
                                                ALU.mult).then_inc(corner_weighted, 1)
                    nc.vector.tensor_tensor(heads4(e[:, :]), heads4(e[:, :]), rinv[sb1 % 2][:, :].unsqueeze(2).to_broadcast([PARTS, PER_GROUP, PARTS]),
                                            ALU.mult).then_inc(weighted, 1)
                    if sb1 >= 4:
                        dve.wait_ge(corner_weighted, ci + 1)
                        need(dve, pv_done, i1 - 1)
                        nc.vector.transpose(PcT[sb1 % 2][:, :], Ec[sb1 % 2][:, :]).then_inc(corner_turned, 1)
                if c.live and s == 7:
                    normalise(c)
                c1 = c.back()
                if c1.live and s == 2:
                    m = FF_CHUNKS[2][1]
                    dve.wait_ge(gelu_done, 2 * c1.n + 1)
                    nc.vector.tensor_tensor(hid[0:m, 2, :], hid[0:m, 2, :], gate[0:m, 2, :], ALU.mult).then_inc(hid2_done, 1)
                    for k in range(2):
                        dve.wait_ge(a_done, c1.n + 1)
                        dve.wait_ge(gelu_done, 2 * c1.n + 2)
                        nc.vector.scalar_tensor_tensor(out=hid[:, k, :], in0=psC[:, 256 * k:256 * k + 256], scalar=cols[:, bass.ds(layer_of(c1.n) + B1 + k * LAYERS, 1)],
                                                       in1=gate[:, k, :], op0=ALU.add, op1=ALU.mult).then_inc(hid_done, 1)
                if c.live and s == 5:
                    dve.wait_ge(var_done, c.n + 1)
                    need(dve, rdev_done, c.n)
                    nc.vector.tensor_scalar(n2[0][:, HEADS:HEADS + TILES] if a.live else var[:, 0:2], psC[:, 256:258], EPS, None, ALU.add).then_inc(eps_added, 1)
                if a.live:
                    tile, which = s // 4, s % 2
                    i = 8 * a.n + s
                    rotated_half = heads8(psA[0][:, :]).rearrange("p h (a d) -> p h a d", a=2)[:, :, ::-1, :]
                    dve.wait_ge(squared, i + 1)
                    need(dve, added, i - 1)
                    nc.vector.tensor_tensor(heads8(qc[s % 2][:, :]), heads8(psA[0][:, :]),
                                            tables[:, table(layer_of(a.n), tile, 2 * which)].unsqueeze(1).to_broadcast([PARTS, 8, HEAD]), ALU.mult).then_inc(cos_done, 1)
                    need(dve, a_turned, i - 3)
                    nc.vector.tensor_tensor(heads8(qs[s % 4][:, :]).rearrange("p h (a d) -> p h a d", a=2), rotated_half,
                                            tables[:, table(layer_of(a.n), tile, 2 * which + 1)].rearrange("p (o a d) -> p o a d", o=1, a=2)
                                            .to_broadcast([PARTS, 8, 2, HEAD // 2]), ALU.mult).then_inc(sin_done, 1)
                    norms = n2[(s // 2) % 2]
                    need(dve, rotated, i - 3 - s % 2)
                    nc.vector.tensor_reduce(norms[:, 8 * which:8 * which + 8], heads8(sq[s % 2][:, :]), AX.X, ALU.add).then_inc(summed, 1)
                    if which:
                        dve.wait_ge(summed, i + 1)
                        nc.vector.tensor_scalar(norms[:, 0:HEADS], norms[:, 0:HEADS], 1e-24, None, ALU.max).then_inc(guarded, 1)
                if s == 6 and (not a.static or 0 < a.n + 1 < UNITS):
                    unit_input(a.n + 1, 1 - a.par)

            def kept(g):
                at = PAIRS * (g % 2) + PER_GROUP * (g // 2)
                return slice(at, at + PER_GROUP)

            def heads4(ap):
                return ap.rearrange("p (h k) -> p h k", k=PARTS)

            over_units(dve, first_slot, BATCHES, 2, BATCHES - 2, -1, BATCHES)
            dve.wait_ge(x_written, 1)
            dve.wait_ge(tables_ready, LAYERS * TILES)
            dve.wait_ge(proj1, BATCHES * 12)
            unit_input(0, 0)
            change_over(first_slot, slot_of)
            dve.wait_ge(x1_kept, 1)
            over_units(dve, slot_of, UNITS, FIRST, LAST, 0, UNITS + 2)

            dve.wait_ge(x_written, UNITS + BATCHES)
            for k in range(4):
                nc.vector.tensor_tensor(y[k], X[:, 512 * k:512 * k + 512], x1[:, 512 * k:512 * k + 512], ALU.add).then_inc(y_ready, 1)
            dve.wait_ge(y_var, 4)
            nc.vector.tensor_scalar(var[:, :], psC[:, 0:16], EPS, None, ALU.add).then_inc(y_eps, 1)
            for k in range(4):
                dve.wait_ge(y_rstd, k + 1)
                nc.vector.tensor_tensor(yn[k], centred_y[k][:, :], y_dev[k], ALU.mult).then_inc(y_normed, 1)


FIRST, LAST = 2, UNITS - 2

_INS = ["L0_attn_x", "L0_attn_q_w", "L0_attn_q_b", "L0_attn_k_w", "L0_attn_k_b", "L0_attn_v_w", "L0_attn_v_b", "L0_attn_l_w", "L0_attn_l_b",
        "L0_ffn_Wqkv", "L0_ffn_q_scale", "L0_ffn_k_scale", "L0_ffn_Wo", "L0_ffn_ln_g", "L0_ffn_ln_b", "L0_ffn_W1", "L0_ffn_b1", "L0_ffn_W2", "L0_ffn_b2"]


def kernel(**inputs):
    import concourse.bacc as _bacc
    from concourse.bass_utils import run_bass_kernel_spmd as _run

    nc = _bacc.Bacc("TRN2", target_bir_lowering=False, num_devices=1)
    arrays, args = {}, []
    given = [(f"in_{n}_dram", np.ascontiguousarray(inputs[n])) for n in _INS]
    for name, a in given + [(f"const_{n}_dram", a) for n, a in constants().items()]:
        if name == "const_rotary_dram":
            a = a.reshape(PARTS, -1)
        arrays[name] = a
        args.append(nc.dram_tensor(name, a.shape, mybir.dt.from_np(a.dtype), kind="ExternalInput").ap())
    args.append(nc.dram_tensor("out_0_dram", (BATCHES, TOKENS, DIM), F32, kind="ExternalOutput").ap())
    postln_kernel(nc, *args)
    r = _run(nc, [arrays], core_ids=[0])
    return r.results[0]["out_0_dram"]
```
